# Optimizing a Trainium2 kernel written in Bass

```python
import numpy as np
import jax
import jax.numpy as jnp

def _softmax(x, axis=-1):
    return jax.nn.softmax(x, axis=axis)

def _gelu(x):
    return jax.nn.gelu(x, approximate=True)

def _silu(x):
    return jax.nn.silu(x)

def _sigmoid(x):
    return jax.nn.sigmoid(x)

def _layernorm(x, axis=-1, eps=1e-05):
    m = jnp.mean(x, axis=axis, keepdims=True)
    v = jnp.var(x, axis=axis, keepdims=True)
    return (x - m) / jnp.sqrt(v + eps)

def _scatter_add(tgt, idx, src, axis=0):
    return tgt.at[idx].add(src)

def _segment_sum(src, seg, n):
    return jax.ops.segment_sum(src, seg, n)
kernel_name = 'mk_seq_preln_d2_jaxref_r8_f95032'

def setup_inputs(seed: int=0):
    np.random.seed(seed)
    _w = jnp.asarray

    def _L0_attn_setup():
        import jax, jax.numpy as jnp
        import numpy as np
        DIM = 256
        N_HEADS = 16
        HEAD_DIM = DIM // N_HEADS
        WINDOW_SIZE = 64
        OMEGA_CONTEXT_WINDOW = 64
        OMEGA_DECAY_BASE = 0.9
        GAMMA_GATE_HIDDEN = 64
        MEM_EXPANSION = 4
        POLY_DEGREE = 2
        FFN_HIDDEN = int(DIM * MEM_EXPANSION * 2 / 3)
        EPS = 1e-06

        def rms_norm(x, w):
            var = jnp.mean(x * x, axis=-1, keepdims=True)
            return x * jax.lax.rsqrt(var + EPS) * w

        def rotate_half(x):
            x1, x2 = jnp.split(x, 2, axis=-1)
            return jnp.concatenate([-x2, x1], axis=-1)

        def apply_rope(q, k, seq_len, head_dim):
            inv_freq = 1.0 / 10000.0 ** (jnp.arange(0, head_dim, 2, dtype=jnp.float32) / head_dim)
            t = jnp.arange(seq_len, dtype=jnp.float32)
            freqs = t[:, None] * inv_freq[None, :]
            emb = jnp.concatenate([freqs, freqs], axis=-1)
            cos = jnp.cos(emb)[None, None]
            sin = jnp.sin(emb)[None, None]
            q = q * cos + rotate_half(q) * sin
            k = k * cos + rotate_half(k) * sin
            return (q, k)
        key = jax.random.key(seed)
        ks = jax.random.split(key, 16)
        B, S, D = (1, 256, DIM)
        s = 0.02
        return {'x': jax.random.normal(ks[0], (B, S, D), jnp.float32), 'w_qkv': jax.random.normal(ks[1], (D, 3 * D), jnp.float32) * s, 'q_scale': jnp.ones((HEAD_DIM,), jnp.float32), 'k_scale': jnp.ones((HEAD_DIM,), jnp.float32), 'norm1_w': jnp.ones((D,), jnp.float32), 'norm2_w': jnp.ones((D,), jnp.float32), 'gg_w1': jax.random.normal(ks[2], (D, GAMMA_GATE_HIDDEN), jnp.float32) * s, 'gg_w2': jax.random.normal(ks[3], (GAMMA_GATE_HIDDEN, 1), jnp.float32) * s, 'w_o': jax.random.normal(ks[4], (D, D), jnp.float32) * (s / 2 ** 0.5), 'mem_w1': jax.random.normal(ks[5], (D, D * MEM_EXPANSION), jnp.float32) * s, 'mem_w2': jax.random.normal(ks[6], (D * MEM_EXPANSION, D), jnp.float32) * s, 'ffn_w1': jax.random.normal(ks[7], (D, FFN_HIDDEN), jnp.float32) * s, 'ffn_w3': jax.random.normal(ks[8], (D, FFN_HIDDEN), jnp.float32) * s, 'ffn_w2': jax.random.normal(ks[9], (FFN_HIDDEN, D), jnp.float32) * s}
    _L0_attn_in = _L0_attn_setup()

    def _L0_ffn_setup():
        import jax, jax.numpy as jnp
        import numpy as np
        DIM = 256
        N_EXPERTS = 8
        TOP_K = 2
        key = jax.random.key(seed)
        ks = jax.random.split(key, 5)
        x = jax.random.normal(ks[0], (4, 512, DIM), dtype=jnp.float32)
        W_up = jax.random.normal(ks[1], (DIM, DIM), dtype=jnp.float32) * (1.0 / np.sqrt(DIM))
        W_down = jax.random.normal(ks[2], (DIM, DIM), dtype=jnp.float32) * (1.0 / np.sqrt(DIM))
        W_gate = jax.random.normal(ks[3], (N_EXPERTS, DIM), dtype=jnp.float32) * (1.0 / np.sqrt(DIM))
        W_expert = jax.random.normal(ks[4], (DIM, DIM), dtype=jnp.float32) * (1.0 / np.sqrt(DIM))
        return {'x': x, 'W_up': W_up, 'W_down': W_down, 'W_gate': W_gate, 'W_expert': W_expert}
    _L0_ffn_in = _L0_ffn_setup()

    def _L1_attn_setup():
        import math
        import jax, jax.numpy as jnp
        import numpy as np
        B, S, HID = (2, 128, 256)
        H, D, R = (16, 128, 64)
        KVC, QC = (64, 192)
        MAX_POS = 512

        def _lin(x, w, b):
            return x @ w.T + b

        def _rotate_half(x):
            x1, x2 = (x[..., :x.shape[-1] // 2], x[..., x.shape[-1] // 2:])
            return jnp.concatenate([-x2, x1], axis=-1)

        def _rope_tables(dim, end, theta=10000.0):
            freqs = 1.0 / theta ** (jnp.arange(0, dim, 2)[:dim // 2].astype(jnp.float32) / dim)
            f = jnp.outer(jnp.arange(end, dtype=jnp.float32), freqs)
            cos, sin = (jnp.cos(f), jnp.sin(f))
            return (jnp.concatenate([cos, cos], -1), jnp.concatenate([sin, sin], -1))

        def _reference_tuple_inner(hidden_states, W_DKV_w, W_DKV_b, W_UK_w, W_UK_b, W_UV_w, W_UV_b, W_KR_w, W_KR_b, W_DQ_w, W_DQ_b, W_UQ_w, W_UQ_b, W_QR_w, W_QR_b, W_O_w, W_O_b):
            b, s = hidden_states.shape[:2]
            c_kv = _lin(hidden_states, W_DKV_w, W_DKV_b)
            k = _lin(c_kv, W_UK_w, W_UK_b).reshape(b, s, H, D)
            v = _lin(c_kv, W_UV_w, W_UV_b).reshape(b, s, H, D)
            c_q = _lin(hidden_states, W_DQ_w, W_DQ_b)
            q = _lin(c_q, W_UQ_w, W_UQ_b).reshape(b, s, H, D)
            k_r = _lin(k, W_KR_w, W_KR_b)
            q_r = _lin(q, W_QR_w, W_QR_b)
            cos, sin = _rope_tables(R, MAX_POS)
            cos_p = cos[:s][:, None, :]
            sin_p = sin[:s][:, None, :]
            q_r = q_r * cos_p + _rotate_half(q_r) * sin_p
            k_r = k_r * cos_p + _rotate_half(k_r) * sin_p
            scale = 1.0 / math.sqrt(D)
            scores = jnp.einsum('bqhd,bkhd->bhqk', q, k) * scale
            probs = jax.nn.softmax(scores, axis=-1)
            attn = jnp.einsum('bhqk,bkhd->bqhd', probs, v).reshape(b, s, H * D)
            output = _lin(attn, W_O_w, W_O_b)
            return (output, c_kv, k_r)
        key = jax.random.key(seed)
        ks = jax.random.split(key, 17)
        w = lambda k, shape: jax.random.normal(k, shape, jnp.float32) * 0.02
        return {'hidden_states': jax.random.normal(ks[0], (B, S, HID), jnp.float32), 'W_DKV_w': w(ks[1], (KVC, HID)), 'W_DKV_b': w(ks[2], (KVC,)), 'W_UK_w': w(ks[3], (H * D, KVC)), 'W_UK_b': w(ks[4], (H * D,)), 'W_UV_w': w(ks[5], (H * D, KVC)), 'W_UV_b': w(ks[6], (H * D,)), 'W_KR_w': w(ks[7], (R, D)), 'W_KR_b': w(ks[8], (R,)), 'W_DQ_w': w(ks[9], (QC, HID)), 'W_DQ_b': w(ks[10], (QC,)), 'W_UQ_w': w(ks[11], (H * D, QC)), 'W_UQ_b': w(ks[12], (H * D,)), 'W_QR_w': w(ks[13], (R, D)), 'W_QR_b': w(ks[14], (R,)), 'W_O_w': w(ks[15], (HID, H * D)), 'W_O_b': w(ks[16], (HID,))}
    _L1_attn_in = _L1_attn_setup()

    def _L1_ffn_setup():
        import jax, jax.numpy as jnp
        import numpy as np
        H, I, E, TOP_K = (256, 176, 16, 6)
        IS = 352
        NORM_TOPK_PROB = False

        def _silu_and_mul(gate_up):
            d = gate_up.shape[-1] // 2
            g, u = (gate_up[..., :d], gate_up[..., d:])
            return jax.nn.silu(g) * u
        key = jax.random.key(seed)
        ks = jax.random.split(key, 6)
        s = 0.02
        return {'x': jax.random.normal(ks[0], (1, 256, H), jnp.float32), 'gate_w': jax.random.normal(ks[1], (E, H), jnp.float32) * s, 'w1': jax.random.normal(ks[2], (E, 2 * I, H), jnp.float32) * s, 'w2': jax.random.normal(ks[3], (E, H, I), jnp.float32) * s, 'shared_w1': jax.random.normal(ks[4], (2 * IS, H), jnp.float32) * s, 'shared_w2': jax.random.normal(ks[5], (H, IS), jnp.float32) * s}
    _L1_ffn_in = _L1_ffn_setup()
    _d = {'L0_attn_x': _L0_attn_in['x'], 'L0_attn_w_qkv': _L0_attn_in['w_qkv'], 'L0_attn_q_scale': _L0_attn_in['q_scale'], 'L0_attn_k_scale': _L0_attn_in['k_scale'], 'L0_attn_norm1_w': _L0_attn_in['norm1_w'], 'L0_attn_norm2_w': _L0_attn_in['norm2_w'], 'L0_attn_gg_w1': _L0_attn_in['gg_w1'], 'L0_attn_gg_w2': _L0_attn_in['gg_w2'], 'L0_attn_w_o': _L0_attn_in['w_o'], 'L0_attn_mem_w1': _L0_attn_in['mem_w1'], 'L0_attn_mem_w2': _L0_attn_in['mem_w2'], 'L0_attn_ffn_w1': _L0_attn_in['ffn_w1'], 'L0_attn_ffn_w3': _L0_attn_in['ffn_w3'], 'L0_attn_ffn_w2': _L0_attn_in['ffn_w2'], 'L0_ffn_W_up': _L0_ffn_in['W_up'], 'L0_ffn_W_down': _L0_ffn_in['W_down'], 'L0_ffn_W_gate': _L0_ffn_in['W_gate'], 'L0_ffn_W_expert': _L0_ffn_in['W_expert'], 'L1_attn_W_DKV_w': _L1_attn_in['W_DKV_w'], 'L1_attn_W_DKV_b': _L1_attn_in['W_DKV_b'], 'L1_attn_W_UK_w': _L1_attn_in['W_UK_w'], 'L1_attn_W_UK_b': _L1_attn_in['W_UK_b'], 'L1_attn_W_UV_w': _L1_attn_in['W_UV_w'], 'L1_attn_W_UV_b': _L1_attn_in['W_UV_b'], 'L1_attn_W_KR_w': _L1_attn_in['W_KR_w'], 'L1_attn_W_KR_b': _L1_attn_in['W_KR_b'], 'L1_attn_W_DQ_w': _L1_attn_in['W_DQ_w'], 'L1_attn_W_DQ_b': _L1_attn_in['W_DQ_b'], 'L1_attn_W_UQ_w': _L1_attn_in['W_UQ_w'], 'L1_attn_W_UQ_b': _L1_attn_in['W_UQ_b'], 'L1_attn_W_QR_w': _L1_attn_in['W_QR_w'], 'L1_attn_W_QR_b': _L1_attn_in['W_QR_b'], 'L1_attn_W_O_w': _L1_attn_in['W_O_w'], 'L1_attn_W_O_b': _L1_attn_in['W_O_b'], 'L1_ffn_gate_w': _L1_ffn_in['gate_w'], 'L1_ffn_w1': _L1_ffn_in['w1'], 'L1_ffn_w2': _L1_ffn_in['w2'], 'L1_ffn_shared_w1': _L1_ffn_in['shared_w1'], 'L1_ffn_shared_w2': _L1_ffn_in['shared_w2']}
    _x0 = _d['L0_attn_x']
    _d['L0_attn_x'] = jax.random.normal(jax.random.fold_in(jax.random.key(seed), 1), (4, 256, 256), dtype=_x0.dtype)
    del _x0
    return _d

def reference(L0_attn_x, L0_attn_w_qkv, L0_attn_q_scale, L0_attn_k_scale, L0_attn_norm1_w, L0_attn_norm2_w, L0_attn_gg_w1, L0_attn_gg_w2, L0_attn_w_o, L0_attn_mem_w1, L0_attn_mem_w2, L0_attn_ffn_w1, L0_attn_ffn_w3, L0_attn_ffn_w2, L0_ffn_W_up, L0_ffn_W_down, L0_ffn_W_gate, L0_ffn_W_expert, L1_attn_W_DKV_w, L1_attn_W_DKV_b, L1_attn_W_UK_w, L1_attn_W_UK_b, L1_attn_W_UV_w, L1_attn_W_UV_b, L1_attn_W_KR_w, L1_attn_W_KR_b, L1_attn_W_DQ_w, L1_attn_W_DQ_b, L1_attn_W_UQ_w, L1_attn_W_UQ_b, L1_attn_W_QR_w, L1_attn_W_QR_b, L1_attn_W_O_w, L1_attn_W_O_b, L1_ffn_gate_w, L1_ffn_w1, L1_ffn_w2, L1_ffn_shared_w1, L1_ffn_shared_w2):

    def _L0_attn_ref(x, w_qkv, q_scale, k_scale, norm1_w, norm2_w, gg_w1, gg_w2, w_o, mem_w1, mem_w2, ffn_w1, ffn_w3, ffn_w2):
        import jax, jax.numpy as jnp
        import numpy as np
        DIM = 256
        N_HEADS = 16
        HEAD_DIM = DIM // N_HEADS
        WINDOW_SIZE = 64
        OMEGA_CONTEXT_WINDOW = 64
        OMEGA_DECAY_BASE = 0.9
        GAMMA_GATE_HIDDEN = 64
        MEM_EXPANSION = 4
        POLY_DEGREE = 2
        FFN_HIDDEN = int(DIM * MEM_EXPANSION * 2 / 3)
        EPS = 1e-06

        def rms_norm(x, w):
            var = jnp.mean(x * x, axis=-1, keepdims=True)
            return x * jax.lax.rsqrt(var + EPS) * w

        def rotate_half(x):
            x1, x2 = jnp.split(x, 2, axis=-1)
            return jnp.concatenate([-x2, x1], axis=-1)

        def apply_rope(q, k, seq_len, head_dim):
            inv_freq = 1.0 / 10000.0 ** (jnp.arange(0, head_dim, 2, dtype=jnp.float32) / head_dim)
            t = jnp.arange(seq_len, dtype=jnp.float32)
            freqs = t[:, None] * inv_freq[None, :]
            emb = jnp.concatenate([freqs, freqs], axis=-1)
            cos = jnp.cos(emb)[None, None]
            sin = jnp.sin(emb)[None, None]
            q = q * cos + rotate_half(q) * sin
            k = k * cos + rotate_half(k) * sin
            return (q, k)
        B, S, D = x.shape
        H, Dh = (N_HEADS, HEAD_DIM)
        scale = Dh ** (-0.5)
        h = rms_norm(x, norm1_w)
        qkv = h @ w_qkv
        q, k, v = jnp.split(qkv, 3, axis=-1)

        def to_heads(t):
            return t.reshape(B, S, H, Dh).transpose(0, 2, 1, 3)
        q, k, v = (to_heads(q), to_heads(k), to_heads(v))
        q = rms_norm(q, q_scale)
        k = rms_norm(k, k_scale)
        q, k = apply_rope(q, k, S, Dh)
        gamma = jax.nn.sigmoid(jax.nn.silu(h @ gg_w1) @ gg_w2)
        pos = jnp.arange(S)
        rel = pos[:, None] - pos[None, :]
        omega_valid = (rel >= 0) & (rel < OMEGA_CONTEXT_WINDOW)
        scores_m = jnp.einsum('bhqd,bhkd->bhqk', q, k) * scale
        scores_m = jnp.where(omega_valid[None, None], scores_m, -jnp.inf)
        w_m = jax.nn.softmax(scores_m, axis=-1)
        decay = jnp.where(omega_valid, OMEGA_DECAY_BASE ** rel.astype(jnp.float32), 0.0)
        w_m = w_m * decay[None, None] * gamma[:, None, None, :, 0]
        q_mem = jnp.einsum('bhqk,bhkd->bhqd', w_m, k)
        q_mem_flat = q_mem.transpose(0, 2, 1, 3).reshape(B, S, D)
        swa_masked = (rel < 0) | (rel > WINDOW_SIZE - 1)
        attn = jnp.einsum('bhqd,bhkd->bhqk', q, k) * scale
        attn = jnp.where(swa_masked[None, None], -jnp.inf, attn)
        attn = jax.nn.softmax(attn, axis=-1)
        attn_out = jnp.einsum('bhqk,bhkd->bhqd', attn, v)
        attn_out = attn_out.transpose(0, 2, 1, 3).reshape(B, S, D) @ w_o
        phi = jax.nn.silu(q_mem_flat @ mem_w1)
        poly = phi
        for p in range(2, POLY_DEGREE + 1):
            poly = poly + phi ** p
        mem_out = poly @ mem_w2
        x = x + attn_out * jax.nn.sigmoid(mem_out)
        y = rms_norm(x, norm2_w)
        x = x + jax.nn.silu(y @ ffn_w1) * (y @ ffn_w3) @ ffn_w2
        return x

    def _L0_ffn_ref(x, W_up, W_down, W_gate, W_expert):
        import jax, jax.numpy as jnp
        import numpy as np
        DIM = 256
        N_EXPERTS = 8
        TOP_K = 2
        logits = jnp.einsum('bsd,ed->bse', x, W_gate)
        routing_weights, selected_experts = jax.lax.top_k(logits, TOP_K)
        shared_out = jnp.einsum('bsd,od->bso', jax.nn.relu(jnp.einsum('bsd,od->bso', x, W_up)), W_down)
        rw = jax.nn.softmax(routing_weights, axis=-1)
        expert_out = jnp.einsum('bsd,do->bso', x, W_expert)
        moe_out = jnp.sum(rw, axis=-1, keepdims=True) * expert_out
        return shared_out + moe_out

    def _L1_attn_ref(hidden_states, W_DKV_w, W_DKV_b, W_UK_w, W_UK_b, W_UV_w, W_UV_b, W_KR_w, W_KR_b, W_DQ_w, W_DQ_b, W_UQ_w, W_UQ_b, W_QR_w, W_QR_b, W_O_w, W_O_b):
        import math
        import jax, jax.numpy as jnp
        import numpy as np
        B, S, HID = (2, 128, 256)
        H, D, R = (16, 128, 64)
        KVC, QC = (64, 192)
        MAX_POS = 512

        def _lin(x, w, b):
            return x @ w.T + b

        def _rotate_half(x):
            x1, x2 = (x[..., :x.shape[-1] // 2], x[..., x.shape[-1] // 2:])
            return jnp.concatenate([-x2, x1], axis=-1)

        def _rope_tables(dim, end, theta=10000.0):
            freqs = 1.0 / theta ** (jnp.arange(0, dim, 2)[:dim // 2].astype(jnp.float32) / dim)
            f = jnp.outer(jnp.arange(end, dtype=jnp.float32), freqs)
            cos, sin = (jnp.cos(f), jnp.sin(f))
            return (jnp.concatenate([cos, cos], -1), jnp.concatenate([sin, sin], -1))

        def _reference_tuple_inner(hidden_states, W_DKV_w, W_DKV_b, W_UK_w, W_UK_b, W_UV_w, W_UV_b, W_KR_w, W_KR_b, W_DQ_w, W_DQ_b, W_UQ_w, W_UQ_b, W_QR_w, W_QR_b, W_O_w, W_O_b):
            b, s = hidden_states.shape[:2]
            c_kv = _lin(hidden_states, W_DKV_w, W_DKV_b)
            k = _lin(c_kv, W_UK_w, W_UK_b).reshape(b, s, H, D)
            v = _lin(c_kv, W_UV_w, W_UV_b).reshape(b, s, H, D)
            c_q = _lin(hidden_states, W_DQ_w, W_DQ_b)
            q = _lin(c_q, W_UQ_w, W_UQ_b).reshape(b, s, H, D)
            k_r = _lin(k, W_KR_w, W_KR_b)
            q_r = _lin(q, W_QR_w, W_QR_b)
            cos, sin = _rope_tables(R, MAX_POS)
            cos_p = cos[:s][:, None, :]
            sin_p = sin[:s][:, None, :]
            q_r = q_r * cos_p + _rotate_half(q_r) * sin_p
            k_r = k_r * cos_p + _rotate_half(k_r) * sin_p
            scale = 1.0 / math.sqrt(D)
            scores = jnp.einsum('bqhd,bkhd->bhqk', q, k) * scale
            probs = jax.nn.softmax(scores, axis=-1)
            attn = jnp.einsum('bhqk,bkhd->bqhd', probs, v).reshape(b, s, H * D)
            output = _lin(attn, W_O_w, W_O_b)
            return (output, c_kv, k_r)
        return _reference_tuple_inner(hidden_states, W_DKV_w, W_DKV_b, W_UK_w, W_UK_b, W_UV_w, W_UV_b, W_KR_w, W_KR_b, W_DQ_w, W_DQ_b, W_UQ_w, W_UQ_b, W_QR_w, W_QR_b, W_O_w, W_O_b)[0]

    def _L1_ffn_ref(x, gate_w, w1, w2, shared_w1, shared_w2):
        import jax, jax.numpy as jnp
        import numpy as np
        H, I, E, TOP_K = (256, 176, 16, 6)
        IS = 352
        NORM_TOPK_PROB = False

        def _silu_and_mul(gate_up):
            d = gate_up.shape[-1] // 2
            g, u = (gate_up[..., :d], gate_up[..., d:])
            return jax.nn.silu(g) * u
        B, S, Hd = x.shape
        xf = x.reshape(-1, Hd)
        T = xf.shape[0]
        shared_out = _silu_and_mul(xf @ shared_w1.T) @ shared_w2.T
        logits = xf @ gate_w.T
        probs = jax.nn.softmax(logits.astype(jnp.float32), axis=-1)
        routing_weights, selected = jax.lax.top_k(probs, TOP_K)
        if NORM_TOPK_PROB:
            routing_weights = routing_weights / routing_weights.sum(-1, keepdims=True)
        combine = jnp.zeros((T, E), jnp.float32).at[jnp.arange(T)[:, None], selected].add(routing_weights).astype(x.dtype)
        gate_up = jnp.einsum('th,eoh->teo', xf, w1)
        act = _silu_and_mul(gate_up)
        moe_out = jnp.einsum('te,tei,ehi->th', combine, act, w2)
        return (moe_out + shared_out).reshape(B, S, Hd)
    x = L0_attn_x
    x = x + _L0_attn_ref(_layernorm(x, axis=-1), L0_attn_w_qkv, L0_attn_q_scale, L0_attn_k_scale, L0_attn_norm1_w, L0_attn_norm2_w, L0_attn_gg_w1, L0_attn_gg_w2, L0_attn_w_o, L0_attn_mem_w1, L0_attn_mem_w2, L0_attn_ffn_w1, L0_attn_ffn_w3, L0_attn_ffn_w2)
    x = x + _L0_ffn_ref(_layernorm(x, axis=-1), L0_ffn_W_up, L0_ffn_W_down, L0_ffn_W_gate, L0_ffn_W_expert)
    x = x + _L1_attn_ref(_layernorm(x, axis=-1), L1_attn_W_DKV_w, L1_attn_W_DKV_b, L1_attn_W_UK_w, L1_attn_W_UK_b, L1_attn_W_UV_w, L1_attn_W_UV_b, L1_attn_W_KR_w, L1_attn_W_KR_b, L1_attn_W_DQ_w, L1_attn_W_DQ_b, L1_attn_W_UQ_w, L1_attn_W_UQ_b, L1_attn_W_QR_w, L1_attn_W_QR_b, L1_attn_W_O_w, L1_attn_W_O_b)
    x = x + _L1_ffn_ref(_layernorm(x, axis=-1), L1_ffn_gate_w, L1_ffn_w1, L1_ffn_w2, L1_ffn_shared_w1, L1_ffn_shared_w2)
    return x

_drawn_inputs = setup_inputs


def setup_inputs(seed=0):
    import zlib

    import numpy as np

    out = dict(_drawn_inputs(seed))
    spreads = {'L0_attn_q_scale': (1.0, 0.6),
     'L0_attn_k_scale': (1.0, 0.6),
     'L0_attn_norm1_w': (1.0, 0.6),
     'L0_attn_norm2_w': (1.0, 0.6)}
    factors = {'L0_attn_w_qkv': 8.0,
     'L0_attn_gg_w1': 8.0,
     'L0_attn_gg_w2': 8.0,
     'L0_attn_w_o': 8.0,
     'L0_attn_mem_w1': 8.0,
     'L0_attn_mem_w2': 8.0,
     'L0_attn_ffn_w1': 3.685,
     'L0_attn_ffn_w3': 3.633,
     'L0_attn_ffn_w2': 3.631,
     'L0_ffn_W_gate': 64.0,
     'L1_attn_W_DKV_w': 8.0,
     'L1_attn_W_DKV_b': 8.0,
     'L1_attn_W_UK_w': 8.0,
     'L1_attn_W_UK_b': 64.0,
     'L1_attn_W_UV_w': 8.0,
     'L1_attn_W_UV_b': 7.021,
     'L1_attn_W_DQ_w': 8.0,
     'L1_attn_W_DQ_b': 8.0,
     'L1_attn_W_UQ_w': 8.0,
     'L1_attn_W_UQ_b': 8.0,
     'L1_attn_W_O_w': 6.961,
     'L1_attn_W_O_b': 51.155,
     'L1_ffn_gate_w': 8.0,
     'L1_ffn_w1': 8.0,
     'L1_ffn_w2': 8.0,
     'L1_ffn_shared_w1': 6.602,
     'L1_ffn_shared_w2': 6.419}
    for name, (base, spread) in spreads.items():
        noise = np.random.default_rng([zlib.crc32(name.encode()), seed]).standard_normal(out[name].shape)
        drawn = base * np.exp(spread * noise) if base else spread * noise
        out[name] = jnp.asarray(drawn.astype(out[name].dtype))
    for name, factor in factors.items():
        out[name] = (out[name] * factor).astype(out[name].dtype)
    return out
```

```python
from contextlib import ExitStack

import numpy as np

import concourse.bass as bass
from concourse import mybir

F32 = mybir.dt.float32
R32 = mybir.dt.float32r
BF16 = mybir.dt.bfloat16
ALU = mybir.AluOpType
ACT = mybir.ActivationFunctionType
AX_X = mybir.AxisListType.X

T = 1024
NT = T // 128
SLOT = 832
NSLOT = 3
NEG = -1.0e30

SM_OFF = {}
_at = 0
for _name, _n in (("ident", 128), ("cos", 32), ("sin", 32), ("qs", 16), ("ks", 16), ("dk", 2), ("dq", 2),
                  ("mh", 8), ("nw", 4), ("ggw2", 64), ("cb", 3), ("bo", 256), ("mask0", 512), ("mask1", 384)):
    SM_OFF[_name] = (_at, _at + _n)
    _at += _n
SM_N = _at

CHUNKS = [("qkv0", 832, True), ("qkv1", 832, True)]
CHUNKS += [("wo", 512, True)]
CHUNKS += [(f"mem{j}", 512, True) for j in range(8)]
CHUNKS += [(f"ffn{j}", 768, True) for j in range(6)]
CHUNKS += [("up", 512, True), ("exp", 528, True), ("down", 512, True)]
CHUNKS += [(f"fuse{h}", 642, False) for h in range(16)]
CHUNKS += [("proj", 768, True)]
CHUNKS += [("gate", 32, True)]
CHUNKS += [(f"moe{j}", 768, True) for j in range(25)]
CH_OFF = {}
_at = 0
for _name, _n, _ in CHUNKS:
    CH_OFF[_name] = _at
    _at += _n
W_N = _at


class Engine:

    def __init__(self, sem):
        self.sem, self.count, self.todo, self.seen = sem, 0, [], {}

    def wait(self, *tokens):
        for sem, value in tokens:
            if self.seen.get(id(sem), 0) < value:
                self.seen[id(sem)] = value
                self.todo.append(lambda e, s=sem, v=value: e.wait_ge(s, v))

    def op(self, f, *tokens, signal=True):
        self.wait(*tokens)
        if signal:
            self.count += 1
            self.todo.append(lambda e: f(e).then_inc(self.sem, 1))
            return (self.sem, self.count)
        self.todo.append(f)
        return None

    def dma(self, out, in_, sem, value, *tokens):
        self.wait(*tokens)
        self.todo.append(lambda e: e.dma_start(out, in_).then_inc(sem, 16))
        return (sem, value)

    def play(self, e):
        for f in self.todo:
            f(e)


class Slot:
    def __init__(self, *parts):
        self.parts, self.free = parts, ()


class Ring:

    def __init__(self, slots):
        self.slots, self.at = slots, 0

    def take(self):
        s = self.slots[self.at % len(self.slots)]
        self.at += 1
        assert s.free is not None
        free, s.free = s.free, None
        return s, free


def build(nc, x, w, sm, sel, out):
    outer = ExitStack()
    with outer:
        def sb(name, shape, dt=F32, ctx=outer):
            return ctx.enter_context(nc.sbuf_tensor(name, shape, dt))

        def semaphore(name):
            return outer.enter_context(nc.semaphore(name))

        banks = [outer.enter_context(nc.psum_tensor(f"ps{i}", [128, 512], F32)) for i in range(8)]
        bank_free = [()] * 8

        def bank_ring(ids):
            r = Ring([Slot(banks[i]) for i in ids])
            for s, i in zip(r.slots, ids):
                s.free = bank_free[i]
            return r

        def ring_done(r, ids):
            for s, i in zip(r.slots, ids):
                bank_free[i] = s.free

        pe = Engine(semaphore("s_pe"))
        dve = Engine(semaphore("s_dve"))
        act = Engine(semaphore("s_act"))
        pool = Engine(semaphore("s_pool"))
        sp = Engine(semaphore("s_sp"))

        XO = sb("XO", [128, NT, 256])
        X1 = sb("X1", [128, NT, 256])
        NB = sb("NB", [128, NT, 256])
        AO = sb("AO", [128, NT, 256])
        AT = (sb("ATh", [128, 2, T], R32), sb("ATl", [128, 2, T], R32))
        BT = (sb("BTh", [128, 2, T], R32), sb("BTl", [128, 2, T], R32))
        SM = sb("SM", [128, SM_N])
        sm_ = lambda n: SM[:, SM_OFF[n][0]:SM_OFF[n][1]]
        ident = sm_("ident")
        ws_ = [Slot(sb(f"wr{i}", [128, SLOT]), sb(f"wh{i}", [128, SLOT], R32), sb(f"wl{i}", [128, SLOT], R32),
                    semaphore(f"s_w{i}")) for i in range(NSLOT)]
        negh = sb("negh", [128, 128])
        st = sb("st", [128, NT, 6])
        mv = sb("mv", [128, NT, 2])
        ve = sb("ve", [128, NT])
        rs = sb("rs", [128, NT])
        r2 = sb("r2", [128, NT])
        v2 = sb("v2", [128, NT])

        s_in = semaphore("s_in")
        s_sm = semaphore("s_sm")
        s_out = semaphore("s_out")

        xv = x.rearrange("(t p) d -> p t d", p=128)
        s_x2 = semaphore("s_x2")
        t_x = [sp.dma(XO[:, 0:4, :], xv[:, 0:4, :], s_in, 16)]
        t_sm = sp.dma(SM[:, :], sm, s_sm, 16)

        index = {n: i for i, (n, _, _) in enumerate(CHUNKS)}
        loaded = [None] * len(CHUNKS)
        split_done = [None] * len(CHUNKS)
        raw_free = [()] * NSLOT
        part_free = [()] * NSLOT

        def load_chunk(i):
            if i >= len(CHUNKS):
                return
            name, n, _ = CHUNKS[i]
            s = i % NSLOT
            loaded[i] = sp.dma(ws_[s].parts[0][:, 0:n], w[:, CH_OFF[name]:CH_OFF[name] + n], ws_[s].parts[3],
                               16 * (i // NSLOT + 1), *raw_free[s])

        def split_chunk(i):
            if i >= len(CHUNKS):
                return
            name, n, split = CHUNKS[i]
            s = i % NSLOT
            raw, hi, lo, _ = ws_[s].parts
            if not split:
                return
            t = pool.op(lambda e: e.tensor_scalar(hi[:, 0:n], raw[:, 0:n], 1.0, 0.0, ALU.mult, ALU.add),
                        loaded[i], *part_free[s])
            t = pool.op(lambda e: e.tensor_tensor(lo[:, 0:n], raw[:, 0:n], hi[:, 0:n].bitcast(F32), ALU.subtract), t)
            split_done[i] = t
            raw_free[s] = (t,)
            load_chunk(i + NSLOT)

        def chunk(name):
            i = index[name]
            raw, hi, lo, _ = ws_[i % NSLOT].parts
            if CHUNKS[i][2]:
                return hi, lo, split_done[i]
            return raw, None, loaded[i]

        def chunk_done(name, token):
            i = index[name]
            s = i % NSLOT
            if CHUNKS[i][2]:
                part_free[s] = (token,)
            else:
                raw_free[s] = (token,)
                load_chunk(i + NSLOT)
            split_chunk(i + NSLOT)

        load_chunk(0)
        load_chunk(1)
        t_x.append(sp.dma(XO[:, 4:8, :], xv[:, 4:8, :], s_x2, 16))
        load_chunk(2)
        t_negh = pool.op(lambda e: e.memset(negh[:, :], -0.5))
        for i in range(NSLOT):
            split_chunk(i)

        def mm3(o, terms, *tokens, first=True, last=True, skip=False, signal=True):
            n = len(terms)
            pe.wait(*tokens)
            t = None
            for i, ((lh, ll), (rh, rl)) in enumerate(terms):
                for c, (a, b) in enumerate(((lh, rh), (lh, rl), (ll, rh))):
                    fin = i == n - 1 and c == 2
                    t = pe.op(lambda e, a=a, b=b, s=(first and i == 0 and c == 0), p=(last and fin):
                              e.matmul(o, a, b, start=s, stop=p, skip_group_check=skip), signal=fin and signal)
            return t

        def split_from(hi, lo, src, *tokens, scale=None):
            if scale is None:
                a = act.op(lambda e: e.copy(hi, src), *tokens)
                return dve.op(lambda e: e.tensor_tensor(lo, src, hi.bitcast(F32), ALU.subtract), a)
            a = act.op(lambda e: e.activation(hi, src, ACT.Copy, scale=scale), *tokens)
            return dve.op(lambda e: e.scalar_tensor_tensor(out=lo, in0=src, scalar=scale, in1=hi.bitcast(F32),
                                                           op0=ALU.mult, op1=ALU.subtract), a)

        def turn(src, dst, ring, half, ready, free=(), scale=None):
            done = []
            for k in range(2):
                s, fr = ring.take()
                b = s.parts[0]
                for c in range(4):
                    t = pe.op(lambda e, c=c, k=k, b=b: e.transpose(b[:, c * 128:(c + 1) * 128],
                              src[:, half * 4 + c, k * 128:(k + 1) * 128], ident), ready[c], t_sm, *fr,
                              signal=c == 3)
                sl = slice(half * 512, half * 512 + 512)
                t = split_from(dst[0][:, k, sl], dst[1][:, k, sl], b[:, :], t, *free,
                               scale=None if scale is None else scale[:, k:k + 1])
                s.free = (t,)
                done.append(t)
            return done[-1]

        def tilemean(src, half, ready):
            for c in range(4):
                t = half * 4 + c
                a = dve.op(lambda e, t=t: e.bn_stats(st[:, t, :], src[:, t, :]), ready[c], signal=True)
                a = dve.op(lambda e, t=t: e.bn_aggr(mv[:, t, :], st[:, t, :]), a)
            return a

        def rsqrt_small(o, i, *tokens):
            n = i.shape[-1]
            return pool.op(lambda e: e.tensor_tensor(o, i, negh[:, 0:n], ALU.pow), t_negh, *tokens)

        def layernorm(src, dst, half, ready, free=()):
            a = tilemean(src, half, ready)
            hs = slice(half * 4, half * 4 + 4)
            a = dve.op(lambda e: e.tensor_scalar(ve[:, hs], mv[:, hs, 1], 1e-5, None, ALU.add), a)
            p = rsqrt_small(rs[:, hs], ve[:, hs], a)
            out_ = []
            for c in range(4):
                t = half * 4 + c
                out_.append(dve.op(lambda e, t=t: e.tensor_scalar(dst[:, t, :], src[:, t, :], mv[:, t, 0:1],
                                   rs[:, t:t + 1], ALU.subtract, ALU.mult), p, *free))
            return out_

        l0 = ExitStack()
        VK = sb("VK", [128, NT, 16 * 33], ctx=l0)
        QKT = sb("QKT", [128, 4, T], ctx=l0)
        KB = [sb(f"KB{i}", [128, 8, 256], ctx=l0) for i in range(2)]
        P0 = [sb(f"P0{i}", [128, 4, 128], ctx=l0) for i in range(2)]
        P1 = [sb(f"P1{i}", [128, 2, 256], ctx=l0) for i in range(3)]
        SS = [sb(f"SS{i}", [128, 512], ctx=l0) for i in range(2)]
        PT = [sb(f"PT{i}", [128, 512], ctx=l0) for i in range(3)]
        QKf = [sb(f"QKf{i}", [128, 512], ctx=l0) for i in range(2)]
        QSf = [sb(f"QSf{i}", [128, 512], ctx=l0) for i in range(2)]
        QRf = [sb(f"QRf{i}", [128, 512], ctx=l0) for i in range(2)]
        sso = sb("sso", [128, NT, 32], ctx=l0)
        rq = sb("rq", [128, NT, 32], ctx=l0)
        CT = sb("CT", [128, 2, 2, 16], ctx=l0)
        ST = sb("ST", [128, 2, 2, 16], ctx=l0)
        identb = sb("identb", [128, 128], BF16, ctx=l0)
        mb0 = sb("mb0", [128, 512], BF16, ctx=l0)
        mb1 = sb("mb1", [128, 384], BF16, ctx=l0)
        gth = sb("gth", [128, 2, 64], ctx=l0)
        gsl = sb("gsl", [128, 2, 64], ctx=l0)
        gj = sb("gj", [128, 64], ctx=l0)
        gz = sb("gz", [128, NT], ctx=l0)
        gt = sb("gt", [128, NT], ctx=l0)
        gq = sb("gq", [128, NT], ctx=l0)
        mx = sb("mx", [128, 6, 4], ctx=l0)
        rc = sb("rc", [128, 4, 8], ctx=l0)
        rg = sb("rg", [128, 4, 8], ctx=l0)

        cosv = sm_("cos").rearrange("p (t d) -> p t d", t=2)
        sinv = sm_("sin").rearrange("p (t d) -> p t d", t=2)
        for s_, f_, nm in ((0, 0.25, "qs"), (1, 1.0, "ks")):
            sc = sm_(nm)
            full = sc.unsqueeze(1).to_broadcast([128, 2, 16])
            lowb = sc[:, 0:8].unsqueeze(1).to_broadcast([128, 2, 8])
            highb = sc[:, 8:16].unsqueeze(1).to_broadcast([128, 2, 8])
            dve.op(lambda e, s_=s_, f_=f_, full=full: e.scalar_tensor_tensor(
                out=CT[:, :, s_, :], in0=cosv, scalar=f_, in1=full, op0=ALU.mult, op1=ALU.mult), t_sm)
            dve.op(lambda e, s_=s_, f_=f_, highb=highb: e.scalar_tensor_tensor(
                out=ST[:, :, s_, 0:8], in0=sinv[:, :, 0:8], scalar=f_, in1=highb, op0=ALU.mult, op1=ALU.mult))
            t_tab = dve.op(lambda e, s_=s_, f_=f_, lowb=lowb: e.scalar_tensor_tensor(
                out=ST[:, :, s_, 8:16], in0=sinv[:, :, 8:16], scalar=f_, in1=lowb, op0=ALU.mult, op1=ALU.mult))
        t_cb = act.op(lambda e: e.copy(identb[:, :], ident), t_sm)
        t_cb = act.op(lambda e: e.copy(mb0[:, :], sm_("mask0")))
        t_cb = act.op(lambda e: e.copy(mb1[:, :], sm_("mask1")))
        for b in P1:
            t_p1z = pool.op(lambda e, b=b: e.memset(b[:, :, 0:64], 0.0))
        vk4 = VK[:, :, :].rearrange("p t (h e) -> p t h e", h=16)
        t_ones = pool.op(lambda e: e.memset(vk4[:, :, :, 32:33], 1.0))

        ring8 = bank_ring(range(8))
        t_h = [None, None]
        for half in range(2):
            hs = slice(half * 4, half * 4 + 4)
            xn = layernorm(XO, X1, half, [t_x[half]] * 4)
            a = dve.op(lambda e, hs=hs: e.tensor_tensor(v2[:, hs], rs[:, hs], rs[:, hs], ALU.mult))
            a = dve.op(lambda e, hs=hs: e.tensor_tensor(v2[:, hs], v2[:, hs], mv[:, hs, 1], ALU.mult), a)
            a = dve.op(lambda e, hs=hs: e.tensor_scalar(v2[:, hs], v2[:, hs], 1e-6, None, ALU.add), a)
            p = rsqrt_small(r2[:, hs], v2[:, hs], a)
            rd = [dve.op(lambda e, t=t: e.tensor_scalar(NB[:, t, :], X1[:, t, :], r2[:, t:t + 1], None, ALU.mult), p,
                         xn[t % 4]) for t in range(half * 4, half * 4 + 4)]
            t_h[half] = turn(NB, AT, ring8, half, rd, scale=sm_("nw")[:, 0:2])

        qkf = Ring([Slot(b) for b in QKf])
        qsf = Ring([Slot(b) for b in QSf])
        qrf = Ring([Slot(b) for b in QRf])
        w0h, w0l, t_w0 = chunk("qkv0")
        w1h, w1l, t_w1 = chunk("qkv1")
        t_vk = [None] * NT
        t_qkt = [None] * NT
        t_gz = None
        later = []

        def qk_turn(t, s, ready):
            q = s.parts[0]
            bs, fr = ring8.take()
            b = bs.parts[0]
            for c in range(4):
                p = pe.op(lambda e, c=c: e.transpose(b[:, c * 128:(c + 1) * 128], q[:, c * 128:(c + 1) * 128], ident),
                          ready, *fr, signal=c == 3)
            t_qkt[t] = act.op(lambda e: e.copy(QKT[:, :, t * 128:(t + 1) * 128],
                                               b[:, :].rearrange("p (c n) -> p c n", c=4)), p)
            bs.free = (t_qkt[t],)
            s.free = (p, t_vk[t])

        for t in range(NT):
            tt = t % 2
            ts_ = slice(t * 128, (t + 1) * 128)
            sa, fa = ring8.take()
            sv, fv = ring8.take()
            ba, bv = sa.parts[0], sv.parts[0]
            xs = [(AT[0][:, k, ts_], AT[1][:, k, ts_]) for k in range(2)]
            pa = mm3(ba[:, :], [(xs[0], (w0h[:, 0:512], w0l[:, 0:512])), (xs[1], (w1h[:, 0:512], w1l[:, 0:512]))],
                     t_h[t // 4], t_w0, t_w1, *fa)
            pv = mm3(bv[:, 0:320], [(xs[0], (w0h[:, 512:832], w0l[:, 512:832])),
                                    (xs[1], (w1h[:, 512:832], w1l[:, 512:832]))], *fv)
            s1, f1 = qkf.take()
            s2, f2 = qsf.take()
            s3, f3 = qrf.take()
            QK, QS, QR = s1.parts[0], s2.parts[0], s3.parts[0]
            a1 = act.op(lambda e, ba=ba, QS=QS: e.activation(QS[:, :], ba[:, :], ACT.Square), pa, *f2)
            a2 = act.op(lambda e, ba=ba, QK=QK: e.copy(QK[:, :], ba[:, :]), *f1)
            sa.free = (a2,)
            a3 = act.op(lambda e, bv=bv, t=t: e.copy(vk4[:, t, :, 0:16], bv[:, 0:256].rearrange("p (h d) -> p h d", h=16)),
                        pv)
            a4 = act.op(lambda e, bv=bv, tt=tt: e.activation(gth[:, tt, :], bv[:, 256:320], ACT.Tanh, scale=0.5),
                        *([t_gz] if t_gz else []))
            d = dve.op(lambda e, QS=QS, t=t: e.tensor_reduce(sso[:, t, :], QS[:, :].rearrange("p (h d) -> p h d", d=16),
                                                             AX_X, ALU.add), a1)
            d = dve.op(lambda e, t=t: e.tensor_scalar(sso[:, t, :], sso[:, t, :], 1.0 / 16, 1e-6, ALU.mult, ALU.add), d)
            p = rsqrt_small(rq[:, t, :], sso[:, t, :], d)
            d = dve.op(lambda e, bv=bv, tt=tt: e.scalar_tensor_tensor(out=gsl[:, tt, :], in0=gth[:, tt, :], scalar=1.0,
                       in1=bv[:, 256:320], op0=ALU.add, op1=ALU.mult), a4)
            sv.free = (d,)
            t_gz = dve.op(lambda e, tt=tt, t=t: e.tensor_tensor_reduce(gj[:, :], gsl[:, tt, :], sm_("ggw2"), 0.5, 0.0,
                          ALU.mult, ALU.add, gz[:, t:t + 1]), d, *([t_gz] if t_gz else []))
            d = dve.op(lambda e, QK=QK, t=t: e.tensor_tensor(
                QK[:, :].rearrange("p (h d) -> p h d", d=16), QK[:, :].rearrange("p (h d) -> p h d", d=16),
                rq[:, t, :].unsqueeze(2).to_broadcast([128, 32, 16]), ALU.mult), a2, p)
            q4 = QK[:, :].rearrange("p (s h d) -> p s h d", s=2, d=16)
            o4 = QS[:, :].rearrange("p (s h d) -> p s h d", s=2, d=16)
            r4 = QR[:, :].rearrange("p (s h d) -> p s h d", s=2, d=16)
            for lo_ in (0, 8):
                pq = []
                for s_ in range(2):
                    pq.append(pool.op(lambda e, lo_=lo_, s_=s_, q4=q4, o4=o4, tt=tt: e.tensor_tensor(
                        o4[:, s_, :, lo_:lo_ + 8], q4[:, s_, :, 8 - lo_:16 - lo_],
                        ST[:, tt, s_, lo_:lo_ + 8].unsqueeze(1).to_broadcast([128, 16, 8]), ALU.mult), d, t_tab))
            for s_ in range(2):
                dc = dve.op(lambda e, s_=s_, q4=q4, r4=r4, tt=tt: e.tensor_tensor(
                    r4[:, s_], q4[:, s_], CT[:, tt, s_, :].unsqueeze(1).to_broadcast([128, 16, 16]), ALU.mult), d, *f3)
            dr = dve.op(lambda e, QR=QR, QS=QS: e.tensor_tensor(QR[:, :], QR[:, :], QS[:, :], ALU.add), dc, pq[-1])
            s1.free = (dc, pq[-1])
            s2.free = (dr,)
            ag = act.op(lambda e, t=t: e.activation(gt[:, t:t + 1], gz[:, t:t + 1], ACT.Tanh, scale=0.5), t_gz)
            dg = dve.op(lambda e, t=t, tt=tt: e.scalar_tensor_tensor(out=gq[:, t:t + 1], in0=gt[:, t:t + 1], scalar=1.0,
                        in1=sm_("dk")[:, tt:tt + 1], op0=ALU.add, op1=ALU.mult), ag)
            t_vk[t] = dve.op(lambda e, QR=QR, t=t, tt=tt: e.tensor_scalar(
                vk4[:, t, :, 16:32], QR[:, 256:512].rearrange("p (h d) -> p h d", d=16),
                gq[:, t:t + 1], None, ALU.mult), dr, dg)
            later.append((t, s3, dr, a3))
            if t >= 1:
                u = later.pop(0)
                qk_turn(*u[:3])
        last_qkv = pv
        chunk_done("qkv0", last_qkv)
        chunk_done("qkv1", last_qkv)
        u = later.pop(0)
        qk_turn(*u[:3])
        t_v = a3
        ring_done(ring8, range(8))

        rS, rT, rO = bank_ring((0, 1, 2)), bank_ring((3, 4)), bank_ring((5, 6, 7))
        pr0 = Ring([Slot(b) for b in P0])
        pr1 = Ring([Slot(b) for b in P1])
        ssr = Ring([Slot(b) for b in SS])
        ptr = Ring([Slot(b) for b in PT])
        mxr = Ring([Slot(mx[:, i, :]) for i in range(6)])
        rcr = Ring([Slot(rc[:, i, :], rg[:, i, :]) for i in range(4)])
        kbr = Ring([Slot(b) for b in KB])
        units = []
        for b in range(4):
            for g in range(2):
                for c in range(2):
                    units.append((b, g, 0, 4 * c, 4))
                for c in range(4):
                    units.append((b, g, 1, 2 * c, 2))
        kb_now = {}

        def make_kb(b, g):
            s, fr = kbr.take()
            for h in range(8):
                eng = dve if h % 2 else pool
                tk = eng.op(lambda e, h=h, s=s: e.tensor_scalar(
                    s.parts[0][:, h, :], QKT[:, 2 + g, b * 256:(b + 1) * 256], sm_("mh")[:, h:h + 1], 0.0,
                    ALU.mult, ALU.add), t_qkt[2 * b], t_qkt[2 * b + 1], *fr)
                if h == 6:
                    tp = tk
            kb_now[(b, g)] = (s, (tp, tk))

        def scores(u):
            b, g, qt, h0, nh = u
            kb, tk = kb_now[(b, g)]
            s, fr = rS.take()
            bk = s.parts[0]
            n = 512 if qt == 0 else 384
            cols = slice(0, 128) if qt == 0 else slice(64, 256)
            pe.op(lambda e: e.matmul(bk[:, 0:n], QKT[:, g, b * 256 + qt * 128:b * 256 + qt * 128 + 128],
                                     kb.parts[0][:, h0:h0 + nh, cols], start=True, stop=False), *tk, *fr, signal=False)
            p = pe.op(lambda e: e.matmul(bk[:, 0:n], identb[:, :], (mb0 if qt == 0 else mb1)[:, :], start=False,
                                         stop=True), t_cb)
            if h0 + nh == 8 and qt == 1:
                kb.free = (p,)
            sm1, fm = mxr.take()
            m = sm1.parts[0]
            v = bk[:, 0:n].rearrange("p (h k) -> p h k", h=nh)
            d1 = dve.op(lambda e: e.tensor_reduce(m[:, 0:nh], v, AX_X, ALU.max), p, *fm)
            s2, f2 = ssr.take()
            d2 = dve.op(lambda e: e.tensor_tensor(s2.parts[0][:, 0:n].rearrange("p (h k) -> p h k", h=nh), v,
                                                  m[:, 0:nh].unsqueeze(2).to_broadcast([128, nh, n // nh]),
                                                  ALU.subtract), d1, *f2)
            s.free = (d2,)
            sm1.free = (d2,)
            s3, f3 = (pr0 if qt == 0 else pr1).take()
            dst = s3.parts[0][:, :, :] if qt == 0 else s3.parts[0][:, :, 64:256]
            a = act.op(lambda e: e.activation(dst, s2.parts[0][:, 0:n].rearrange("p (h k) -> p h k", h=nh), ACT.Exp),
                       d2, *f3)
            s2.free = (a,)
            return s3, a

        def turns(u, s3, a):
            b, g, qt, h0, nh = u
            s, fr = rT.take()
            bk = s.parts[0]
            pf = s3.parts[0][:, :, :].rearrange("p h k -> p (h k)")
            for c in range(4):
                p = pe.op(lambda e, c=c: e.transpose(bk[:, c * 128:(c + 1) * 128], pf[:, c * 128:(c + 1) * 128], ident),
                          a, t_p1z, *fr, signal=c == 3)
            s3.free = (p,)
            s4, f4 = ptr.take()
            a = act.op(lambda e: e.copy(s4.parts[0][:, :], bk[:, :]), p, *f4)
            s.free = (a,)
            return s4, a

        obank = {}

        def weigh(u, s4, a):
            b, g, qt, h0, nh = u
            t = 2 * b + qt
            if h0 == 0:
                obank[(b, g, qt)] = rO.take()
            so, fo = obank[(b, g, qt)]
            bk = so.parts[0]
            for i in range(nh):
                h = h0 + i
                o = bk[:, h * 33:(h + 1) * 33]
                H = 8 * g + h
                if qt == 0:
                    p = pe.op(lambda e, o=o, i=i, H=H: e.matmul(o, s4.parts[0][:, i * 128:(i + 1) * 128], vk4[:, t, H, :],
                              start=True, stop=True), a, t_v, t_ones, t_vk[t], *fo, signal=i == nh - 1)
                else:
                    for k in range(2):
                        p = pe.op(lambda e, o=o, i=i, k=k, H=H: e.matmul(
                            o, s4.parts[0][:, (2 * i + k) * 128:(2 * i + k + 1) * 128], vk4[:, t - 1 + k, H, :],
                            start=k == 0, stop=k == 1), a, t_v, t_ones, t_vk[t], *fo,
                            signal=i == nh - 1 and k == 1)
            s4.free = (p,)
            if h0 + nh < 8:
                return
            o3 = bk[:, 0:264].rearrange("p (h e) -> p h e", h=8)
            sr, fr = rcr.take()
            c1, c2 = sr.parts
            d = dve.op(lambda e: e.reciprocal(c1, o3[:, :, 32]), p, *fr)
            d1 = dve.op(lambda e: e.tensor_scalar(c2, c1, sm_("dq")[:, qt:qt + 1], None, ALU.mult), d)
            hd = slice(g * 128, g * 128 + 128)
            d2 = dve.op(lambda e: e.tensor_tensor(AO[:, t, hd].rearrange("p (h d) -> p h d", d=16), o3[:, :, 0:16],
                                                  c1.unsqueeze(2).to_broadcast([128, 8, 16]), ALU.mult))
            d3 = dve.op(lambda e: e.tensor_tensor(NB[:, t, hd].rearrange("p (h d) -> p h d", d=16), o3[:, :, 16:32],
                                                  c2.unsqueeze(2).to_broadcast([128, 8, 16]), ALU.mult), d1, t_h[1])
            so.free = (d3,)
            sr.free = (d3,)
            t_ao[t] = d3

        t_ao = [None] * NT
        make_kb(0, 0)
        s_out_, t_out_ = {}, {}
        n = len(units)
        for i in range(n + 3):
            if i < n:
                if i % 6 == 3 and i // 6 + 1 < 8:
                    j = i // 6 + 1
                    make_kb(j // 2, j % 2)
                s_out_[i] = scores(units[i])
            if 0 <= i - 2 < n:
                t_out_[i - 2] = turns(units[i - 2], *s_out_[i - 2])
            if 0 <= i - 3 < n:
                weigh(units[i - 3], *t_out_[i - 3])
        ring_done(rS, (0, 1, 2))
        ring_done(rT, (3, 4))
        ring_done(rO, (5, 6, 7))
        l0.close()

        mlp = ExitStack()
        T1 = [sb(f"T1{i}", [128, 512], ctx=mlp) for i in range(2)]
        T2 = [sb(f"T2{i}", [128, 512], ctx=mlp) for i in range(2)]
        HH = [(sb(f"HHh{i}", [128, 512], R32, ctx=mlp), sb(f"HHl{i}", [128, 512], R32, ctx=mlp)) for i in range(3)]
        t1r = Ring([Slot(b) for b in T1])
        t2r = Ring([Slot(b) for b in T2])
        hr = Ring([Slot(*b) for b in HH])
        l0_end = (t_ao[7], pe_last(pe), act_last(act), dve_last(dve), pool_last(pool))
        for r in (t1r, t2r, hr):
            for s in r.slots:
                s.free = l0_end

        def run_mlp(steps, xin, ready, act_fn, names, combine=None, tail=None):
            ring = bank_ring((4, 5, 6, 7))
            ytok = [None] * NT
            yfree = [bank_free[i] for i in range(4)]
            pend = []

            def down(j, half, name, woff, hslot, th, final):
                hi, lo, _ = chunk(name)
                for c in range(4):
                    t = half * 4 + c
                    yb = banks[t // 2][:, (t % 2) * 256:(t % 2) * 256 + 256]
                    tk = mm3(yb, [((hslot.parts[0][:, c * 128:(c + 1) * 128], hslot.parts[1][:, c * 128:(c + 1) * 128]),
                                   (hi[:, woff:woff + 256], lo[:, woff:woff + 256]))], th, *(yfree[t // 2] if j == 0 else ()),
                             first=(j == 0 and t % 2 == 0), last=final, skip=True, signal=True)
                    ytok[t] = tk
                hslot.free = (tk,)
                if half == 1:
                    chunk_done(name, tk)

            for j, (name, gated, cc) in enumerate(steps):
                hi, lo, tw = chunk(name)
                for half in range(2):
                    sl = slice(half * 512, half * 512 + 512)
                    xs = [(xin[0][:, k, sl], xin[1][:, k, sl]) for k in range(2)]
                    got = []
                    if cc is not None:
                        sc, fc = ring.take()
                        pc = combine(sc.parts[0], cc, sl, *fc)
                    for part in range(2 if gated else 1):
                        sg, fg = ring.take()
                        o = part * 256
                        pg = mm3(sg.parts[0][:, :], [((hi[:, o + k * 128:o + k * 128 + 128], lo[:, o + k * 128:o + k * 128 + 128]),
                                                      xs[k]) for k in range(2)], tw, ready[half], *fg)
                        got.append((sg, pg))
                    s1, f1 = t1r.take()
                    s2, f2 = t2r.take()
                    A, B = s1.parts[0], s2.parts[0]
                    sg, pg = got[0]
                    a = act.op(lambda e, A=A, g=sg.parts[0]: e.activation(A[:, :], g[:, :], ACT.Silu), pg, *f1)
                    sg.free = (a,)
                    if gated:
                        su, pu = got[1]
                        d = dve.op(lambda e, A=A, B=B, u=su.parts[0]: e.tensor_tensor(B[:, :], A[:, :], u[:, :], ALU.mult),
                                   a, pu, *f2)
                        su.free = (d,)
                        s1.free = (d,)
                        if cc is not None:
                            d = dve.op(lambda e, B=B, u=sc.parts[0]: e.tensor_tensor(B[:, :], B[:, :], u[:, :], ALU.mult),
                                       d, pc)
                            sc.free = (d,)
                    else:
                        d = dve.op(lambda e, A=A, B=B: e.scalar_tensor_tensor(out=B[:, :], in0=A[:, :], scalar=1.0,
                                   in1=A[:, :], op0=ALU.add, op1=ALU.mult), a, *f2)
                        s1.free = (d,)
                    s3, f3 = hr.take()
                    th = split_from(s3.parts[0][:, :], s3.parts[1][:, :], B[:, :], d, *f3)
                    s2.free = (th,)
                    pend.append((j, half, name, 512 if gated else 256, s3, th, j == len(steps) - 1))
                    if len(pend) > 1:
                        down(*pend.pop(0))
            while pend:
                down(*pend.pop(0))
            ring_done(ring, (4, 5, 6, 7))
            return ytok

        def ybank(t):
            return banks[t // 2][:, (t % 2) * 256:(t % 2) * 256 + 256]

        ring8 = bank_ring(range(8))
        t_qm = [turn(NB, AT, ring8, half, t_ao[half * 4:half * 4 + 4]) for half in range(2)]
        t_at = [turn(AO, BT, ring8, half, t_ao[half * 4:half * 4 + 4]) for half in range(2)]
        hi, lo, tw = chunk("wo")
        t_ow = []
        for t in range(NT):
            s, fr = ring8.take()
            b = s.parts[0]
            ts_ = slice(t * 128, (t + 1) * 128)
            p = mm3(b[:, 0:256], [((BT[0][:, k, ts_], BT[1][:, k, ts_]), (hi[:, k * 256:k * 256 + 256], lo[:, k * 256:k * 256 + 256]))
                                  for k in range(2)], tw, t_at[t // 4], *fr)
            a = act.op(lambda e, b=b, t=t: e.copy(AO[:, t, :], b[:, 0:256]), p)
            s.free = (a,)
            t_ow.append(a)
        chunk_done("wo", p)
        ring_done(ring8, range(8))
        y = run_mlp([(f"mem{j}", False, None) for j in range(8)], AT, t_qm, None, None)
        t_x1, t_xo = [], []
        for t in range(NT):
            s1, f1 = t1r.take()
            A = s1.parts[0]
            a = act.op(lambda e, A=A, t=t: e.activation(A[:, 0:256], ybank(t), ACT.Tanh, scale=0.5), y[t], y[t | 1], *f1)
            bank_free[t // 2] = (a,)
            d = dve.op(lambda e, A=A, t=t: e.scalar_tensor_tensor(out=A[:, 0:256], in0=A[:, 0:256], scalar=1.0,
                       in1=AO[:, t, :], op0=ALU.add, op1=ALU.mult), a, t_ow[t])
            d = dve.op(lambda e, A=A, t=t: e.scalar_tensor_tensor(out=X1[:, t, :], in0=A[:, 0:256], scalar=0.5,
                       in1=X1[:, t, :], op0=ALU.mult, op1=ALU.add), d)
            s1.free = (d,)
            t_x1.append(d)
            t_xo.append(pool.op(lambda e, t=t: e.tensor_tensor(XO[:, t, :], XO[:, t, :], X1[:, t, :], ALU.add), d))
        ring4 = bank_ring((4, 5, 6, 7))
        t_h = [None, None]
        for half in range(2):
            hs = slice(half * 4, half * 4 + 4)
            a = tilemean(X1, half, t_x1[half * 4:half * 4 + 4])
            a = dve.op(lambda e, hs=hs: e.tensor_tensor(v2[:, hs], mv[:, hs, 0], mv[:, hs, 0], ALU.mult), a)
            a = dve.op(lambda e, hs=hs: e.scalar_tensor_tensor(out=v2[:, hs], in0=v2[:, hs], scalar=1e-6,
                       in1=mv[:, hs, 1], op0=ALU.add, op1=ALU.add), a)
            p = rsqrt_small(r2[:, hs], v2[:, hs], a)
            rd = [dve.op(lambda e, t=t: e.tensor_scalar(NB[:, t, :], X1[:, t, :], r2[:, t:t + 1], None, ALU.mult), p)
                  for t in range(half * 4, half * 4 + 4)]
            t_h[half] = turn(NB, BT, ring4, half, rd, scale=sm_("nw")[:, 2:4])
        ring_done(ring4, (4, 5, 6, 7))
        y = run_mlp([(f"ffn{j}", True, None) for j in range(6)], BT, t_h, None, None)
        t_x = []
        for t in range(NT):
            d = dve.op(lambda e, t=t: e.tensor_tensor(XO[:, t, :], XO[:, t, :], ybank(t), ALU.add), y[t], y[t | 1], t_xo[t])
            bank_free[t // 2] = (d,)
            t_x.append(d)

        ring4 = bank_ring((4, 5, 6, 7))
        t_h = [None, None]
        for half in range(2):
            rd = layernorm(XO, NB, half, t_x[half * 4:half * 4 + 4])
            t_h[half] = turn(NB, AT, ring4, half, rd)
        ring_done(ring4, (4, 5, 6, 7))
        ring8 = bank_ring((4, 5, 6, 7, 0, 1, 2, 3))
        hi, lo, tw = chunk("up")
        t_r = [None, None]
        for half in range(2):
            sl = slice(half * 512, half * 512 + 512)
            for m in range(2):
                s, fr = ring8.take()
                b = s.parts[0]
                p = mm3(b[:, :], [((hi[:, m * 256 + k * 128:m * 256 + k * 128 + 128], lo[:, m * 256 + k * 128:m * 256 + k * 128 + 128]),
                                   (AT[0][:, k, sl], AT[1][:, k, sl])) for k in range(2)], tw, t_h[half], *fr)
                a = act.op(lambda e, b=b, m=m, sl=sl: e.activation(BT[0][:, m, sl], b[:, :], ACT.Relu), p)
                d = dve.op(lambda e, b=b, m=m, sl=sl: e.scalar_tensor_tensor(
                    out=BT[1][:, m, sl], in0=b[:, :], scalar=0.0, in1=BT[0][:, m, sl].bitcast(F32), op0=ALU.max,
                    op1=ALU.subtract), a)
                s.free = (d,)
            t_r[half] = d
        chunk_done("up", p)
        hi, lo, tw = chunk("exp")
        top = sb("top", [128, NT, 8], ctx=mlp)
        e2 = sb("e2", [128, 4, NT], ctx=mlp)
        lg = []
        for t in range(NT):
            s, fr = ring8.take()
            b = s.parts[0]
            ts_ = slice(t * 128, (t + 1) * 128)
            p = mm3(b[:, 0:264], [((AT[0][:, k, ts_], AT[1][:, k, ts_]), (hi[:, k * 264:k * 264 + 264], lo[:, k * 264:k * 264 + 264]))
                                  for k in range(2)], tw, t_h[t // 4], *fr)
            d = dve.op(lambda e, b=b, t=t: e.max(top[:, t, :], b[:, 256:264]), p)
            a = act.op(lambda e, b=b, t=t: e.copy(AO[:, t, :], b[:, 0:256]), d)
            s.free = (a,)
            lg.append(a)
        chunk_done("exp", p)
        d = dve.op(lambda e: e.tensor_tensor(e2[:, 0, :], top[:, :, 1], top[:, :, 0], ALU.subtract), d)
        a = act.op(lambda e: e.activation(e2[:, 1, :], e2[:, 0, :], ACT.Exp), d)
        d = dve.op(lambda e: e.tensor_scalar(e2[:, 2, :], e2[:, 1, :], 1.0, None, ALU.add), a)
        d = dve.op(lambda e: e.reciprocal(e2[:, 3, :], e2[:, 2, :]), d)
        d = dve.op(lambda e: e.tensor_tensor(e2[:, 2, :], e2[:, 1, :], e2[:, 3, :], ALU.mult), d)
        t_rw = dve.op(lambda e: e.tensor_tensor(e2[:, 0, :], e2[:, 2, :], e2[:, 3, :], ALU.add), d)
        hi, lo, tw = chunk("down")
        t_x2 = []
        for t in range(NT):
            s, fr = ring8.take()
            b = s.parts[0]
            ts_ = slice(t * 128, (t + 1) * 128)
            p = mm3(b[:, 0:256], [((BT[0][:, k, ts_], BT[1][:, k, ts_]), (hi[:, k * 256:k * 256 + 256], lo[:, k * 256:k * 256 + 256]))
                                  for k in range(2)], tw, t_r[t // 4], *fr)
            d = dve.op(lambda e, t=t: e.scalar_tensor_tensor(out=XO[:, t, :], in0=AO[:, t, :], scalar=e2[:, 0, t:t + 1],
                       in1=XO[:, t, :], op0=ALU.mult, op1=ALU.add), t_rw, lg[t])
            d = dve.op(lambda e, b=b, t=t: e.tensor_tensor(XO[:, t, :], XO[:, t, :], b[:, 0:256], ALU.add), p, d)
            s.free = (d,)
            t_x2.append(d)
        chunk_done("down", p)
        ring_done(ring8, (4, 5, 6, 7, 0, 1, 2, 3))
        mlp_end = (pe_last(pe), act_last(act), dve_last(dve), pool_last(pool))
        mlp.close()

        l1 = ExitStack()
        NTW = (sb("NTh", [128, 8, 256], R32, ctx=l1), sb("NTl", [128, 8, 256], R32, ctx=l1))
        MTW = (sb("MTh", [128, 2, 1024], R32, ctx=l1), sb("MTl", [128, 2, 1024], R32, ctx=l1))
        RTW = (sb("RTh", [128, 2, 16], R32, ctx=l1), sb("RTl", [128, 2, 16], R32, ctx=l1))
        bout = sb("bout", [128, 256], ctx=l1)
        QH = [(sb(f"QHh{i}", [128, 8, 256], R32, ctx=l1), sb(f"QHl{i}", [128, 8, 256], R32, ctx=l1)) for i in range(2)]
        UT = (sb("UTh", [128, 8, 256], R32, ctx=l1), sb("UTl", [128, 8, 256], R32, ctx=l1))
        CD = (sb("CDh", [128, T], R32, ctx=l1), sb("CDl", [128, T], R32, ctx=l1))
        CN = sb("CN", [128, NT, 64], ctx=l1)
        rr = sb("rr", [128, NT, 16], ctx=l1)
        rrs = sb("rrs", [128, NT, 16], ctx=l1)
        PB = [sb(f"PB{i}", [128, 2, 256], ctx=l1) for i in range(3)]
        PN = [sb(f"PN{i}", [128, 512], ctx=l1) for i in range(3)]
        sml = sb("sml", [128, 6, 10], ctx=l1)

        ring4 = bank_ring((4, 5, 6, 7))
        f_m0, f_m1, f_n, f_b = bank_ring((0, 1)), bank_ring((2, 3)), bank_ring((4, 5, 6)), bank_ring((7,))
        sbias, fb = f_b.take()
        sm_split = []
        h_t = [None, None]

        def fuse(h):
            raw, _, tw = chunk(f"fuse{h}")
            uq, uk, uv, wo_ = raw[:, 0:256], raw[:, 256:321], raw[:, 321:385], raw[:, 386:642]
            buv = raw[:, 385:386]
            if h % 4 == 0:
                fuse.m = [f_m0.take(), f_m1.take()]
            if h % 4 == 0:
                fuse.tok = []
            for k in range(2):
                s, fr = fuse.m[k]
                p = pe.op(lambda e, s=s, k=k, h=h: e.matmul(s.parts[0][:, (h % 4) * 65:(h % 4) * 65 + 65],
                          uq[:, k * 128:(k + 1) * 128], uk, start=True, stop=True), tw, *fr)
            if h % 2 == 0:
                fuse.n = f_n.take()
            s, fr = fuse.n
            lo_ = 64 * (h % 2)
            pn = pe.op(lambda e, s=s, lo_=lo_: e.matmul(s.parts[0][lo_:lo_ + 64, 0:256], uv, wo_, start=True, stop=True), *fr)
            pb = pe.op(lambda e, h=h: e.matmul(sbias.parts[0][:, 0:256], buv.to_broadcast([128, 128]), wo_, start=h == 0,
                                               stop=h == 15), *fb)
            chunk_done(f"fuse{h}", pb)
            if h % 2 == 1:
                j = h // 2
                t = split_from(NTW[0][:, j, :], NTW[1][:, j, :], s.parts[0][:, 0:256], pn, *mlp_end)
                s.free = (t,)
            if h % 4 == 3:
                j = h // 4
                for k in range(2):
                    s, fr = fuse.m[k]
                    v = s.parts[0][:, 0:260].rearrange("p (h c) -> p h c", c=65)
                    mh_, ml_ = (m[:, k, j * 256:j * 256 + 256].rearrange("p (h c) -> p h c", c=64) for m in MTW)
                    t = split_from(mh_, ml_, v[:, :, 0:64], p, *mlp_end)
                    t = split_from(RTW[0][:, k, 4 * j:4 * j + 4], RTW[1][:, k, 4 * j:4 * j + 4], v[:, :, 64], t)
                    s.free = (t,)
                fuse.done = t
            if h == 15:
                fuse.bias = dve.op(lambda e: e.tensor_tensor(bout[:, :], sbias.parts[0][:, 0:256], sm_("bo"), ALU.add), pb)
                sbias.free = (fuse.bias,)

        rd = [layernorm(XO, NB, half, t_x2[half * 4:half * 4 + 4]) for half in range(2)]
        for h in range(16):
            fuse(h)
        ring_done(f_m0, (0, 1))
        ring_done(f_m1, (2, 3))
        ring_done(f_n, (4, 5, 6))
        ring_done(f_b, (7,))
        ring8 = bank_ring(range(8))
        t_h = [turn(NB, AT, ring8, half, rd[half]) for half in range(2)]
        hi, lo, tw = chunk("proj")
        cb = sm_("cb")
        t_c, t_cq = [], []
        for half in range(2):
            sl = slice(half * 512, half * 512 + 512)
            for m in range(3):
                s, fr = ring8.take()
                b = s.parts[0]
                p = mm3(b[:, :], [((hi[:, k * 384 + m * 128:k * 384 + m * 128 + 128], lo[:, k * 384 + m * 128:k * 384 + m * 128 + 128]),
                                   (AT[0][:, k, sl], AT[1][:, k, sl])) for k in range(2)], tw, t_h[half], *fr)
                ho, lo2 = (CD[0][:, sl], CD[1][:, sl]) if m == 0 else (BT[0][:, m - 1, sl], BT[1][:, m - 1, sl])
                a = act.op(lambda e, b=b, m=m, ho=ho: e.activation(ho, b[:, :], ACT.Identity, bias=cb[:, m:m + 1]), p)
                d = dve.op(lambda e, b=b, m=m, ho=ho, lo2=lo2: e.scalar_tensor_tensor(
                    out=lo2, in0=b[:, :], scalar=cb[:, m:m + 1], in1=ho.bitcast(F32), op0=ALU.add, op1=ALU.subtract), a)
                if m == 0:
                    d = dve.op(lambda e, b=b, sl=sl: e.tensor_scalar(X1[:, sl2(sl), :].rearrange("p t d -> p (t d)")[:, 0:512],
                               b[:, :], cb[:, 0:1], None, ALU.add))
                    t_c.append(d)
                s.free = (d,)
            t_cq.append(d)
        chunk_done("proj", p)
        for half in range(2):
            s, fr = ring8.take()
            b = s.parts[0]
            cf = X1[:, half * 2:half * 2 + 2, :].rearrange("p t d -> p (t d)")
            for c in range(4):
                p = pe.op(lambda e, c=c, b=b, cf=cf: e.transpose(b[:, c * 64:c * 64 + 64], cf[0:64, c * 128:(c + 1) * 128],
                          ident[0:64, 0:64]), t_c[half], *fr)
            t_cn = act.op(lambda e, b=b, half=half: e.copy(CN[:, half * 4:half * 4 + 4, :],
                          b[:, 0:256].rearrange("p (t c) -> p t c", c=64)), p)
            s.free = (t_cn,)
        s, fr = ring8.take()
        for t in range(NT):
            ts_ = slice(t * 128, (t + 1) * 128)
            p = mm3(s.parts[0][:, t * 16:(t + 1) * 16], [((BT[0][:, k, ts_], BT[1][:, k, ts_]),
                    (RTW[0][:, k, :], RTW[1][:, k, :])) for k in range(2)], t_cq[t // 4], fuse.done, *fr)
        SC = float(1.0 / np.sqrt(128.0))
        a = dve.op(lambda e, s=s: e.tensor_copy(rr[:, :, :], s.parts[0][:, 0:128].rearrange("p (t h) -> p t h", h=16)), p)
        t_rr = dve.op(lambda e: e.tensor_scalar(rrs[:, :, :], rr[:, :, :], SC, None, ALU.mult), a)
        s.free = (a,)
        ring_done(ring8, range(8))

        rS, rT, rU, rM = bank_ring((0, 1, 2)), bank_ring((3, 4)), bank_ring((5, 6)), bank_ring((7,))
        pbr = Ring([Slot(b) for b in PB])
        pnr = Ring([Slot(b) for b in PN])
        smr = Ring([Slot(sml[:, i, :]) for i in range(6)])
        qhr = Ring([Slot(*q) for q in QH])
        qh = {}
        tq = {}

        def latent_q(b, j2):
            if j2 == 0:
                qh[b] = qhr.take()
            sq, fq = qh[b]
            s, fr = rM.take()
            bk = s.parts[0]
            bs_ = slice(b * 256, b * 256 + 256)
            for i in range(2):
                j = 2 * j2 + i
                p = mm3(bk[:, i * 256:i * 256 + 256], [((MTW[0][:, k, j * 128:j * 128 + 128], MTW[1][:, k, j * 128:j * 128 + 128]),
                        (BT[0][:, k, bs_], BT[1][:, k, bs_])) for k in range(2)], t_cq[b // 2], fuse.done, *fr)
            t = split_from(sq.parts[0][:, 2 * j2:2 * j2 + 2, :].rearrange("p j n -> p (j n)"),
                           sq.parts[1][:, 2 * j2:2 * j2 + 2, :].rearrange("p j n -> p (j n)"), bk[:, :], p, *fq)
            s.free = (t,)
            tq[(b, j2)] = t

        def l1_scores(b, h):
            sq, _ = qh[b]
            j, o = h // 2, 64 * (h % 2)
            s, fr = rS.take()
            bk = s.parts[0]
            kv = [c[o:o + 64, b * 256:b * 256 + 256] for c in CD]
            for qt in range(2):
                p = mm3(bk[:, qt * 256:qt * 256 + 256], [(tuple(q[o:o + 64, j, qt * 128:qt * 128 + 128] for q in sq.parts), kv)],
                        tq[(b, j // 2)], t_c[b // 2], *fr)
            if h == 15:
                sq.free = (p,)
            v = bk[:, :].rearrange("p (q k) -> p q k", q=2)
            ss, fs = smr.take()
            m = ss.parts[0]
            d = dve.op(lambda e: e.tensor_reduce(m[:, 0:2], v, AX_X, ALU.max), p, *fs)
            rv, rsv = rr[:, 2 * b:2 * b + 2, h], rrs[:, 2 * b:2 * b + 2, h]
            d = dve.op(lambda e: e.tensor_tensor(m[:, 2:4], m[:, 0:2], rv, ALU.add), d, t_rr)
            d = dve.op(lambda e: e.scalar_tensor_tensor(out=m[:, 4:6], in0=m[:, 2:4], scalar=-SC, in1=rsv, op0=ALU.mult,
                                                        op1=ALU.add), d)
            sp_, fp = pbr.take()
            P = sp_.parts[0]
            for qt in range(2):
                a = act.op(lambda e, qt=qt: e.activation(P[:, qt, :], v[:, qt, :], ACT.Exp, bias=m[:, 4 + qt:5 + qt], scale=SC,
                                                         accum_out=m[:, 6 + qt:7 + qt]), d, *fp)
            s.free = (a,)
            d = dve.op(lambda e: e.reciprocal(m[:, 8:10], m[:, 6:8]), a)
            for qt in range(2):
                d2 = dve.op(lambda e, qt=qt: e.tensor_scalar(P[:, qt, :], P[:, qt, :], m[:, 8 + qt:9 + qt], None, ALU.mult), d)
            ss.free = (d2,)
            return sp_, d2

        def l1_turns(b, h, sp_, d):
            s, fr = rT.take()
            bk = s.parts[0]
            P = sp_.parts[0]
            for kc in range(2):
                for qt in range(2):
                    p = pe.op(lambda e, kc=kc, qt=qt: e.transpose(bk[:, kc * 256 + qt * 128:kc * 256 + qt * 128 + 128],
                              P[:, qt, kc * 128:kc * 128 + 128], ident), d, *fr, signal=kc == 1 and qt == 1)
            sp_.free = (p,)
            s4, f4 = pnr.take()
            a = (act if h % 2 else act).op(lambda e: e.copy(s4.parts[0][:, :], bk[:, :]), p, *f4)
            s.free = (a,)
            return s4, a

        ub = {}
        ut_free = [()]
        ut_tok = {}

        def l1_weigh(b, h, s4, a):
            j, o = h // 2, 64 * (h % 2)
            if h % 2 == 0:
                ub[(b, j)] = rU.take()
            s, fr = ub[(b, j)]
            bk = s.parts[0]
            for kc in range(2):
                p = pe.op(lambda e, kc=kc: e.matmul(bk[o:o + 64, 0:256], CN[:, 2 * b + kc, :], s4.parts[0][:, kc * 256:kc * 256 + 256],
                                                    start=kc == 0, stop=kc == 1), a, t_cn, *fr, signal=kc == 1)
            s4.free = (p,)
            if h % 2 == 1:
                t = split_from(UT[0][:, j, :], UT[1][:, j, :], bk[:, 0:256], p, *ut_free[0])
                s.free = (t,)
                ut_tok[b] = t

        t_x3 = [None] * NT

        def l1_out(b, qt):
            s, fr = rM.take()
            bk = s.parts[0]
            t = 2 * b + qt
            qs_ = slice(qt * 128, qt * 128 + 128)
            p = mm3(bk[:, 0:256], [((UT[0][:, j, qs_], UT[1][:, j, qs_]), (NTW[0][:, j, :], NTW[1][:, j, :])) for j in range(8)],
                    ut_tok[b], *fr)
            if qt == 1:
                ut_free[0] = (p,)
            d = dve.op(lambda e: e.tensor_tensor(XO[:, t, :], XO[:, t, :], bk[:, 0:256], ALU.add), p)
            s.free = (d,)
            t_x3[t] = dve.op(lambda e: e.tensor_tensor(XO[:, t, :], XO[:, t, :], bout[:, :], ALU.add), d, fuse.bias)

        for j2 in range(4):
            latent_q(0, j2)
        us = [(b, h) for b in range(4) for h in range(16)]
        so_, to_ = {}, {}
        for i in range(len(us) + 3):
            if i < len(us):
                so_[i] = l1_scores(*us[i])
                b, h = us[i]
                if h in (6, 8, 10, 12) and b < 3:
                    latent_q(b + 1, (h - 6) // 2)
            if 0 <= i - 2 < len(us):
                to_[i - 2] = l1_turns(*us[i - 2], *so_[i - 2])
            if 0 <= i - 3 < len(us):
                l1_weigh(*us[i - 3], *to_[i - 3])
                if us[i - 3][1] == 15:
                    l1_out(us[i - 3][0], 0)
                    l1_out(us[i - 3][0], 1)
        ring_done(rS, (0, 1, 2))
        ring_done(rT, (3, 4))
        ring_done(rU, (5, 6))
        ring_done(rM, (7,))
        l1_end = (pe_last(pe), act_last(act), dve_last(dve), pool_last(pool))
        l1.close()

        m1 = ExitStack()
        T1 = [sb(f"U1{i}", [128, 512], ctx=m1) for i in range(2)]
        T2 = [sb(f"U2{i}", [128, 512], ctx=m1) for i in range(3)]
        HH = [(sb(f"VVh{i}", [128, 512], R32, ctx=m1), sb(f"VVl{i}", [128, 512], R32, ctx=m1)) for i in range(3)]
        SELf = sb("SELf", [32, 22 * 128], ctx=m1)
        SELr = sb("SELr", [32, 22 * 128], R32, ctx=m1)
        CTr = sb("CTr", [32, T], R32, ctx=m1)
        pr = sb("pr", [128, NT, 24], ctx=m1)
        rp = sb("rp", [128, NT, 24], ctx=m1)
        tp8 = sb("tp8", [128, NT, 8], ctx=m1)
        nm = sb("nm", [128, 4, NT], ctx=m1)
        chr_ = sb("chr", [128, NT, 16], R32, ctx=m1)
        cl = sb("cl", [128, NT, 32], ctx=m1)
        t1r = Ring([Slot(b) for b in T1])
        t2r = Ring([Slot(b) for b in T2])
        hr = Ring([Slot(*b) for b in HH])
        for r in (t1r, t2r, hr):
            for s in r.slots:
                s.free = l1_end
        s_sel = semaphore("s_sel")
        t_sel = sp.dma(SELf[:, :], sel, s_sel, 16, *l1_end)
        t_sel = pool.op(lambda e: e.tensor_scalar(SELr[:, :], SELf[:, :], 1.0, 0.0, ALU.mult, ALU.add), t_sel)

        ring8 = bank_ring(range(8))
        t_h = [None, None]
        for half in range(2):
            rd = layernorm(XO, NB, half, t_x3[half * 4:half * 4 + 4])
            t_h[half] = turn(NB, AT, ring8, half, rd)
        hi, lo, tw = chunk("gate")
        s, fr = ring8.take()
        for t in range(NT):
            ts_ = slice(t * 128, (t + 1) * 128)
            p = mm3(s.parts[0][:, t * 16:(t + 1) * 16], [((AT[0][:, k, ts_], AT[1][:, k, ts_]),
                    (hi[:, k * 16:k * 16 + 16], lo[:, k * 16:k * 16 + 16])) for k in range(2)], tw, t_h[t // 4], *fr)
        chunk_done("gate", p)
        g3 = s.parts[0][:, 0:128].rearrange("p (t h) -> p t h", h=16)
        z = dve.op(lambda e: e.memset(pr[:, :, 16:24], -1.0), *l1_end)
        d = dve.op(lambda e: e.tensor_reduce(nm[:, 0, :], g3, AX_X, ALU.max), p)
        d = dve.op(lambda e: e.tensor_tensor(pr[:, :, 0:16], g3, nm[:, 0, :].unsqueeze(2).to_broadcast([128, NT, 16]),
                                             ALU.subtract), d)
        s.free = (d,)
        a = act.op(lambda e: e.activation(pr[:, :, 0:16], pr[:, :, 0:16], ACT.Exp), d)
        d = dve.op(lambda e: e.tensor_reduce(nm[:, 1, :], pr[:, :, 0:16], AX_X, ALU.add), a)
        d = dve.op(lambda e: e.reciprocal(nm[:, 2, :], nm[:, 1, :]), d)
        d = dve.op(lambda e: e.tensor_tensor(pr[:, :, 0:16], pr[:, :, 0:16], nm[:, 2, :].unsqueeze(2).to_broadcast([128, NT, 16]),
                                             ALU.mult), d)
        ds_ = [dve.op(lambda e, t=t: e.max(tp8[:, t, :], pr[:, t, 0:16]), d, z) for t in range(NT)]
        d = dve.op(lambda e: e.memset(tp8[:, :, 6:8], -1.0), ds_[-1])
        for t in range(NT):
            m = dve.op(lambda e, t=t: e.match_replace(rp[:, t, :], tp8[:, t, :], pr[:, t, :], -2.0), d)
        d = dve.op(lambda e: e.scalar_tensor_tensor(out=cl[:, :, 16:32], in0=rp[:, :, 0:16], scalar=0.0, in1=pr[:, :, 0:16],
                                                    op0=ALU.is_lt, op1=ALU.mult), m)
        d = dve.op(lambda e: e.tensor_copy(chr_[:, :, :], cl[:, :, 16:32]), d)
        d = dve.op(lambda e: e.tensor_copy(cl[:, :, 0:16], chr_[:, :, :].bitcast(F32)), d)
        d = dve.op(lambda e: e.tensor_tensor(cl[:, :, 16:32], cl[:, :, 16:32], chr_[:, :, :].bitcast(F32), ALU.subtract), d)
        for half in range(2):
            s, fr = ring8.take()
            for c in range(4):
                p = pe.op(lambda e, c=c, half=half, s=s: e.transpose(s.parts[0][0:32, c * 128:(c + 1) * 128],
                          cl[:, half * 4 + c, :], ident), d, *fr)
            t_ct = act.op(lambda e, half=half, s=s: e.copy(CTr[:, half * 512:half * 512 + 512], s.parts[0][0:32, :]), p)
            s.free = (t_ct,)
        ring_done(ring8, range(8))

        def combine(b, j, sl, *fr):
            return pe.op(lambda e: e.matmul(b[:, :], SELr[:, j * 128:(j + 1) * 128], CTr[:, sl], start=True, stop=True),
                         t_sel, t_ct, *fr)

        y = run_mlp([(f"moe{j}", True, None if j < 3 else j - 3) for j in range(25)], AT, t_h, None, None, combine=combine)
        n_out = 0
        ov = out.rearrange("(t p) d -> p t d", p=128)
        for t in range(NT):
            d = dve.op(lambda e, t=t: e.tensor_tensor(XO[:, t, :], XO[:, t, :], ybank(t), ALU.add), y[t], y[t | 1])
            n_out += 16
            o = sp.dma(ov[:, t, :], XO[:, t, :], s_out, n_out, d)
        sp.wait(o)
        m1.close()

        with nc.Block() as block:
            @block.sync
            def _(e):
                sp.play(e)

            @block.tensor
            def _(e):
                pe.play(e)

            @block.vector
            def _(e):
                dve.play(e)

            @block.scalar
            def _(e):
                act.play(e)

            @block.gpsimd
            def _(e):
                pool.play(e)


def sl2(sl):
    return slice(sl.start // 256, sl.stop // 256)


def last_of(engine):
    return (engine.sem, engine.count)


pe_last = act_last = dve_last = pool_last = last_of


def _layout(i):
    f = np.float32
    a = {k: np.asarray(v) for k, v in i.items()}

    def kmajor(m):
        return m.reshape(-1, 128, m.shape[-1]).transpose(1, 0, 2).reshape(128, -1)

    def pad(m, n, axis):
        w = [(0, 0)] * m.ndim
        w[axis] = (0, n - m.shape[axis])
        return np.pad(m, w)

    ch = {}
    qkv = np.concatenate([a["L0_attn_w_qkv"], a["L0_attn_gg_w1"]], 1)
    ch["qkv0"], ch["qkv1"] = qkv[0:128], qkv[128:256]
    ch["wo"] = kmajor(a["L0_attn_w_o"])
    for j in range(8):
        s = slice(j * 128, j * 128 + 128)
        ch[f"mem{j}"] = np.concatenate([kmajor(a["L0_attn_mem_w1"][:, s]), a["L0_attn_mem_w2"][s]], 1)
    w1, w3 = pad(a["L0_attn_ffn_w1"], 768, 1), pad(a["L0_attn_ffn_w3"], 768, 1)
    w2 = pad(a["L0_attn_ffn_w2"], 768, 0)
    for j in range(6):
        s = slice(j * 128, j * 128 + 128)
        ch[f"ffn{j}"] = np.concatenate([kmajor(w1[:, s]), kmajor(w3[:, s]), w2[s]], 1)
    up = a["L0_ffn_W_up"].T
    ch["up"] = np.concatenate([kmajor(up[:, 0:128]), kmajor(up[:, 128:256])], 1)
    ch["exp"] = kmajor(np.concatenate([a["L0_ffn_W_expert"], a["L0_ffn_W_gate"].T], 1))
    ch["down"] = kmajor(a["L0_ffn_W_down"].T)
    uq, uk, uv = (a[f"L1_attn_W_{n}_w"].reshape(16, 128, -1) for n in ("UQ", "UK", "UV"))
    buq, buk, buv = (a[f"L1_attn_W_{n}_b"].reshape(16, 128, 1) for n in ("UQ", "UK", "UV"))
    wo = a["L1_attn_W_O_w"].T.reshape(16, 128, 256)
    for h in range(16):
        ch[f"fuse{h}"] = np.concatenate([pad(np.concatenate([uq[h], buq[h]], 1), 256, 1), uk[h], buk[h], uv[h], buv[h], wo[h]], 1)
    dkv, dq = a["L1_attn_W_DKV_w"].T, a["L1_attn_W_DQ_w"].T
    ch["proj"] = kmajor(np.concatenate([dkv, dkv, pad(dq, 256, 1)], 1))
    ch["gate"] = kmajor(a["L1_ffn_gate_w"].T)
    e1, e2 = a["L1_ffn_w1"], a["L1_ffn_w2"]
    g = e1[:, 0:176].reshape(2816, 256).T
    u = e1[:, 176:352].reshape(2816, 256).T
    dn = e2.transpose(0, 2, 1).reshape(2816, 256)
    s1 = a["L1_ffn_shared_w1"].T
    sg, su, sd = pad(s1[:, 0:352], 384, 1), pad(s1[:, 352:704], 384, 1), pad(a["L1_ffn_shared_w2"].T, 384, 0)
    g, u, dn = np.concatenate([sg, g], 1), np.concatenate([su, u], 1), np.concatenate([sd, dn], 0)
    for j in range(25):
        s = slice(j * 128, j * 128 + 128)
        ch[f"moe{j}"] = np.concatenate([kmajor(g[:, s]), kmajor(u[:, s]), dn[s]], 1)
    w = np.concatenate([ch[n] for n, _, _ in CHUNKS], 1)

    sm = np.zeros((128, SM_N), f)

    def put(name, v):
        sm[:, SM_OFF[name][0]:SM_OFF[name][1]] = v

    p = np.arange(128)
    put("ident", np.eye(128, dtype=f))
    inv = (f(1.0) / np.power(f(10000.0), np.arange(0, 16, 2, dtype=f) / f(16))).astype(f)
    fr = (np.arange(256, dtype=f)[:, None] * inv[None, :]).astype(f).astype(np.float64)
    fr = np.concatenate([fr, fr], 1)
    cos, sin = np.cos(fr).astype(f), np.sin(fr).astype(f)
    sin[:, 0:8] = -sin[:, 0:8]
    put("cos", cos.reshape(2, 128, 16).transpose(1, 0, 2).reshape(128, 32))
    put("sin", sin.reshape(2, 128, 16).transpose(1, 0, 2).reshape(128, 32))
    put("qs", a["L0_attn_q_scale"][None, :])
    put("ks", a["L0_attn_k_scale"][None, :])
    pos = (p[:, None] + 128 * np.arange(2)[None, :]).astype(np.float64)
    put("dk", (0.5 * 0.9 ** -pos).astype(f))
    put("dq", (0.9 ** pos).astype(f))
    put("mh", (p[:, None] // 16 == np.arange(8)[None, :]).astype(f))
    put("nw", np.concatenate([a["L0_attn_norm1_w"].reshape(2, 128).T, a["L0_attn_norm2_w"].reshape(2, 128).T], 1))
    put("ggw2", a["L0_attn_gg_w2"].reshape(1, 64))
    cb = np.zeros((128, 3), f)
    cb[0:64, 0] = cb[64:128, 0] = a["L1_attn_W_DKV_b"]
    cb[:, 1] = a["L1_attn_W_DQ_b"][0:128]
    cb[0:64, 2] = a["L1_attn_W_DQ_b"][128:192]
    cb[64, 2] = 1.0
    put("cb", cb)
    put("bo", a["L1_attn_W_O_b"][None, :])
    rel = p[:, None] - p[None, :]
    m0 = np.where((rel >= 0) & (rel < 64), 0.0, NEG).astype(f)
    rel = p[:, None] + 64 - np.arange(192)[None, :]
    m1 = np.where((rel >= 0) & (rel < 64), 0.0, NEG).astype(f)
    put("mask0", np.tile(m0, (1, 4)))
    put("mask1", np.tile(m1, (1, 2)))
    sel = np.zeros((32, 22 * 128), f)
    hid = np.arange(22 * 128)
    sel[hid // 176, hid] = 1.0
    sel[16 + hid // 176, hid] = 1.0
    return {"x": a["L0_attn_x"].reshape(T, 256), "w": w, "sm": sm, "sel": sel}


def kernel(**inputs):
    import concourse.bacc as _bacc
    from concourse import mybir as _mybir
    from concourse.bass_utils import run_bass_kernel_spmd as _run

    nc = _bacc.Bacc("TRN2", target_bir_lowering=False, num_devices=1)
    arrays = {f"in_{k}": np.ascontiguousarray(v) for k, v in _layout(inputs).items()}
    args = [nc.dram_tensor(k, v.shape, _mybir.dt.from_np(v.dtype), kind="ExternalInput").ap() for k, v in arrays.items()]
    o = nc.dram_tensor("out_dram", (T, 256), F32, kind="ExternalOutput").ap()
    build(nc, *args, o)
    r = _run(nc, [arrays], core_ids=[0])
    return r.results[0]["out_dram"].reshape(4, 256, 256)
```

```python
from contextlib import ExitStack

import numpy as np

import concourse.bass as bass
from concourse import mybir

F32 = mybir.dt.float32
R32 = mybir.dt.float32r
BF16 = mybir.dt.bfloat16
I32 = mybir.dt.int32
ALU = mybir.AluOpType
ACT = mybir.ActivationFunctionType
AX_X = mybir.AxisListType.X

T = 1024
NT = T // 128
SLOT = 832
NRAW = 3
NPART = 4
NEG = -1.0e30

SM_OFF = {}
_at = 0
for _name, _n in (("ident", 128), ("cos", 32), ("sin", 32), ("qs", 16), ("ks", 16), ("dk", 2), ("dq", 2),
                  ("mh", 8), ("nw", 4), ("ggw2", 64), ("cb", 3), ("bo", 256), ("mask0", 512), ("mask1", 384)):
    SM_OFF[_name] = (_at, _at + _n)
    _at += _n
SM_N = _at

CHUNKS = [("qkv0", 832, True), ("qkv1", 832, True)]
CHUNKS += [(f"fuse{h}", 642, False) for h in range(16)]
CHUNKS += [("wo", 512, True)]
CHUNKS += [(f"mem{j}", 512, True) for j in range(8)]
CHUNKS += [(f"ffn{j}", 768, True) for j in range(6)]
CHUNKS += [("up", 512, True), ("exp", 528, True), ("down", 512, True)]
CHUNKS += [("proj", 768, True)]
CHUNKS += [("gate", 32, True)]
CHUNKS += [(f"moe{j}", 768, True) for j in range(25)]
CH_OFF = {}
_at = 0
for _name, _n, _ in CHUNKS:
    CH_OFF[_name] = _at
    _at += _n
W_N = _at


class Engine:

    def __init__(self, sem):
        self.sem, self.count, self.todo, self.seen = sem, 0, [], {}

    def wait(self, *tokens):
        for sem, value in tokens:
            if self.seen.get(id(sem), 0) < value:
                self.seen[id(sem)] = value
                self.todo.append(lambda e, s=sem, v=value: e.wait_ge(s, v))

    def op(self, f, *tokens, signal=True):
        self.wait(*tokens)
        if signal:
            self.count += 1
            self.todo.append(lambda e: f(e).then_inc(self.sem, 1))
            return (self.sem, self.count)
        self.todo.append(f)
        return None

    def dma(self, out, in_, sem, value, *tokens):
        self.wait(*tokens)
        self.todo.append(lambda e: e.dma_start(out, in_).then_inc(sem, 16))
        return (sem, value)

    def play(self, e):
        for f in self.todo:
            f(e)


class Slot:
    def __init__(self, *parts):
        self.parts, self.free = parts, ()


class Ring:

    def __init__(self, slots):
        self.slots, self.at = slots, 0

    def take(self):
        s = self.slots[self.at % len(self.slots)]
        self.at += 1
        assert s.free is not None
        free, s.free = s.free, None
        return s, free


def build(nc, x, w, sm, sel, out):
    outer = ExitStack()
    with outer:
        def sb(name, shape, dt=F32, ctx=outer):
            return ctx.enter_context(nc.sbuf_tensor(name, shape, dt))

        def semaphore(name):
            return outer.enter_context(nc.semaphore(name))

        banks = [outer.enter_context(nc.psum_tensor(f"ps{i}", [128, 512], F32)) for i in range(8)]
        bank_free = [()] * 8

        def bank_ring(ids):
            r = Ring([Slot(banks[i]) for i in ids])
            for s, i in zip(r.slots, ids):
                s.free = bank_free[i]
            return r

        def ring_done(r, ids):
            for s, i in zip(r.slots, ids):
                bank_free[i] = s.free

        pe = Engine(semaphore("s_pe"))
        dve = Engine(semaphore("s_dve"))
        act = Engine(semaphore("s_act"))
        pool = Engine(semaphore("s_pool"))
        sp = Engine(semaphore("s_sp"))

        XO = sb("XO", [128, NT, 256])
        X1 = sb("X1", [128, NT, 256])
        NB = sb("NB", [128, NT, 256])
        AO = sb("AO", [128, NT, 256])
        AT = (sb("ATh", [128, 2, T], R32), sb("ATl", [128, 2, T], R32))
        BT = (sb("BTh", [128, 2, T], R32), sb("BTl", [128, 2, T], R32))
        SM = sb("SM", [128, SM_OFF["mask0"][0]])
        sm_ = lambda n: SM[:, SM_OFF[n][0]:SM_OFF[n][1]]
        ident = sm_("ident")
        raws = [(sb(f"wr{i}", [128, SLOT]), semaphore(f"s_w{i}")) for i in range(NRAW)]
        parts = [(sb(f"wh{i}", [128, SLOT], R32), sb(f"wl{i}", [128, SLOT], R32)) for i in range(NPART)]
        NTW = (sb("NTh", [128, 8, 256], R32), sb("NTl", [128, 8, 256], R32))
        MTW = (sb("MTh", [128, 2, 1024], R32), sb("MTl", [128, 2, 1024], R32))
        RTW = (sb("RTh", [128, 2, 16], R32), sb("RTl", [128, 2, 16], R32))
        bout = sb("bout", [128, 256])
        negh = sb("negh", [128, 128])
        st = sb("st", [128, NT, 6])
        mv = sb("mv", [128, NT, 2])
        ve = sb("ve", [128, NT])
        rs = sb("rs", [128, NT])
        r2 = sb("r2", [128, NT])
        v2 = sb("v2", [128, NT])

        s_in = semaphore("s_in")
        s_sm = semaphore("s_sm")
        s_out = semaphore("s_out")

        xv = x.rearrange("(t p) d -> p t d", p=128)
        s_x2 = semaphore("s_x2")
        n_early = SM_OFF["mask0"][0]
        t_x = [sp.dma(XO[:, 0:4, :], xv[:, 0:4, :], s_in, 16)]
        t_sm = sp.dma(SM[:, 0:n_early], sm[:, 0:n_early], s_sm, 16)

        index = {n: i for i, (n, _, _) in enumerate(CHUNKS)}
        part_of = {}
        for i, (_, _, split) in enumerate(CHUNKS):
            if split:
                part_of[i] = len(part_of)
        loaded, raw_read, split_done, part_read = {}, {}, {}, {}
        nxt = {"load": 0, "split": 0}

        def pump():
            going = True
            while going:
                going = False
                i = nxt["load"]
                if i < len(CHUNKS) and (i < NRAW or i - NRAW in raw_read):
                    name, n, _ = CHUNKS[i]
                    buf, sem = raws[i % NRAW]
                    free = (raw_read[i - NRAW],) if i >= NRAW else ()
                    loaded[i] = sp.dma(buf[:, 0:n], w[:, CH_OFF[name]:CH_OFF[name] + n], sem, 16 * (i // NRAW + 1), *free)
                    nxt["load"] += 1
                    going = True
                i = nxt["split"]
                while i < len(CHUNKS) and not CHUNKS[i][2]:
                    i += 1
                nxt["split"] = i
                if i < len(CHUNKS) and i in loaded:
                    k = part_of[i]
                    if k < NPART or k - NPART in part_read:
                        n = CHUNKS[i][1]
                        raw, (hi, lo) = raws[i % NRAW][0], parts[k % NPART]
                        free = (part_read[k - NPART],) if k >= NPART else ()
                        t = pool.op(lambda e, raw=raw, hi=hi, n=n: e.tensor_scalar(
                            hi[:, 0:n], raw[:, 0:n], 1.0, 0.0, ALU.mult, ALU.add), loaded[i], *free)
                        t = pool.op(lambda e, raw=raw, hi=hi, lo=lo, n=n: e.tensor_tensor(
                            lo[:, 0:n], raw[:, 0:n], hi[:, 0:n].bitcast(F32), ALU.subtract), t)
                        split_done[i] = raw_read[i] = t
                        nxt["split"] += 1
                        going = True

        def chunk(name):
            i = index[name]
            if CHUNKS[i][2]:
                hi, lo = parts[part_of[i] % NPART]
                return hi, lo, split_done[i]
            return raws[i % NRAW][0], None, loaded[i]

        def chunk_done(name, token):
            i = index[name]
            if CHUNKS[i][2]:
                part_read[part_of[i]] = token
            else:
                raw_read[i] = token
            pump()

        t_negh = pool.op(lambda e: e.memset(negh[:, :], -0.5))
        pump()
        t_x.append(sp.dma(XO[:, 4:8, :], xv[:, 4:8, :], s_x2, 16))
        s_mk = semaphore("s_mk")
        masks = AO[:, :, :].rearrange("p t d -> p (t d)")[:, 0:896]
        t_mk = sp.dma(masks, sm[:, n_early:], s_mk, 16)

        def mm3(o, terms, *tokens, first=True, last=True, skip=False, signal=True):
            n = len(terms)
            pe.wait(*tokens)
            t = None
            for i, ((lh, ll), (rh, rl)) in enumerate(terms):
                for c, (a, b) in enumerate(((lh, rh), (lh, rl), (ll, rh))):
                    fin = i == n - 1 and c == 2
                    t = pe.op(lambda e, a=a, b=b, s=(first and i == 0 and c == 0), p=(last and fin):
                              e.matmul(o, a, b, start=s, stop=p, skip_group_check=skip), signal=fin and signal)
            return t

        def split_from(hi, lo, src, *tokens, scale=None):
            if scale is None:
                a = act.op(lambda e: e.copy(hi, src), *tokens)
                return dve.op(lambda e: e.tensor_tensor(lo, src, hi.bitcast(F32), ALU.subtract), a)
            a = act.op(lambda e: e.activation(hi, src, ACT.Copy, scale=scale), *tokens)
            return dve.op(lambda e: e.scalar_tensor_tensor(out=lo, in0=src, scalar=scale, in1=hi.bitcast(F32),
                                                           op0=ALU.mult, op1=ALU.subtract), a)

        def turn(src, dst, ring, half, ready, free=(), scale=None):
            done = []
            for k in range(2):
                s, fr = ring.take()
                b = s.parts[0]
                for c in range(4):
                    t = pe.op(lambda e, c=c, k=k, b=b: e.transpose(b[:, c * 128:(c + 1) * 128],
                              src[:, half * 4 + c, k * 128:(k + 1) * 128], ident), ready[c], t_sm, *fr,
                              signal=c == 3)
                sl = slice(half * 512, half * 512 + 512)
                t = split_from(dst[0][:, k, sl], dst[1][:, k, sl], b[:, :], t, *free,
                               scale=None if scale is None else scale[:, k:k + 1])
                s.free = (t,)
                done.append(t)
            return done[-1]

        def tilemean(src, half, ready):
            for c in range(4):
                t = half * 4 + c
                a = dve.op(lambda e, t=t: e.bn_stats(st[:, t, :], src[:, t, :]), ready[c], signal=True)
                a = dve.op(lambda e, t=t: e.bn_aggr(mv[:, t, :], st[:, t, :]), a)
            return a

        def rsqrt_small(o, i, *tokens):
            n = i.shape[-1]
            return pool.op(lambda e: e.tensor_tensor(o, i, negh[:, 0:n], ALU.pow), t_negh, *tokens)

        def rsqrt_newton(y, v, hx, tmp, *tokens):
            dve.op(lambda e: e.tensor_scalar(hx, v, -0.5, None, ALU.mult), *tokens)
            d = dve.op(lambda e: e.tensor_scalar(y.bitcast(I32), v.bitcast(I32), -0.5, 1597463007.0, ALU.mult, ALU.add))
            for _ in range(3):
                d = dve.op(lambda e: e.tensor_tensor(tmp, y, y, ALU.mult), d)
                d = dve.op(lambda e: e.tensor_tensor(tmp, tmp, hx, ALU.mult), d)
                d = dve.op(lambda e: e.scalar_tensor_tensor(out=y, in0=tmp, scalar=1.5, in1=y, op0=ALU.add,
                                                            op1=ALU.mult), d)
            return d

        def layernorm(src, dst, half, ready, free=()):
            a = tilemean(src, half, ready)
            hs = slice(half * 4, half * 4 + 4)
            a = dve.op(lambda e: e.tensor_scalar(ve[:, hs], mv[:, hs, 1], 1e-5, None, ALU.add), a)
            p = rsqrt_small(rs[:, hs], ve[:, hs], a)
            out_ = []
            for c in range(4):
                t = half * 4 + c
                out_.append(dve.op(lambda e, t=t: e.tensor_scalar(dst[:, t, :], src[:, t, :], mv[:, t, 0:1],
                                   rs[:, t:t + 1], ALU.subtract, ALU.mult), p, *free))
            return out_

        l0 = ExitStack()
        VK = sb("VK", [128, NT, 16 * 33], ctx=l0)
        QKT = sb("QKT", [128, 4, T], ctx=l0)
        KB = [sb("KB0", [128, 8, 256], ctx=l0)]
        identb = sb("identb", [128, 128], BF16, ctx=l0)
        mb0 = sb("mb0", [128, 512], BF16, ctx=l0)
        mb1 = sb("mb1", [128, 384], BF16, ctx=l0)
        mx = sb("mx", [128, 6, 4], ctx=l0)
        rc = sb("rc", [128, 4, 8], ctx=l0)
        rg = sb("rg", [128, 4, 8], ctx=l0)
        lq = ExitStack()
        QKf = [sb(f"QKf{i}", [128, 512], ctx=lq) for i in range(4)]
        QSf = [sb(f"QSf{i}", [128, 512], ctx=lq) for i in range(4)]
        QRf = [sb(f"QRf{i}", [128, 512], ctx=lq) for i in range(2)]
        sso = sb("sso", [128, NT * 32], ctx=lq)
        rq = sb("rq", [128, NT * 32], ctx=lq)
        hx = sb("hx", [128, 64], ctx=lq)
        ntmp = sb("ntmp", [128, 64], ctx=lq)
        CT = sb("CT", [128, 2, 2, 16], ctx=lq)
        ST = sb("ST", [128, 2, 2, 16], ctx=lq)
        gth = sb("gth", [128, 2, 64], ctx=lq)
        gsl = sb("gsl", [128, 2, 64], ctx=lq)
        gj = sb("gj", [128, 64], ctx=lq)
        gz = sb("gz", [128, NT], ctx=lq)
        gt = sb("gt", [128, NT], ctx=lq)
        gq = sb("gq", [128, NT], ctx=lq)

        cosv = sm_("cos").rearrange("p (t d) -> p t d", t=2)
        sinv = sm_("sin").rearrange("p (t d) -> p t d", t=2)
        for s_, f_, nm in ((0, 0.25, "qs"), (1, 1.0, "ks")):
            sc = sm_(nm)
            full = sc.unsqueeze(1).to_broadcast([128, 2, 16])
            lowb = sc[:, 0:8].unsqueeze(1).to_broadcast([128, 2, 8])
            highb = sc[:, 8:16].unsqueeze(1).to_broadcast([128, 2, 8])
            dve.op(lambda e, s_=s_, f_=f_, full=full: e.scalar_tensor_tensor(
                out=CT[:, :, s_, :], in0=cosv, scalar=f_, in1=full, op0=ALU.mult, op1=ALU.mult), t_sm)
            dve.op(lambda e, s_=s_, f_=f_, highb=highb: e.scalar_tensor_tensor(
                out=ST[:, :, s_, 0:8], in0=sinv[:, :, 0:8], scalar=f_, in1=highb, op0=ALU.mult, op1=ALU.mult))
            t_tab = dve.op(lambda e, s_=s_, f_=f_, lowb=lowb: e.scalar_tensor_tensor(
                out=ST[:, :, s_, 8:16], in0=sinv[:, :, 8:16], scalar=f_, in1=lowb, op0=ALU.mult, op1=ALU.mult))
        vk4 = VK[:, :, :].rearrange("p t (h e) -> p t h e", h=16)
        t_ones = pool.op(lambda e: e.memset(vk4[:, :, :, 32:33], 1.0))

        f_m0, f_m1, f_n, f_b = bank_ring((0,)), bank_ring((1,)), bank_ring((2,)), bank_ring((3,))
        sbias, fb = f_b.take()

        def fuse(h):
            raw, _, tw = chunk(f"fuse{h}")
            uq, uk, uv, wo_ = raw[:, 0:256], raw[:, 256:321], raw[:, 321:385], raw[:, 386:642]
            buv = raw[:, 385:386]
            if h % 4 == 0:
                fuse.m = [f_m0.take(), f_m1.take()]
            if h % 4 == 0:
                fuse.tok = []
            for k in range(2):
                s, fr = fuse.m[k]
                p = pe.op(lambda e, s=s, k=k, h=h: e.matmul(s.parts[0][:, (h % 4) * 65:(h % 4) * 65 + 65],
                          uq[:, k * 128:(k + 1) * 128], uk, start=True, stop=True), tw, *fr)
            if h % 2 == 0:
                fuse.n = f_n.take()
            s, fr = fuse.n
            lo_ = 64 * (h % 2)
            pn = pe.op(lambda e, s=s, lo_=lo_: e.matmul(s.parts[0][lo_:lo_ + 64, 0:256], uv, wo_, start=True, stop=True), *fr)
            pb = pe.op(lambda e, h=h: e.matmul(sbias.parts[0][:, 0:256], buv.to_broadcast([128, 128]), wo_, start=h == 0,
                                               stop=h == 15), *fb)
            chunk_done(f"fuse{h}", pb)
            if h % 2 == 1:
                j = h // 2
                t = split_from(NTW[0][:, j, :], NTW[1][:, j, :], s.parts[0][:, 0:256], pn)
                s.free = (t,)
            if h % 4 == 3:
                j = h // 4
                for k in range(2):
                    s, fr = fuse.m[k]
                    v = s.parts[0][:, 0:260].rearrange("p (h c) -> p h c", c=65)
                    mh_, ml_ = (m[:, k, j * 256:j * 256 + 256].rearrange("p (h c) -> p h c", c=64) for m in MTW)
                    t = split_from(mh_, ml_, v[:, :, 0:64], p)
                    t = split_from(RTW[0][:, k, 4 * j:4 * j + 4], RTW[1][:, k, 4 * j:4 * j + 4], v[:, :, 64], t)
                    s.free = (t,)
                fuse.done = t
            if h == 15:
                fuse.bias = dve.op(lambda e: e.tensor_tensor(bout[:, :], sbias.parts[0][:, 0:256], sm_("bo"), ALU.add), pb)
                sbias.free = (fuse.bias,)
                for r, ids in ((f_m0, (0,)), (f_m1, (1,)), (f_n, (2,)), (f_b, (3,))):
                    ring_done(r, ids)

        ring4 = bank_ring((4, 5, 6, 7))
        t_h = [None, None]
        xn, rd0 = {}, {}

        def first_norm(half):
            hs = slice(half * 4, half * 4 + 4)
            xn[half] = layernorm(XO, X1, half, [t_x[half]] * 4)
            a = dve.op(lambda e, hs=hs: e.tensor_tensor(v2[:, hs], rs[:, hs], rs[:, hs], ALU.mult))
            a = dve.op(lambda e, hs=hs: e.tensor_tensor(v2[:, hs], v2[:, hs], mv[:, hs, 1], ALU.mult), a)
            a = dve.op(lambda e, hs=hs: e.tensor_scalar(v2[:, hs], v2[:, hs], 1e-6, None, ALU.add), a)
            p = rsqrt_small(r2[:, hs], v2[:, hs], a)
            rd0[half] = [dve.op(lambda e, t=t: e.tensor_scalar(NB[:, t, :], X1[:, t, :], r2[:, t:t + 1], None, ALU.mult), p,
                                xn[half][t % 4]) for t in range(half * 4, half * 4 + 4)]

        def first_turn(half):
            t_h[half] = turn(NB, AT, ring4, half, rd0[half], scale=sm_("nw")[:, 0:2])

        qkf = Ring([Slot(b) for b in QKf])
        qsf = Ring([Slot(b) for b in QSf])
        qrf = Ring([Slot(b) for b in QRf])
        w0h, w0l, t_w0 = chunk("qkv0")
        w1h, w1l, t_w1 = chunk("qkv1")
        t_vk, t_qkt, t_rope = [None] * NT, [None] * NT, [None] * NT
        t_gz, t_v, held, t_sq = [None] * NT, [None] * NT, {}, [None] * NT

        def project(t):
            tt = t % 2
            ts_ = slice(t * 128, (t + 1) * 128)
            sa, fa = ring4.take()
            ba = sa.parts[0]
            xs = [(AT[0][:, k, ts_], AT[1][:, k, ts_]) for k in range(2)]
            pa = mm3(ba[:, :], [(xs[0], (w0h[:, 0:512], w0l[:, 0:512])), (xs[1], (w1h[:, 0:512], w1l[:, 0:512]))],
                     t_h[t // 4], t_w0, t_w1, *fa)
            sv, fv = ring4.take()
            bv = sv.parts[0]
            project.last = mm3(bv[:, 0:320], [(xs[0], (w0h[:, 512:832], w0l[:, 512:832])),
                                              (xs[1], (w1h[:, 512:832], w1l[:, 512:832]))], *fv)
            s1, f1 = qkf.take()
            s2, f2 = qsf.take()
            QK, QS = s1.parts[0], s2.parts[0]
            a1 = act.op(lambda e: e.activation(QS[:, :], ba[:, :], ACT.Square), pa, *f2)
            a2 = act.op(lambda e: e.copy(QK[:, :], ba[:, :]), *f1)
            sa.free = (a2,)
            t_v[t] = act.op(lambda e: e.copy(vk4[:, t, :, 0:16], bv[:, 0:256].rearrange("p (h d) -> p h d", h=16)),
                            project.last)
            a4 = act.op(lambda e: e.activation(gth[:, tt, :], bv[:, 256:320], ACT.Tanh, scale=0.5),
                        *([t_gz[t - 2]] if t >= 2 else []))
            t_sq[t] = dve.op(lambda e: e.tensor_reduce(sso[:, t * 32:t * 32 + 32], QS[:, :].rearrange("p (h d) -> p h d", d=16),
                                                       AX_X, ALU.add), a1)
            d = dve.op(lambda e: e.scalar_tensor_tensor(out=gsl[:, tt, :], in0=gth[:, tt, :], scalar=1.0,
                       in1=bv[:, 256:320], op0=ALU.add, op1=ALU.mult), a4)
            sv.free = (d,)
            t_gz[t] = dve.op(lambda e: e.tensor_tensor_reduce(gj[:, :], gsl[:, tt, :], sm_("ggw2"), 0.5, 0.0,
                             ALU.mult, ALU.add, gz[:, t:t + 1]), d, *([t_gz[t - 1]] if t else []))
            held[t] = (s1, s2, a2)

        def head_norms(b):
            cs = slice(b * 64, b * 64 + 64)
            d = dve.op(lambda e: e.tensor_scalar(sso[:, cs], sso[:, cs], 1.0 / 16, 1e-6, ALU.mult, ALU.add), t_sq[2 * b + 1])
            t_rope[2 * b] = t_rope[2 * b + 1] = rsqrt_newton(rq[:, cs], sso[:, cs], hx[:, :], ntmp[:, :], d)
            ag = act.op(lambda e: e.activation(gt[:, 2 * b:2 * b + 2], gz[:, 2 * b:2 * b + 2], ACT.Tanh, scale=0.5),
                        t_gz[2 * b + 1])
            held[("g", b)] = dve.op(lambda e: e.scalar_tensor_tensor(out=gq[:, 2 * b:2 * b + 2], in0=gt[:, 2 * b:2 * b + 2],
                                    scalar=1.0, in1=sm_("dk"), op0=ALU.add, op1=ALU.mult), ag)

        def rotate(t):
            tt = t % 2
            s1, s2, a2 = held[t]
            s3, f3 = qrf.take()
            QK, QS, QR = s1.parts[0], s2.parts[0], s3.parts[0]
            d = dve.op(lambda e: e.tensor_tensor(
                QK[:, :].rearrange("p (h d) -> p h d", d=16), QK[:, :].rearrange("p (h d) -> p h d", d=16),
                rq[:, t * 32:t * 32 + 32].unsqueeze(2).to_broadcast([128, 32, 16]), ALU.mult), a2, t_rope[t])
            q4 = QK[:, :].rearrange("p (s h d) -> p s h d", s=2, d=16)
            o4 = QS[:, :].rearrange("p (s h d) -> p s h d", s=2, d=16)
            r4 = QR[:, :].rearrange("p (s h d) -> p s h d", s=2, d=16)
            for lo_ in (0, 8):
                for s_ in range(2):
                    pq = pool.op(lambda e, lo_=lo_, s_=s_: e.tensor_tensor(
                        o4[:, s_, :, lo_:lo_ + 8], q4[:, s_, :, 8 - lo_:16 - lo_],
                        ST[:, tt, s_, lo_:lo_ + 8].unsqueeze(1).to_broadcast([128, 16, 8]), ALU.mult), d, t_tab)
            for s_ in range(2):
                dc = dve.op(lambda e, s_=s_: e.tensor_tensor(
                    r4[:, s_], q4[:, s_], CT[:, tt, s_, :].unsqueeze(1).to_broadcast([128, 16, 16]), ALU.mult), d, *f3)
            held[t] = (s1, s2, s3, dc, pq)

        def rotated(t):
            tt = t % 2
            s1, s2, s3, dc, pq = held[t]
            QS, QR = s2.parts[0], s3.parts[0]
            dr = dve.op(lambda e: e.tensor_tensor(QR[:, :], QR[:, :], QS[:, :], ALU.add), dc, pq)
            s1.free = (dc, pq)
            s2.free = (dr,)
            t_vk[t] = dve.op(lambda e: e.tensor_scalar(
                vk4[:, t, :, 16:32], QR[:, 256:512].rearrange("p (h d) -> p h d", d=16),
                gq[:, t:t + 1], None, ALU.mult), dr, held[("g", t // 2)])
            bs, fr = ring4.take()
            b = bs.parts[0]
            for c in range(4):
                p = pe.op(lambda e, c=c: e.transpose(b[:, c * 128:(c + 1) * 128], QR[:, c * 128:(c + 1) * 128], ident),
                          dr, *fr, signal=c == 3)
            t_qkt[t] = act.op(lambda e: e.copy(QKT[:, :, t * 128:(t + 1) * 128],
                                               b[:, :].rearrange("p (c n) -> p c n", c=4)), p)
            bs.free = (t_qkt[t],)
            s3.free = (p, t_vk[t])

        first_norm(0)
        fuse(0)
        fuse(1)
        first_turn(0)
        first_norm(1)
        nf = 2
        for b in range(5):
            if b < 4:
                for t in (2 * b, 2 * b + 1):
                    project(t)
                    for _ in range(2):
                        if nf < 16:
                            fuse(nf)
                            nf += 1
                    if t == 1:
                        first_turn(1)
                if b == 3:
                    chunk_done("qkv0", project.last)
                    chunk_done("qkv1", project.last)
                head_norms(b)
            if b >= 1:
                rotated(2 * b - 2)
                rotated(2 * b - 1)
            if b < 4:
                rotate(2 * b)
                rotate(2 * b + 1)
        ring_done(ring4, (4, 5, 6, 7))
        lq_end = (last_of(pe), last_of(act), last_of(dve), last_of(pool))
        lq.close()
        KB.append(sb("KB1", [128, 8, 256], ctx=l0))
        P0 = [sb(f"P0{i}", [128, 4, 128], ctx=l0) for i in range(2)]
        P1 = [sb(f"P1{i}", [128, 2, 256], ctx=l0) for i in range(3)]
        SS = [sb(f"SS{i}", [128, 512], ctx=l0) for i in range(2)]
        PT = [sb(f"PT{i}", [128, 512], ctx=l0) for i in range(3)]
        t_cb = act.op(lambda e: e.copy(identb[:, :], ident), t_sm)
        t_cb = act.op(lambda e: e.copy(mb0[:, :], masks[:, 0:512]), t_mk)
        t_cb = act.op(lambda e: e.copy(mb1[:, :], masks[:, 512:896]))
        for b in P1:
            t_p1z = pool.op(lambda e, b=b: e.memset(b[:, :, 0:64], 0.0), *lq_end)
        rS, rT, rO, rM = bank_ring((0, 1, 2)), bank_ring((3, 4)), bank_ring((5, 6)), bank_ring((7,))
        pr0 = Ring([Slot(b) for b in P0])
        pr1 = Ring([Slot(b) for b in P1])
        ssr = Ring([Slot(b) for b in SS])
        ptr = Ring([Slot(b) for b in PT])
        for r in (pr0, pr1, ssr, ptr):
            for s in r.slots:
                s.free = lq_end
        mxr = Ring([Slot(mx[:, i, :]) for i in range(6)])
        rcr = Ring([Slot(rc[:, i, :], rg[:, i, :]) for i in range(4)])
        kbr = Ring([Slot(b) for b in KB])
        kbr.slots[1].free = lq_end
        units = []
        for b in range(4):
            for g in range(2):
                for c in range(2):
                    units.append((b, g, 0, 4 * c, 4))
                for c in range(4):
                    units.append((b, g, 1, 2 * c, 2))
        kb_now = {}

        def make_kb(b, g):
            s, fr = kbr.take()
            for h in range(8):
                eng = dve if h % 2 else pool
                tk = eng.op(lambda e, h=h, s=s: e.tensor_scalar(
                    s.parts[0][:, h, :], QKT[:, 2 + g, b * 256:(b + 1) * 256], sm_("mh")[:, h:h + 1], 0.0,
                    ALU.mult, ALU.add), t_qkt[2 * b], t_qkt[2 * b + 1], *fr)
                if h == 6:
                    tp = tk
            kb_now[(b, g)] = (s, (tp, tk))

        def scores(u):
            b, g, qt, h0, nh = u
            kb, tk = kb_now[(b, g)]
            s, fr = rS.take()
            bk = s.parts[0]
            n = 512 if qt == 0 else 384
            cols = slice(0, 128) if qt == 0 else slice(64, 256)
            pe.op(lambda e: e.matmul(bk[:, 0:n], QKT[:, g, b * 256 + qt * 128:b * 256 + qt * 128 + 128],
                                     kb.parts[0][:, h0:h0 + nh, cols], start=True, stop=False), *tk, *fr, signal=False)
            p = pe.op(lambda e: e.matmul(bk[:, 0:n], identb[:, :], (mb0 if qt == 0 else mb1)[:, :], start=False,
                                         stop=True), t_cb)
            if h0 + nh == 8 and qt == 1:
                kb.free = (p,)
            sm1, fm = mxr.take()
            m = sm1.parts[0]
            v = bk[:, 0:n].rearrange("p (h k) -> p h k", h=nh)
            d1 = dve.op(lambda e: e.tensor_reduce(m[:, 0:nh], v, AX_X, ALU.max), p, *fm)
            s2, f2 = ssr.take()
            d2 = dve.op(lambda e: e.tensor_tensor(s2.parts[0][:, 0:n].rearrange("p (h k) -> p h k", h=nh), v,
                                                  m[:, 0:nh].unsqueeze(2).to_broadcast([128, nh, n // nh]),
                                                  ALU.subtract), d1, *f2)
            s.free = (d2,)
            sm1.free = (d2,)
            s3, f3 = (pr0 if qt == 0 else pr1).take()
            dst = s3.parts[0][:, :, :] if qt == 0 else s3.parts[0][:, :, 64:256]
            a = act.op(lambda e: e.activation(dst, s2.parts[0][:, 0:n].rearrange("p (h k) -> p h k", h=nh), ACT.Exp),
                       d2, *f3)
            s2.free = (a,)
            return s3, a

        def turns(u, s3, a):
            b, g, qt, h0, nh = u
            s, fr = rT.take()
            bk = s.parts[0]
            pf = s3.parts[0][:, :, :].rearrange("p h k -> p (h k)")
            for c in range(4):
                p = pe.op(lambda e, c=c: e.transpose(bk[:, c * 128:(c + 1) * 128], pf[:, c * 128:(c + 1) * 128], ident),
                          a, t_p1z, *fr, signal=c == 3)
            s3.free = (p,)
            s4, f4 = ptr.take()
            a = act.op(lambda e: e.copy(s4.parts[0][:, :], bk[:, :]), p, *f4)
            s.free = (a,)
            return s4, a

        obank = {}

        def weigh(u, s4, a):
            b, g, qt, h0, nh = u
            t = 2 * b + qt
            if h0 == 0:
                obank[(b, g, qt)] = rO.take()
            so, fo = obank[(b, g, qt)]
            bk = so.parts[0]
            for i in range(nh):
                h = h0 + i
                o = bk[:, h * 33:(h + 1) * 33]
                H = 8 * g + h
                if qt == 0:
                    p = pe.op(lambda e, o=o, i=i, H=H: e.matmul(o, s4.parts[0][:, i * 128:(i + 1) * 128], vk4[:, t, H, :],
                              start=True, stop=True), a, t_v[t], t_ones, t_vk[t], *fo, signal=i == nh - 1)
                else:
                    for k in range(2):
                        p = pe.op(lambda e, o=o, i=i, k=k, H=H: e.matmul(
                            o, s4.parts[0][:, (2 * i + k) * 128:(2 * i + k + 1) * 128], vk4[:, t - 1 + k, H, :],
                            start=k == 0, stop=k == 1), a, t_v[t], t_ones, t_vk[t], *fo,
                            signal=i == nh - 1 and k == 1)
            s4.free = (p,)
            if h0 + nh < 8:
                return
            o3 = bk[:, 0:264].rearrange("p (h e) -> p h e", h=8)
            sr, fr = rcr.take()
            c1, c2 = sr.parts
            d = dve.op(lambda e: e.reciprocal(c1, o3[:, :, 32]), p, *fr)
            d1 = dve.op(lambda e: e.tensor_scalar(c2, c1, sm_("dq")[:, qt:qt + 1], None, ALU.mult), d)
            hd = slice(g * 128, g * 128 + 128)
            d2 = dve.op(lambda e: e.tensor_tensor(AO[:, t, hd].rearrange("p (h d) -> p h d", d=16), o3[:, :, 0:16],
                                                  c1.unsqueeze(2).to_broadcast([128, 8, 16]), ALU.mult))
            d3 = dve.op(lambda e: e.tensor_tensor(NB[:, t, hd].rearrange("p (h d) -> p h d", d=16), o3[:, :, 16:32],
                                                  c2.unsqueeze(2).to_broadcast([128, 8, 16]), ALU.mult), d1, t_h[1])
            so.free = (d3,)
            sr.free = (d3,)
            t_ao[t] = d3

        t_ao = [None] * NT
        t_qm, t_at, t_ow = [None, None], [None, None], [None] * NT

        def o_project(t, ring):
            hi, lo, tw = chunk("wo")
            s, fr = ring.take()
            b = s.parts[0]
            ts_ = slice(t * 128, (t + 1) * 128)
            p = mm3(b[:, 0:256], [((BT[0][:, k, ts_], BT[1][:, k, ts_]), (hi[:, k * 256:k * 256 + 256], lo[:, k * 256:k * 256 + 256]))
                                  for k in range(2)], tw, t_at[t // 4], *fr)
            t_ow[t] = act.op(lambda e: e.copy(AO[:, t, :], b[:, 0:256]), p)
            s.free = (t_ow[t],)
            if t == NT - 1:
                chunk_done("wo", p)

        def turn_qm(half, ring):
            t_qm[half] = turn(NB, AT, ring, half, t_ao[half * 4:half * 4 + 4])

        def turn_at(half, ring):
            t_at[half] = turn(AO, BT, ring, half, t_ao[half * 4:half * 4 + 4])

        fill = {29: lambda: turn_qm(0, rM), 31: lambda: turn_at(0, rM)}
        for t in range(4):
            fill[33 + 2 * t] = lambda t=t: o_project(t, rM)
        make_kb(0, 0)
        s_out_, t_out_ = {}, {}
        n = len(units)
        for i in range(n + 3):
            if 0 <= i - 2 < n:
                t_out_[i - 2] = turns(units[i - 2], *s_out_[i - 2])
            if i < n:
                if i % 6 == 3 and i // 6 + 1 < 8:
                    j = i // 6 + 1
                    make_kb(j // 2, j % 2)
                s_out_[i] = scores(units[i])
            if 0 <= i - 3 < n:
                weigh(units[i - 3], *t_out_[i - 3])
            if i in fill:
                fill[i]()
        ring_done(rS, (0, 1, 2))
        ring_done(rT, (3, 4))
        ring_done(rO, (5, 6))
        ring_done(rM, (7,))
        l0_end = (last_of(pe), last_of(act), last_of(dve), last_of(pool))
        l0.close()

        mlp = ExitStack()
        T1 = [sb(f"T1{i}", [128, 512], ctx=mlp) for i in range(2)]
        T2 = [sb(f"T2{i}", [128, 512], ctx=mlp) for i in range(2)]
        HH = [(sb(f"HHh{i}", [128, 512], R32, ctx=mlp), sb(f"HHl{i}", [128, 512], R32, ctx=mlp)) for i in range(3)]
        t1r = Ring([Slot(b) for b in T1])
        t2r = Ring([Slot(b) for b in T2])
        hr = Ring([Slot(*b) for b in HH])
        for r in (t1r, t2r, hr):
            for s in r.slots:
                s.free = l0_end

        def run_mlp(names, gated, ring, xin, ready, before=(), after=lambda half: (), combine=None, lag=2, at={}):
            n = len(names)
            yfree = [bank_free[i] for i in range(4)]
            pend, pieces, tail = [], list(before), {}
            ytok = [None] * NT

            def down(j, half, hslot, th):
                hi, lo, _ = chunk(names[j])
                o = 512 if gated else 256
                for c in range(4):
                    t = half * 4 + c
                    tk = mm3(ybank(t), [((hslot.parts[0][:, c * 128:(c + 1) * 128], hslot.parts[1][:, c * 128:(c + 1) * 128]),
                                         (hi[:, o:o + 256], lo[:, o:o + 256]))], th, *(yfree[t // 2] if j == 0 else ()),
                             first=(j == 0 and t % 2 == 0), last=j == n - 1, skip=True, signal=c == 3 or j == n - 1)
                    ytok[t] = tk
                hslot.free = (tk,)
                if half == 1:
                    chunk_done(names[j], tk)
                if j == n - 1:
                    tail[half] = list(after(half, ytok))
                    if half == 0:
                        while len(tail[0]) > 1:
                            tail[0].pop(0)()

            def step(j, half):
                hi, lo, tw = chunk(names[j])
                sl = slice(half * 512, half * 512 + 512)
                xs = [(xin[0][:, k, sl], xin[1][:, k, sl]) for k in range(2)]
                got = []
                cc = combine is not None and j >= 3
                if cc:
                    sc, fc = ring.take()
                    pc = combine(sc.parts[0], j - 3, sl, *fc)
                for part in range(2 if gated else 1):
                    sg, fg = ring.take()
                    o = part * 256
                    pg = mm3(sg.parts[0][:, :], [((hi[:, o + k * 128:o + k * 128 + 128], lo[:, o + k * 128:o + k * 128 + 128]),
                                                  xs[k]) for k in range(2)], tw, ready[half], *fg)
                    got.append((sg, pg))
                s1, f1 = t1r.take()
                s2, f2 = t2r.take()
                A, B = s1.parts[0], s2.parts[0]
                sg, pg = got[0]
                g = sg.parts[0]
                a = act.op(lambda e: e.activation(A[:, :], g[:, :], ACT.Silu), pg, *f1)
                sg.free = (a,)
                if gated:
                    su, pu = got[1]
                    u = su.parts[0]
                    d = dve.op(lambda e: e.tensor_tensor(B[:, :], A[:, :], u[:, :], ALU.mult), a, pu, *f2)
                    su.free = (d,)
                    s1.free = (d,)
                    if cc:
                        d = dve.op(lambda e, c=sc.parts[0]: e.tensor_tensor(B[:, :], B[:, :], c[:, :], ALU.mult), d, pc)
                        sc.free = (d,)
                else:
                    d = dve.op(lambda e: e.scalar_tensor_tensor(out=B[:, :], in0=A[:, :], scalar=1.0, in1=A[:, :],
                                                                op0=ALU.add, op1=ALU.mult), a, *f2)
                    s1.free = (d,)
                s3, f3 = hr.take()
                th = split_from(s3.parts[0][:, :], s3.parts[1][:, :], B[:, :], d, *f3)
                s2.free = (th,)
                pend.append((j, half, s3, th))

            order = []
            for j in range(n + lag):
                if j < n:
                    order.append((j, 0))
                if j >= lag:
                    order.append((j - lag, 1))
            for i, (j, half) in enumerate(order):
                if (j, half) == (0, 1):
                    while pieces:
                        pieces.pop(0)()
                step(j, half)
                if len(pend) > 1:
                    down(*pend.pop(0))
                if (j, half) in at:
                    at[(j, half)]()
                for _ in range(2):
                    if pieces:
                        pieces.pop(0)()
            while pend:
                down(*pend.pop(0))
            for f in tail[0]:
                f()
            return tail[1]

        def ybank(t):
            return banks[t // 2][:, (t % 2) * 256:(t % 2) * 256 + 256]

        ring4 = bank_ring((4, 5, 6, 7))
        turn_qm(1, ring4)

        def second_half():
            turn_at(1, ring4)
            for t in range(4, 8):
                o_project(t, ring4)

        t_x1, t_xo, t_x, t_x2 = [None] * NT, [None] * NT, [None] * NT, [None] * NT
        t_hf, t_hm = [None, None], [None, None]

        def after_mem(half, y):
            def one(t):
                s1, f1 = t1r.take()
                A = s1.parts[0]
                a = act.op(lambda e: e.activation(A[:, 0:256], ybank(t), ACT.Tanh, scale=0.5), y[t | 1], *f1)
                bank_free[t // 2] = (a,)
                d = dve.op(lambda e: e.scalar_tensor_tensor(out=A[:, 0:256], in0=A[:, 0:256], scalar=1.0,
                           in1=AO[:, t, :], op0=ALU.add, op1=ALU.mult), a, t_ow[t])
                d = dve.op(lambda e: e.scalar_tensor_tensor(out=X1[:, t, :], in0=A[:, 0:256], scalar=0.5,
                           in1=X1[:, t, :], op0=ALU.mult, op1=ALU.add), d)
                s1.free = (d,)
                t_x1[t] = d

            def pair(c):
                one(half * 4 + c)
                one(half * 4 + c + 1)

            def norm():
                hs = slice(half * 4, half * 4 + 4)
                a = tilemean(X1, half, t_x1[half * 4:half * 4 + 4])
                a = dve.op(lambda e: e.tensor_tensor(v2[:, hs], mv[:, hs, 0], mv[:, hs, 0], ALU.mult), a)
                a = dve.op(lambda e: e.scalar_tensor_tensor(out=v2[:, hs], in0=v2[:, hs], scalar=1e-6,
                           in1=mv[:, hs, 1], op0=ALU.add, op1=ALU.add), a)
                p = rsqrt_small(r2[:, hs], v2[:, hs], a)
                norm.rd = [dve.op(lambda e, t=t: e.tensor_scalar(NB[:, t, :], X1[:, t, :], r2[:, t:t + 1], None, ALU.mult),
                                  p, t_qm[1]) for t in range(half * 4, half * 4 + 4)]

            def turned():
                for t in range(half * 4, half * 4 + 4):
                    t_xo[t] = pool.op(lambda e, t=t: e.tensor_tensor(XO[:, t, :], XO[:, t, :], X1[:, t, :], ALU.add),
                                      t_x1[t])
                t_hf[half] = turn(NB, BT, ring4, half, norm.rd, scale=sm_("nw")[:, 2:4])

            return [lambda: pair(0), lambda: pair(2), norm, turned]

        rest = run_mlp([f"mem{j}" for j in range(8)], False, ring4, AT, t_qm, before=[second_half], after=after_mem)

        t_hn = [None, None]

        def after_ffn(half, y):
            def add():
                for t in range(half * 4, half * 4 + 4):
                    t_x[t] = dve.op(lambda e, t=t: e.tensor_tensor(XO[:, t, :], XO[:, t, :], ybank(t), ALU.add),
                                    y[t | 1], t_xo[t])
                    bank_free[t // 2] = (t_x[t],)

            def norm():
                norm.rd = layernorm(XO, NB, half, t_x[half * 4:half * 4 + 4], free=(t_hf[half],))

            def turned():
                t_hn[half] = turn(NB, AT, ring4, half, norm.rd)

            return [add, norm, turned]

        rest = run_mlp([f"ffn{j}" for j in range(6)], True, ring4, BT, t_hf, before=rest, after=after_ffn)

        t_r = [None, None]
        top = sb("top", [128, NT, 8], ctx=mlp)
        e2 = sb("e2", [128, 4, NT], ctx=mlp)
        lg = [None] * NT
        t_rw = [None, None]
        t_hl = [None, None]

        def up(half):
            hi, lo, tw = chunk("up")
            sl = slice(half * 512, half * 512 + 512)
            for m in range(2):
                s, fr = ring4.take()
                b = s.parts[0]
                p = mm3(b[:, :], [((hi[:, m * 256 + k * 128:m * 256 + k * 128 + 128], lo[:, m * 256 + k * 128:m * 256 + k * 128 + 128]),
                                   (AT[0][:, k, sl], AT[1][:, k, sl])) for k in range(2)], tw, t_hn[half], *fr)
                a = act.op(lambda e, b=b, m=m: e.activation(BT[0][:, m, sl], b[:, :], ACT.Relu), p)
                d = dve.op(lambda e, b=b, m=m: e.scalar_tensor_tensor(
                    out=BT[1][:, m, sl], in0=b[:, :], scalar=0.0, in1=BT[0][:, m, sl].bitcast(F32), op0=ALU.max,
                    op1=ALU.subtract), a)
                s.free = (d,)
            t_r[half] = d
            if half == 1:
                chunk_done("up", p)

        def expert(half):
            hi, lo, tw = chunk("exp")
            for t in range(half * 4, half * 4 + 4):
                s, fr = ring4.take()
                b = s.parts[0]
                ts_ = slice(t * 128, (t + 1) * 128)
                p = mm3(b[:, 0:264], [((AT[0][:, k, ts_], AT[1][:, k, ts_]), (hi[:, k * 264:k * 264 + 264], lo[:, k * 264:k * 264 + 264]))
                                      for k in range(2)], tw, t_hn[half], *fr)
                d = dve.op(lambda e, b=b, t=t: e.max(top[:, t, :], b[:, 256:264]), p)
                lg[t] = act.op(lambda e, b=b, t=t: e.copy(AO[:, t, :], b[:, 0:256]), d)
                s.free = (lg[t],)
            if half == 1:
                chunk_done("exp", p)
            h = slice(half * 4, half * 4 + 4)
            d = dve.op(lambda e: e.tensor_tensor(e2[:, 0, h], top[:, h, 1], top[:, h, 0], ALU.subtract), d)
            a = act.op(lambda e: e.activation(e2[:, 1, h], e2[:, 0, h], ACT.Exp), d)
            d = dve.op(lambda e: e.tensor_scalar(e2[:, 2, h], e2[:, 1, h], 1.0, None, ALU.add), a)
            d = dve.op(lambda e: e.reciprocal(e2[:, 3, h], e2[:, 2, h]), d)
            d = dve.op(lambda e: e.tensor_tensor(e2[:, 2, h], e2[:, 1, h], e2[:, 3, h], ALU.mult), d)
            t_rw[half] = dve.op(lambda e: e.tensor_tensor(e2[:, 0, h], e2[:, 2, h], e2[:, 3, h], ALU.add), d)

        def ffn_down(half):
            hi, lo, tw = chunk("down")
            for t in range(half * 4, half * 4 + 4):
                s, fr = ring4.take()
                b = s.parts[0]
                ts_ = slice(t * 128, (t + 1) * 128)
                p = mm3(b[:, 0:256], [((BT[0][:, k, ts_], BT[1][:, k, ts_]), (hi[:, k * 256:k * 256 + 256], lo[:, k * 256:k * 256 + 256]))
                                      for k in range(2)], tw, t_r[half], *fr)
                d = dve.op(lambda e, t=t: e.scalar_tensor_tensor(out=XO[:, t, :], in0=AO[:, t, :], scalar=e2[:, 0, t:t + 1],
                           in1=XO[:, t, :], op0=ALU.mult, op1=ALU.add), t_rw[half], lg[t])
                d = dve.op(lambda e, b=b, t=t: e.tensor_tensor(XO[:, t, :], XO[:, t, :], b[:, 0:256], ALU.add), p, d)
                s.free = (d,)
                t_x2[t] = d
            if half == 1:
                chunk_done("down", p)

        def next_norm(half):
            next_norm.rd = layernorm(XO, NB, half, t_x2[half * 4:half * 4 + 4], free=(t_hn[half],))

        up(0)
        rest[0]()
        rest[1]()
        expert(0)
        rest[2]()
        up(1)
        ffn_down(0)
        next_norm(0)
        expert(1)
        rd_l = [next_norm.rd, None]
        ffn_down(1)
        t_hl[0] = turn(NB, AT, ring4, 0, rd_l[0])
        next_norm(1)
        rd_l[1] = next_norm.rd
        ring_done(ring4, (4, 5, 6, 7))
        mlp_end = (last_of(pe), last_of(act), last_of(dve), last_of(pool))
        mlp.close()

        l1 = ExitStack()
        QH = [(sb(f"QHh{i}", [128, 8, 256], R32, ctx=l1), sb(f"QHl{i}", [128, 8, 256], R32, ctx=l1)) for i in range(2)]
        UT = (sb("UTh", [128, 8, 256], R32, ctx=l1), sb("UTl", [128, 8, 256], R32, ctx=l1))
        CD = (sb("CDh", [128, T], R32, ctx=l1), sb("CDl", [128, T], R32, ctx=l1))
        x1f = X1[:, :, :].rearrange("p t d -> p (t d)")
        aof = AO[:, :, :].rearrange("p t d -> p (t d)")
        CF = x1f[:, 0:1024]
        CN = x1f[:, 1024:1536].rearrange("p (t c) -> p t c", t=NT)
        rr = sb("rr", [128, NT, 16], ctx=l1)
        rrs = sb("rrs", [128, NT, 16], ctx=l1)
        PB = [sb(f"PB{i}", [128, 4, 256], ctx=l1) for i in range(3)]
        PN = [aof[:, i * 512:i * 512 + 512] for i in range(4)]
        sml = sb("sml", [128, 4, 20], ctx=l1)

        cb = sm_("cb")
        t_c, t_cq, t_cn, t_rr = [None, None], [None, None], [None, None], [None, None]
        SC = float(1.0 / np.sqrt(128.0))

        def latent(half, m, ring):
            hi, lo, tw = chunk("proj")
            sl = slice(half * 512, half * 512 + 512)
            s, fr = ring.take()
            b = s.parts[0]
            p = mm3(b[:, :], [((hi[:, k * 384 + m * 128:k * 384 + m * 128 + 128], lo[:, k * 384 + m * 128:k * 384 + m * 128 + 128]),
                               (AT[0][:, k, sl], AT[1][:, k, sl])) for k in range(2)], tw, t_hl[half], *fr)
            ho, lo2 = (CD[0][:, sl], CD[1][:, sl]) if m == 0 else (BT[0][:, m - 1, sl], BT[1][:, m - 1, sl])
            a = act.op(lambda e: e.activation(ho, b[:, :], ACT.Identity, bias=cb[:, m:m + 1]), p, *mlp_end)
            d = dve.op(lambda e: e.scalar_tensor_tensor(
                out=lo2, in0=b[:, :], scalar=cb[:, m:m + 1], in1=ho.bitcast(F32), op0=ALU.add, op1=ALU.subtract), a)
            if m == 0:
                d = dve.op(lambda e: e.tensor_scalar(CF[:, sl], b[:, :], cb[:, 0:1], None, ALU.add))
                t_c[half] = d
            s.free = (d,)
            t_cq[half] = d
            if half == 1 and m == 2:
                chunk_done("proj", p)

        def latent_rest(half, ring):
            s, fr = ring.take()
            b = s.parts[0]
            for c in range(4):
                p = pe.op(lambda e, c=c: e.transpose(b[:, c * 64:c * 64 + 64],
                          CF[0:64, half * 512 + c * 128:half * 512 + (c + 1) * 128], ident[0:64, 0:64]), t_c[half], *fr)
            hs = slice(half * 4, half * 4 + 4)
            for c in range(4):
                t = half * 4 + c
                ts_ = slice(t * 128, (t + 1) * 128)
                p = mm3(b[:, 256 + c * 16:256 + (c + 1) * 16], [((BT[0][:, k, ts_], BT[1][:, k, ts_]),
                        (RTW[0][:, k, :], RTW[1][:, k, :])) for k in range(2)], t_cq[half], fuse.done)
            t_cn[half] = act.op(lambda e: e.copy(CN[:, hs, :], b[:, 0:256].rearrange("p (t c) -> p t c", c=64)), p)
            a = dve.op(lambda e: e.tensor_copy(rr[:, hs, :], b[:, 256:320].rearrange("p (t h) -> p t h", h=16)), t_cn[half])
            t_rr[half] = dve.op(lambda e: e.tensor_scalar(rrs[:, hs, :], rr[:, hs, :], SC, None, ALU.mult), a)
            s.free = (a,)

        rS, rT, rU, rM = bank_ring((0, 1, 2)), bank_ring((3, 4)), bank_ring((5, 6)), bank_ring((7,))
        pbr = Ring([Slot(b) for b in PB])
        pnr = Ring([Slot(b) for b in PN])
        smr = Ring([Slot(sml[:, i, :]) for i in range(4)])
        qhr = Ring([Slot(*q) for q in QH])
        for r in (pbr, pnr, smr, qhr):
            for s in r.slots:
                s.free = mlp_end
        qh = {}
        tq = {}

        def latent_q(b, j2):
            if j2 == 0:
                qh[b] = qhr.take()
            sq, fq = qh[b]
            s, fr = rM.take()
            bk = s.parts[0]
            bs_ = slice(b * 256, b * 256 + 256)
            for i in range(2):
                j = 2 * j2 + i
                p = mm3(bk[:, i * 256:i * 256 + 256], [((MTW[0][:, k, j * 128:j * 128 + 128], MTW[1][:, k, j * 128:j * 128 + 128]),
                        (BT[0][:, k, bs_], BT[1][:, k, bs_])) for k in range(2)], t_cq[b // 2], fuse.done, *fr)
            t = split_from(sq.parts[0][:, 2 * j2:2 * j2 + 2, :].rearrange("p j n -> p (j n)"),
                           sq.parts[1][:, 2 * j2:2 * j2 + 2, :].rearrange("p j n -> p (j n)"), bk[:, :], p, *fq)
            s.free = (t,)
            tq[(b, j2)] = t

        def l1_scores(b, j):
            sq, _ = qh[b]
            ss, fs = smr.take()
            m = ss.parts[0]
            m4 = lambda c: m[:, 4 * c:4 * c + 4]
            got = []
            for i in range(2):
                o = 64 * i
                s, fr = rS.take()
                bk = s.parts[0]
                kv = [c[o:o + 64, b * 256:b * 256 + 256] for c in CD]
                for qt in range(2):
                    p = mm3(bk[:, qt * 256:qt * 256 + 256], [(tuple(q[o:o + 64, j, qt * 128:qt * 128 + 128] for q in sq.parts), kv)],
                            tq[(b, j // 2)], t_c[b // 2], *fr)
                v = bk[:, :].rearrange("p (q k) -> p q k", q=2)
                d = dve.op(lambda e, i=i, v=v: e.tensor_reduce(m[:, 2 * i:2 * i + 2], v, AX_X, ALU.max), p, *fs)
                got.append((s, v))
            if j == 7:
                sq.free = (p,)
            rv, rsv = (a[:, 2 * b:2 * b + 2, 2 * j:2 * j + 2].rearrange("p t h -> p h t") for a in (rr, rrs))
            m3 = lambda c: m4(c).rearrange("p (h t) -> p h t", h=2)
            d = dve.op(lambda e: e.tensor_tensor(m3(1), m3(0), rv, ALU.add), d, t_rr[b // 2])
            d = dve.op(lambda e: e.scalar_tensor_tensor(out=m3(2), in0=m3(1), scalar=-SC, in1=rsv, op0=ALU.mult,
                                                        op1=ALU.add), d)
            sp_, fp = pbr.take()
            P = sp_.parts[0]
            for i, (s, v) in enumerate(got):
                for qt in range(2):
                    c = 2 * i + qt
                    a = act.op(lambda e, c=c, qt=qt, v=v: e.activation(P[:, c, :], v[:, qt, :], ACT.Exp, bias=m[:, 8 + c:9 + c],
                                                                       scale=SC, accum_out=m[:, 12 + c:13 + c]), d, *fp)
                s.free = (a,)
            return ss, sp_, a

        def l1_norm(ss, sp_, a):
            m, P = ss.parts[0], sp_.parts[0]
            d = dve.op(lambda e: e.reciprocal(m[:, 16:20], m[:, 12:16]), a)
            ready = []
            for c in range(4):
                t = pool.op(lambda e, c=c: e.tensor_scalar(P[:, c, :], P[:, c, :], m[:, 16 + c:17 + c], 1.0, ALU.mult,
                                                           ALU.mult), d)
                if c % 2:
                    ready.append(t)
            ss.free = (t,)
            return sp_, ready

        def l1_turns(b, j, sp_, ready):
            P = sp_.parts[0]
            got = []
            for i in range(2):
                s, fr = rT.take()
                bk = s.parts[0]
                for kc in range(2):
                    for qt in range(2):
                        p = pe.op(lambda e, kc=kc, qt=qt, bk=bk, i=i: e.transpose(
                            bk[:, kc * 256 + qt * 128:kc * 256 + qt * 128 + 128],
                            P[:, 2 * i + qt, kc * 128:kc * 128 + 128], ident), ready[i], *fr, signal=kc == 1 and qt == 1)
                s4, f4 = pnr.take()
                a = act.op(lambda e, s4=s4, bk=bk: e.copy(s4.parts[0], bk[:, :]), p, *f4)
                s.free = (a,)
                got.append((s4, a))
            sp_.free = (p,)
            return got

        ut_free = [mlp_end]
        ut_tok = {}

        def l1_weigh(b, j, got):
            s, fr = rU.take()
            bk = s.parts[0]
            for i, (s4, a) in enumerate(got):
                o = 64 * i
                for kc in range(2):
                    p = pe.op(lambda e, kc=kc, o=o, s4=s4: e.matmul(bk[o:o + 64, 0:256], CN[:, 2 * b + kc, :],
                              s4.parts[0][:, kc * 256:kc * 256 + 256], start=kc == 0, stop=kc == 1),
                              a, t_cn[b // 2], *fr, signal=kc == 1)
                s4.free = (p,)
            ut_tok[b] = split_from(UT[0][:, j, :], UT[1][:, j, :], bk[:, 0:256], p, *ut_free[0])
            s.free = (ut_tok[b],)

        t_x3 = [None] * NT

        def l1_out(b):
            s, fr = rM.take()
            bk = s.parts[0]
            for qt in range(2):
                qs_ = slice(qt * 128, qt * 128 + 128)
                p = mm3(bk[:, qt * 256:qt * 256 + 256], [((UT[0][:, j, qs_], UT[1][:, j, qs_]),
                        (NTW[0][:, j, :], NTW[1][:, j, :])) for j in range(8)], ut_tok[b], *fr)
            ut_free[0] = (p,)
            v = XO[:, 2 * b:2 * b + 2, :]
            d = dve.op(lambda e: e.tensor_tensor(v, v, bk[:, :].rearrange("p (t n) -> p t n", t=2), ALU.add), p)
            s.free = (d,)
            t_x3[2 * b] = t_x3[2 * b + 1] = dve.op(lambda e: e.tensor_tensor(
                v, v, bout[:, :].unsqueeze(1).to_broadcast([128, 2, 256]), ALU.add), d, fuse.bias)

        t_h4 = [None, None]
        rd4 = [None, None]

        def last_norm(half):
            rd4[half] = layernorm(XO, NB, half, t_x3[half * 4:half * 4 + 4], free=(t_hl[half],))

        def last_turn(half, ring):
            t_h4[half] = turn(NB, AT, ring, half, rd4[half], free=(t_cq[1],))

        for m in range(3):
            latent(0, m, rM)
        latent_rest(0, rM)
        for j2 in range(4):
            latent_q(0, j2)
        def turn1(k):
            s, fr = rM.take()
            bk = s.parts[0]
            for c in range(4):
                t = pe.op(lambda e, c=c: e.transpose(bk[:, c * 128:(c + 1) * 128], NB[:, 4 + c, k * 128:(k + 1) * 128],
                                                     ident), rd_l[1][c], *fr, signal=c == 3)
            t_hl[1] = split_from(AT[0][:, k, 512:1024], AT[1][:, k, 512:1024], bk[:, :], t)
            s.free = (t_hl[1],)

        fill = {(0, 0): [lambda: turn1(0)], (0, 1): [lambda: turn1(1)], (0, 2): [lambda: latent(1, 0, rM)],
                (0, 3): [lambda: latent(1, 1, rM)], (0, 4): [lambda: latent(1, 2, rM)],
                (0, 5): [lambda: latent_rest(1, rM)],
                (2, 4): [lambda: last_norm(0)], (2, 6): [lambda: last_turn(0, rM)]}
        for b in range(3):
            for j2 in range(4):
                fill.setdefault((b, 4 + j2), []).append(lambda b=b, j2=j2: latent_q(b + 1, j2))
        us = [(b, j) for b in range(4) for j in range(8)]
        so_, to_ = {}, {}
        for i in range(len(us) + 4):
            if 0 <= i - 1 < len(us):
                so_[i - 1] = l1_norm(*so_[i - 1])
            if 0 <= i - 2 < len(us):
                to_[i - 2] = l1_turns(*us[i - 2], *so_[i - 2])
            if i < len(us):
                so_[i] = l1_scores(*us[i])
            if 0 <= i - 4 < len(us) and us[i - 4][1] == 7:
                l1_out(us[i - 4][0])
            if 0 <= i - 3 < len(us):
                l1_weigh(*us[i - 3], to_[i - 3])
            if i < len(us):
                for f in fill.get(us[i], ()):
                    f()
        ring_done(rS, (0, 1, 2))
        ring_done(rT, (3, 4))
        ring_done(rU, (5, 6))
        ring_done(rM, (7,))
        l1_end = (last_of(pe), last_of(act), last_of(dve), last_of(pool))
        l1.close()

        m1 = ExitStack()
        T1 = [sb(f"U1{i}", [128, 512], ctx=m1) for i in range(2)]
        T2 = [sb(f"U2{i}", [128, 512], ctx=m1) for i in range(3)]
        HH = [(sb(f"VVh{i}", [128, 512], R32, ctx=m1), sb(f"VVl{i}", [128, 512], R32, ctx=m1)) for i in range(3)]
        SELf = sb("SELf", [32, 22 * 128], ctx=m1)
        SELr = sb("SELr", [32, 22 * 128], R32, ctx=m1)
        CTr = sb("CTr", [32, T], R32, ctx=m1)
        pr = sb("pr", [128, NT, 24], ctx=m1)
        rp = sb("rp", [128, NT, 24], ctx=m1)
        tp8 = sb("tp8", [128, NT, 8], ctx=m1)
        nm = sb("nm", [128, 4, NT], ctx=m1)
        chr_ = sb("chr", [128, NT, 16], R32, ctx=m1)
        cl = sb("cl", [128, NT, 32], ctx=m1)
        t1r = Ring([Slot(b) for b in T1])
        t2r = Ring([Slot(b) for b in T2])
        hr = Ring([Slot(*b) for b in HH])
        for r in (t1r, t2r, hr):
            for s in r.slots:
                s.free = l1_end
        s_sel = semaphore("s_sel")
        t_sel = sp.dma(SELf[:, :], sel, s_sel, 16, *l1_end)
        t_sel = pool.op(lambda e: e.tensor_scalar(SELr[:, :], SELf[:, :], 1.0, 0.0, ALU.mult, ALU.add), t_sel)

        ring4 = bank_ring((4, 5, 6, 7))
        t_ct = [None, None]
        t_pad = dve.op(lambda e: e.memset(pr[:, :, 16:24], -1.0), *l1_end)
        gates = {}

        def gate(half):
            hi, lo, tw = chunk("gate")
            s, fr = ring4.take()
            for c in range(4):
                ts_ = slice((half * 4 + c) * 128, (half * 4 + c + 1) * 128)
                p = mm3(s.parts[0][:, c * 16:(c + 1) * 16], [((AT[0][:, k, ts_], AT[1][:, k, ts_]),
                        (hi[:, k * 16:k * 16 + 16], lo[:, k * 16:k * 16 + 16])) for k in range(2)], tw, t_h4[half], *fr)
            if half == 1:
                chunk_done("gate", p)
            g3 = s.parts[0][:, 0:64].rearrange("p (t h) -> p t h", h=16)
            hs = slice(half * 4, half * 4 + 4)
            d = dve.op(lambda e: e.tensor_reduce(nm[:, 0, hs], g3, AX_X, ALU.max), p)
            d = dve.op(lambda e: e.tensor_tensor(pr[:, hs, 0:16], g3, nm[:, 0, hs].unsqueeze(2).to_broadcast([128, 4, 16]),
                                                 ALU.subtract), d)
            s.free = (d,)
            gates[half] = act.op(lambda e: e.activation(pr[:, hs, 0:16], pr[:, hs, 0:16], ACT.Exp), d)

        def route(half):
            hs = slice(half * 4, half * 4 + 4)
            d = dve.op(lambda e: e.tensor_reduce(nm[:, 1, hs], pr[:, hs, 0:16], AX_X, ALU.add), gates[half])
            d = dve.op(lambda e: e.reciprocal(nm[:, 2, hs], nm[:, 1, hs]), d)
            d = dve.op(lambda e: e.tensor_tensor(pr[:, hs, 0:16], pr[:, hs, 0:16],
                                                 nm[:, 2, hs].unsqueeze(2).to_broadcast([128, 4, 16]), ALU.mult), d)
            for t in range(half * 4, half * 4 + 4):
                m = dve.op(lambda e, t=t: e.max(tp8[:, t, :], pr[:, t, 0:16]), d)
            d = dve.op(lambda e: e.memset(tp8[:, hs, 6:8], -1.0), m)
            for t in range(half * 4, half * 4 + 4):
                m = dve.op(lambda e, t=t: e.match_replace(rp[:, t, :], tp8[:, t, :], pr[:, t, :], -2.0), d, t_pad)
            d = dve.op(lambda e: e.scalar_tensor_tensor(out=cl[:, hs, 16:32], in0=rp[:, hs, 0:16], scalar=0.0,
                                                        in1=pr[:, hs, 0:16], op0=ALU.is_lt, op1=ALU.mult), m)
            d = dve.op(lambda e: e.tensor_copy(chr_[:, hs, :], cl[:, hs, 16:32]), d)
            d = dve.op(lambda e: e.tensor_copy(cl[:, hs, 0:16], chr_[:, hs, :].bitcast(F32)), d)
            gates[half] = dve.op(lambda e: e.tensor_tensor(cl[:, hs, 16:32], cl[:, hs, 16:32], chr_[:, hs, :].bitcast(F32),
                                                           ALU.subtract), d)

        def spread(half):
            s, fr = ring4.take()
            for c in range(4):
                p = pe.op(lambda e, c=c: e.transpose(s.parts[0][0:32, c * 128:(c + 1) * 128],
                          cl[:, half * 4 + c, :], ident), gates[half], *fr)
            t_ct[half] = act.op(lambda e: e.copy(CTr[:, half * 512:half * 512 + 512], s.parts[0][0:32, :]), p)
            s.free = (t_ct[half],)

        def combine(b, j, sl, *fr):
            return pe.op(lambda e: e.matmul(b[:, :], SELr[:, j * 128:(j + 1) * 128], CTr[:, sl], start=True, stop=True),
                         t_sel, t_ct[sl.start // 512], *fr)

        ov = out.rearrange("(t p) d -> p t d", p=128)
        sent = []

        def after_moe(half, y):
            def one(c):
                t = half * 4 + c
                d = dve.op(lambda e: e.tensor_tensor(XO[:, t, :], XO[:, t, :], ybank(t), ALU.add), y[t | 1])
                sent.append(sp.dma(ov[:, t, :], XO[:, t, :], s_out, 16 * len(sent) + 16, d))
            return [lambda c=c: one(c) for c in range(4)]

        last_norm(1)
        gate(0)
        last_turn(1, ring4)
        route(0)
        rest = run_mlp([f"moe{j}" for j in range(25)], True, ring4, AT, t_h4, after=after_moe, combine=combine,
                       before=[lambda: gate(1)], at={(1, 0): lambda: route(1), (2, 0): lambda: spread(0),
                                                     (0, 1): lambda: spread(1)})
        for f in rest:
            f()
        sp.wait(sent[-1])
        m1.close()

        with nc.Block() as block:
            @block.sync
            def _(e):
                sp.play(e)

            @block.tensor
            def _(e):
                pe.play(e)

            @block.vector
            def _(e):
                dve.play(e)

            @block.scalar
            def _(e):
                act.play(e)

            @block.gpsimd
            def _(e):
                pool.play(e)


def last_of(engine):
    return (engine.sem, engine.count)


def _layout(i):
    f = np.float32
    a = {k: np.asarray(v) for k, v in i.items()}

    def kmajor(m):
        return m.reshape(-1, 128, m.shape[-1]).transpose(1, 0, 2).reshape(128, -1)

    def pad(m, n, axis):
        w = [(0, 0)] * m.ndim
        w[axis] = (0, n - m.shape[axis])
        return np.pad(m, w)

    ch = {}
    qkv = np.concatenate([a["L0_attn_w_qkv"], a["L0_attn_gg_w1"]], 1)
    ch["qkv0"], ch["qkv1"] = qkv[0:128], qkv[128:256]
    ch["wo"] = kmajor(a["L0_attn_w_o"])
    for j in range(8):
        s = slice(j * 128, j * 128 + 128)
        ch[f"mem{j}"] = np.concatenate([kmajor(a["L0_attn_mem_w1"][:, s]), a["L0_attn_mem_w2"][s]], 1)
    w1, w3 = pad(a["L0_attn_ffn_w1"], 768, 1), pad(a["L0_attn_ffn_w3"], 768, 1)
    w2 = pad(a["L0_attn_ffn_w2"], 768, 0)
    for j in range(6):
        s = slice(j * 128, j * 128 + 128)
        ch[f"ffn{j}"] = np.concatenate([kmajor(w1[:, s]), kmajor(w3[:, s]), w2[s]], 1)
    up = a["L0_ffn_W_up"].T
    ch["up"] = np.concatenate([kmajor(up[:, 0:128]), kmajor(up[:, 128:256])], 1)
    ch["exp"] = kmajor(np.concatenate([a["L0_ffn_W_expert"], a["L0_ffn_W_gate"].T], 1))
    ch["down"] = kmajor(a["L0_ffn_W_down"].T)
    uq, uk, uv = (a[f"L1_attn_W_{n}_w"].reshape(16, 128, -1) for n in ("UQ", "UK", "UV"))
    buq, buk, buv = (a[f"L1_attn_W_{n}_b"].reshape(16, 128, 1) for n in ("UQ", "UK", "UV"))
    wo = a["L1_attn_W_O_w"].T.reshape(16, 128, 256)
    for h in range(16):
        ch[f"fuse{h}"] = np.concatenate([pad(np.concatenate([uq[h], buq[h]], 1), 256, 1), uk[h], buk[h], uv[h], buv[h], wo[h]], 1)
    dkv, dq = a["L1_attn_W_DKV_w"].T, a["L1_attn_W_DQ_w"].T
    ch["proj"] = kmajor(np.concatenate([dkv, dkv, pad(dq, 256, 1)], 1))
    ch["gate"] = kmajor(a["L1_ffn_gate_w"].T)
    e1, e2 = a["L1_ffn_w1"], a["L1_ffn_w2"]
    g = e1[:, 0:176].reshape(2816, 256).T
    u = e1[:, 176:352].reshape(2816, 256).T
    dn = e2.transpose(0, 2, 1).reshape(2816, 256)
    s1 = a["L1_ffn_shared_w1"].T
    sg, su, sd = pad(s1[:, 0:352], 384, 1), pad(s1[:, 352:704], 384, 1), pad(a["L1_ffn_shared_w2"].T, 384, 0)
    g, u, dn = np.concatenate([sg, g], 1), np.concatenate([su, u], 1), np.concatenate([sd, dn], 0)
    for j in range(25):
        s = slice(j * 128, j * 128 + 128)
        ch[f"moe{j}"] = np.concatenate([kmajor(g[:, s]), kmajor(u[:, s]), dn[s]], 1)
    w = np.concatenate([ch[n] for n, _, _ in CHUNKS], 1)

    sm = np.zeros((128, SM_N), f)

    def put(name, v):
        sm[:, SM_OFF[name][0]:SM_OFF[name][1]] = v

    p = np.arange(128)
    put("ident", np.eye(128, dtype=f))
    inv = (f(1.0) / np.power(f(10000.0), np.arange(0, 16, 2, dtype=f) / f(16))).astype(f)
    fr = (np.arange(256, dtype=f)[:, None] * inv[None, :]).astype(f).astype(np.float64)
    fr = np.concatenate([fr, fr], 1)
    cos, sin = np.cos(fr).astype(f), np.sin(fr).astype(f)
    sin[:, 0:8] = -sin[:, 0:8]
    put("cos", cos.reshape(2, 128, 16).transpose(1, 0, 2).reshape(128, 32))
    put("sin", sin.reshape(2, 128, 16).transpose(1, 0, 2).reshape(128, 32))
    put("qs", a["L0_attn_q_scale"][None, :])
    put("ks", a["L0_attn_k_scale"][None, :])
    pos = (p[:, None] + 128 * np.arange(2)[None, :]).astype(np.float64)
    put("dk", (0.5 * 0.9 ** -pos).astype(f))
    put("dq", (0.9 ** pos).astype(f))
    put("mh", (p[:, None] // 16 == np.arange(8)[None, :]).astype(f))
    put("nw", np.concatenate([a["L0_attn_norm1_w"].reshape(2, 128).T, a["L0_attn_norm2_w"].reshape(2, 128).T], 1))
    put("ggw2", a["L0_attn_gg_w2"].reshape(1, 64))
    cb = np.zeros((128, 3), f)
    cb[0:64, 0] = cb[64:128, 0] = a["L1_attn_W_DKV_b"]
    cb[:, 1] = a["L1_attn_W_DQ_b"][0:128]
    cb[0:64, 2] = a["L1_attn_W_DQ_b"][128:192]
    cb[64, 2] = 1.0
    put("cb", cb)
    put("bo", a["L1_attn_W_O_b"][None, :])
    rel = p[:, None] - p[None, :]
    m0 = np.where((rel >= 0) & (rel < 64), 0.0, NEG).astype(f)
    rel = p[:, None] + 64 - np.arange(192)[None, :]
    m1 = np.where((rel >= 0) & (rel < 64), 0.0, NEG).astype(f)
    put("mask0", np.tile(m0, (1, 4)))
    put("mask1", np.tile(m1, (1, 2)))
    sel = np.zeros((32, 22 * 128), f)
    hid = np.arange(22 * 128)
    sel[hid // 176, hid] = 1.0
    sel[16 + hid // 176, hid] = 1.0
    return {"x": a["L0_attn_x"].reshape(T, 256), "w": w, "sm": sm, "sel": sel}


def kernel(**inputs):
    import concourse.bacc as _bacc
    from concourse import mybir as _mybir
    from concourse.bass_utils import run_bass_kernel_spmd as _run

    nc = _bacc.Bacc("TRN2", target_bir_lowering=False, num_devices=1)
    arrays = {f"in_{k}": np.ascontiguousarray(v) for k, v in _layout(inputs).items()}
    args = [nc.dram_tensor(k, v.shape, _mybir.dt.from_np(v.dtype), kind="ExternalInput").ap() for k, v in arrays.items()]
    o = nc.dram_tensor("out_dram", (T, 256), F32, kind="ExternalOutput").ap()
    build(nc, *args, o)
    r = _run(nc, [arrays], core_ids=[0])
    return r.results[0]["out_dram"].reshape(4, 256, 256)
```

```python
from contextlib import ExitStack

import numpy as np

import concourse.bass as bass
from concourse import mybir

F32 = mybir.dt.float32
R32 = mybir.dt.float32r
BF16 = mybir.dt.bfloat16
I32 = mybir.dt.int32
ALU = mybir.AluOpType
ACT = mybir.ActivationFunctionType
AX_X = mybir.AxisListType.X

T = 1024
NT = T // 128
SLOT = 832
NRAW = 3
NPART = 4
NMORE = 3
LAG = 5
NEG = -1.0e30

SM_OFF = {}
_at = 0
for _name, _n in (("ident", 128), ("cos", 32), ("sin", 32), ("qs", 16), ("ks", 16), ("dk", 2), ("dq", 2),
                  ("mh", 8), ("nw", 4), ("ggw2", 64), ("cb", 3), ("bo", 256), ("mask0", 512), ("mask1", 384)):
    SM_OFF[_name] = (_at, _at + _n)
    _at += _n
SM_N = _at

CHUNKS = [("qkv0", 832, True), ("qkv1", 832, True)]
CHUNKS += [(f"fuse{h}", 642, False) for h in range(16)]
CHUNKS += [("wo", 512, True)]
CHUNKS += [(f"mem{j}", 512, True) for j in range(8)]
CHUNKS += [(f"ffn{j}", 768, True) for j in range(6)]
CHUNKS += [("up", 512, True), ("exp", 528, True), ("down", 512, True)]
CHUNKS += [("proj", 768, True)]
CHUNKS += [("gate", 32, True)]
CHUNKS += [(f"moe{j}", 768, True) for j in range(25)]
CH_OFF = {}
_at = 0
for _name, _n, _ in CHUNKS:
    CH_OFF[_name] = _at
    _at += _n
W_N = _at


class Engine:

    def __init__(self, sem):
        self.sem, self.count, self.todo, self.seen = sem, 0, [], {}

    def wait(self, *tokens):
        for sem, value in tokens:
            if self.seen.get(id(sem), 0) < value:
                self.seen[id(sem)] = value
                self.todo.append(lambda e, s=sem, v=value: e.wait_ge(s, v))

    def op(self, f, *tokens, signal=True):
        self.wait(*tokens)
        if signal:
            self.count += 1
            self.todo.append(lambda e: f(e).then_inc(self.sem, 1))
            return (self.sem, self.count)
        self.todo.append(f)
        return None

    def dma(self, out, in_, sem, value, *tokens):
        self.wait(*tokens)
        self.todo.append(lambda e: e.dma_start(out, in_).then_inc(sem, 16))
        return (sem, value)

    def play(self, e):
        for f in self.todo:
            f(e)


class Slot:
    def __init__(self, *parts):
        self.parts, self.free = parts, ()


class Ring:

    def __init__(self, slots):
        self.slots, self.at = slots, 0

    def take(self):
        s = self.slots[self.at % len(self.slots)]
        self.at += 1
        assert s.free is not None
        free, s.free = s.free, None
        return s, free


def build(nc, x, w, sm, sel, out):
    outer = ExitStack()
    with outer:
        def sb(name, shape, dt=F32, ctx=outer):
            return ctx.enter_context(nc.sbuf_tensor(name, shape, dt))

        def semaphore(name):
            return outer.enter_context(nc.semaphore(name))

        banks = [outer.enter_context(nc.psum_tensor(f"ps{i}", [128, 512], F32)) for i in range(8)]
        bank_free = [()] * 8

        def bank_ring(ids):
            r = Ring([Slot(banks[i]) for i in ids])
            for s, i in zip(r.slots, ids):
                s.free = bank_free[i]
            return r

        def ring_done(r, ids):
            for s, i in zip(r.slots, ids):
                bank_free[i] = s.free

        pe = Engine(semaphore("s_pe"))
        dve = Engine(semaphore("s_dve"))
        act = Engine(semaphore("s_act"))
        pool = Engine(semaphore("s_pool"))
        sp = Engine(semaphore("s_sp"))

        XO = sb("XO", [128, NT, 256])
        X1 = sb("X1", [128, NT, 256])
        NB = sb("NB", [128, NT, 256])
        AO = sb("AO", [128, NT, 256])
        AT = (sb("ATh", [128, 2, T], R32), sb("ATl", [128, 2, T], R32))
        BT = (sb("BTh", [128, 2, T], R32), sb("BTl", [128, 2, T], R32))
        SM = sb("SM", [128, SM_OFF["mask0"][0]])
        sm_ = lambda n: SM[:, SM_OFF[n][0]:SM_OFF[n][1]]
        ident = sm_("ident")
        raws = [(sb(f"wr{i}", [128, SLOT]), semaphore(f"s_w{i}")) for i in range(NRAW)]
        parts = [(sb(f"wh{i}", [128, SLOT], R32), sb(f"wl{i}", [128, SLOT], R32)) for i in range(NPART)]
        NTW = (sb("NTh", [128, 8, 256], R32), sb("NTl", [128, 8, 256], R32))
        MTW = (sb("MTh", [128, 2, 1024], R32), sb("MTl", [128, 2, 1024], R32))
        RTW = (sb("RTh", [128, 2, 16], R32), sb("RTl", [128, 2, 16], R32))
        bout = sb("bout", [128, 256])
        negh = sb("negh", [128, 128])
        st = sb("st", [128, NT, 6])
        mv = sb("mv", [128, NT, 2])
        ve = sb("ve", [128, NT])
        rs = sb("rs", [128, NT])
        r2 = sb("r2", [128, NT])
        v2 = sb("v2", [128, NT])

        s_in = semaphore("s_in")
        s_sm = semaphore("s_sm")
        s_out = semaphore("s_out")

        xv = x.rearrange("(t p) d -> p t d", p=128)
        s_x2 = semaphore("s_x2")
        n_early = SM_OFF["mask0"][0]
        t_x = [sp.dma(XO[:, 0:4, :], xv[:, 0:4, :], s_in, 16)]
        t_sm = sp.dma(SM[:, 0:n_early], sm[:, 0:n_early], s_sm, 16)

        index = {n: i for i, (n, _, _) in enumerate(CHUNKS)}
        loaded, raw_read, split_done, slot_of = {}, {}, {}, {}
        slots = [[b, (), len(CHUNKS)] for b in parts]

        def more_slots(bufs, last, token):
            slots.extend([b, token, index[last]] for b in bufs)
            pump()

        nxt = {"load": 0, "split": 0}

        def pump(until=len(CHUNKS)):
            going = True
            while going:
                going = False
                i = nxt["load"]
                if i < len(CHUNKS) and (i < NRAW or i - NRAW in raw_read):
                    name, n, _ = CHUNKS[i]
                    buf, sem = raws[i % NRAW]
                    free = (raw_read[i - NRAW],) if i >= NRAW else ()
                    loaded[i] = sp.dma(buf[:, 0:n], w[:, CH_OFF[name]:CH_OFF[name] + n], sem, 16 * (i // NRAW + 1), *free)
                    nxt["load"] += 1
                    going = True
                i = nxt["split"]
                while i < len(CHUNKS) and not CHUNKS[i][2]:
                    i += 1
                nxt["split"] = i
                if i < until and i in loaded:
                    open_ = [q for q in slots if q[1] is not None and i <= q[2]]
                    if open_:
                        slot = min(open_, key=lambda q: (q[2], q[3] if len(q) > 3 else 0))
                        n = CHUNKS[i][1]
                        raw, (hi, lo) = raws[i % NRAW][0], slot[0]
                        free, slot[1] = slot[1], None
                        slot_of[i] = slot
                        if i < 2:
                            t = act.op(lambda e, raw=raw, hi=hi, n=n: e.copy(hi[:, 0:n], raw[:, 0:n]), loaded[i])
                            t = dve.op(lambda e, raw=raw, hi=hi, lo=lo, n=n: e.tensor_tensor(
                                lo[:, 0:n], raw[:, 0:n], hi[:, 0:n].bitcast(F32), ALU.subtract), t)
                        else:
                            t = pool.op(lambda e, raw=raw, hi=hi, n=n: e.tensor_scalar(
                                hi[:, 0:n], raw[:, 0:n], 1.0, 0.0, ALU.mult, ALU.add), loaded[i], *free)
                            t = pool.op(lambda e, raw=raw, hi=hi, lo=lo, n=n: e.tensor_tensor(
                                lo[:, 0:n], raw[:, 0:n], hi[:, 0:n].bitcast(F32), ALU.subtract), t)
                        split_done[i] = raw_read[i] = t
                        nxt["split"] += 1
                        going = True

        def chunk(name):
            i = index[name]
            if CHUNKS[i][2]:
                hi, lo = slot_of[i][0]
                return hi, lo, split_done[i]
            return raws[i % NRAW][0], None, loaded[i]

        def chunk_done(name, token):
            i = index[name]
            if CHUNKS[i][2]:
                slot_of[i][1:] = [(token,), slot_of[i][2], i]
            else:
                raw_read[i] = token
            pump()

        t_negh = pool.op(lambda e: e.memset(negh[:, :], -0.5))
        t_x.append(sp.dma(XO[:, 4:8, :], xv[:, 4:8, :], s_x2, 16))
        pump(0)
        s_mk = semaphore("s_mk")
        masks = AO[:, :, :].rearrange("p t d -> p (t d)")[:, 0:896]
        t_mk = sp.dma(masks, sm[:, n_early:], s_mk, 16)

        def mm3(o, terms, *tokens, first=True, last=True, skip=False, signal=True):
            n = len(terms)
            pe.wait(*tokens)
            t = None
            for i, ((lh, ll), (rh, rl)) in enumerate(terms):
                for c, (a, b) in enumerate(((lh, rh), (lh, rl), (ll, rh))):
                    fin = i == n - 1 and c == 2
                    t = pe.op(lambda e, a=a, b=b, s=(first and i == 0 and c == 0), p=(last and fin):
                              e.matmul(o, a, b, start=s, stop=p, skip_group_check=skip), signal=fin and signal)
            return t

        def split_from(hi, lo, src, *tokens, scale=None):
            if scale is None:
                a = act.op(lambda e: e.copy(hi, src), *tokens)
                return dve.op(lambda e: e.tensor_tensor(lo, src, hi.bitcast(F32), ALU.subtract), a)
            a = act.op(lambda e: e.activation(hi, src, ACT.Copy, scale=scale), *tokens)
            return dve.op(lambda e: e.scalar_tensor_tensor(out=lo, in0=src, scalar=scale, in1=hi.bitcast(F32),
                                                           op0=ALU.mult, op1=ALU.subtract), a)

        def turn(src, dst, ring, half, ready, free=(), scale=None, ks=(0, 1)):
            done = []
            for k in ks:
                s, fr = ring.take()
                b = s.parts[0]
                for c in range(4):
                    t = pe.op(lambda e, c=c, k=k, b=b: e.transpose(b[:, c * 128:(c + 1) * 128],
                              src[:, half * 4 + c, k * 128:(k + 1) * 128], ident), ready[c], t_sm, *fr,
                              signal=c == 3)
                sl = slice(half * 512, half * 512 + 512)
                t = split_from(dst[0][:, k, sl], dst[1][:, k, sl], b[:, :], t, *free,
                               scale=None if scale is None else scale[:, k:k + 1])
                s.free = (t,)
                done.append(t)
            return done[-1]

        def tilemean(src, half, ready, tiles=(0, 1, 2, 3)):
            for c in tiles:
                t = half * 4 + c
                a = dve.op(lambda e, t=t: e.bn_stats(st[:, t, :], src[:, t, :]), ready[c], signal=True)
                a = dve.op(lambda e, t=t: e.bn_aggr(mv[:, t, :], st[:, t, :]), a)
            return a

        def rsqrt_small(o, i, *tokens):
            n = i.shape[-1]
            return pool.op(lambda e: e.tensor_tensor(o, i, negh[:, 0:n], ALU.pow), t_negh, *tokens)

        def rsqrt_newton(y, v, hx, tmp, *tokens):
            dve.op(lambda e: e.tensor_scalar(hx, v, -0.5, None, ALU.mult), *tokens)
            d = dve.op(lambda e: e.tensor_scalar(y.bitcast(I32), v.bitcast(I32), -0.5, 1597463007.0, ALU.mult, ALU.add))
            for _ in range(3):
                d = dve.op(lambda e: e.tensor_tensor(tmp, y, y, ALU.mult), d)
                d = dve.op(lambda e: e.tensor_tensor(tmp, tmp, hx, ALU.mult), d)
                d = dve.op(lambda e: e.scalar_tensor_tensor(out=y, in0=tmp, scalar=1.5, in1=y, op0=ALU.add,
                                                            op1=ALU.mult), d)
            return d

        def layernorm(src, dst, half, ready, free=(), tiles=(0, 1, 2, 3)):
            return layernorm_apply(src, dst, half, layernorm_rstd(half, tilemean(src, half, ready, tiles)), free)

        def layernorm_rstd(half, a):
            hs = slice(half * 4, half * 4 + 4)
            a = dve.op(lambda e: e.tensor_scalar(ve[:, hs], mv[:, hs, 1], 1e-5, None, ALU.add), a)
            return rsqrt_small(rs[:, hs], ve[:, hs], a)

        def layernorm_apply(src, dst, half, p, free=()):
            out_ = []
            for c in range(4):
                t = half * 4 + c
                out_.append(dve.op(lambda e, t=t: e.tensor_scalar(dst[:, t, :], src[:, t, :], mv[:, t, 0:1],
                                   rs[:, t:t + 1], ALU.subtract, ALU.mult), p, *free))
            return out_

        l0 = ExitStack()
        VK = sb("VK", [128, NT, 16 * 33], ctx=l0)
        QKT = sb("QKT", [128, 4, T], ctx=l0)
        KB = [sb("KB0", [128, 8, 256], ctx=l0)]
        identb = sb("identb", [128, 128], BF16, ctx=l0)
        mb0 = sb("mb0", [128, 512], BF16, ctx=l0)
        mb1 = sb("mb1", [128, 384], BF16, ctx=l0)
        mx = sb("mx", [128, 6, 4], ctx=l0)
        rc = sb("rc", [128, 4, 8], ctx=l0)
        rg = sb("rg", [128, 4, 8], ctx=l0)
        lq = ExitStack()
        QKf = [sb(f"QKf{i}", [128, 512], ctx=lq) for i in range(4)]
        QSf = [sb(f"QSf{i}", [128, 512], ctx=lq) for i in range(4)]
        QRf = [sb(f"QRf{i}", [128, 512], ctx=lq) for i in range(2)]
        sso = sb("sso", [128, NT * 32], ctx=lq)
        rq = sb("rq", [128, NT * 32], ctx=lq)
        hx = sb("hx", [128, 64], ctx=lq)
        ntmp = sb("ntmp", [128, 64], ctx=lq)
        CT = sb("CT", [128, 2, 2, 16], ctx=lq)
        ST = sb("ST", [128, 2, 2, 16], ctx=lq)
        gth = sb("gth", [128, 2, 64], ctx=lq)
        gsl = sb("gsl", [128, 2, 64], ctx=lq)
        gj = sb("gj", [128, 64], ctx=lq)
        gz = sb("gz", [128, NT], ctx=lq)
        gt = sb("gt", [128, NT], ctx=lq)
        gq = sb("gq", [128, NT], ctx=lq)

        vk4 = VK[:, :, :].rearrange("p t (h e) -> p t h e", h=16)
        t_ones = pool.op(lambda e: e.memset(vk4[:, :, :, 32:33], 1.0))

        f_m0, f_m1, f_n, f_b = bank_ring((0,)), bank_ring((1,)), bank_ring((2,)), bank_ring((3,))
        sbias, fb = f_b.take()

        def fuse(h):
            raw, _, tw = chunk(f"fuse{h}")
            uq, uk, uv, wo_ = raw[:, 0:256], raw[:, 256:321], raw[:, 321:385], raw[:, 386:642]
            buv = raw[:, 385:386]
            if h % 4 == 0:
                fuse.m = [f_m0.take(), f_m1.take()]
            if h % 4 == 0:
                fuse.tok = []
            for k in range(2):
                s, fr = fuse.m[k]
                p = pe.op(lambda e, s=s, k=k, h=h: e.matmul(s.parts[0][:, (h % 4) * 65:(h % 4) * 65 + 65],
                          uq[:, k * 128:(k + 1) * 128], uk, start=True, stop=True), tw, *fr)
            if h % 2 == 0:
                fuse.n = f_n.take()
            s, fr = fuse.n
            lo_ = 64 * (h % 2)
            pn = pe.op(lambda e, s=s, lo_=lo_: e.matmul(s.parts[0][lo_:lo_ + 64, 0:256], uv, wo_, start=True, stop=True), *fr)
            pb = pe.op(lambda e, h=h: e.matmul(sbias.parts[0][:, 0:256], buv.to_broadcast([128, 128]), wo_, start=h == 0,
                                               stop=h == 15), *fb)
            chunk_done(f"fuse{h}", pb)
            if h % 2 == 1:
                j = h // 2
                t = split_from(NTW[0][:, j, :], NTW[1][:, j, :], s.parts[0][:, 0:256], pn)
                s.free = (t,)
            if h % 4 == 3:
                j = h // 4
                for k in range(2):
                    s, fr = fuse.m[k]
                    v = s.parts[0][:, 0:260].rearrange("p (h c) -> p h c", c=65)
                    mh_, ml_ = (m[:, k, j * 256:j * 256 + 256].rearrange("p (h c) -> p h c", c=64) for m in MTW)
                    rh_, rl_ = (r[:, k, 4 * j:4 * j + 4] for r in RTW)
                    act.op(lambda e, mh_=mh_, v=v: e.copy(mh_, v[:, :, 0:64]), p)
                    a = act.op(lambda e, rh_=rh_, v=v: e.copy(rh_, v[:, :, 64]))
                    dve.op(lambda e, mh_=mh_, ml_=ml_, v=v: e.tensor_tensor(ml_, v[:, :, 0:64], mh_.bitcast(F32),
                                                                            ALU.subtract), a)
                    t = dve.op(lambda e, rh_=rh_, rl_=rl_, v=v: e.tensor_tensor(rl_, v[:, :, 64], rh_.bitcast(F32),
                                                                                ALU.subtract))
                    s.free = (t,)
                fuse.done = t
            if h == 15:
                fuse.bias = dve.op(lambda e: e.tensor_tensor(bout[:, :], sbias.parts[0][:, 0:256], sm_("bo"), ALU.add), pb)
                sbias.free = (fuse.bias,)
                for r, ids in ((f_m0, (0,)), (f_m1, (1,)), (f_n, (2,)), (f_b, (3,))):
                    ring_done(r, ids)

        ring4 = bank_ring((4, 5, 6, 7))
        t_h = [None, None]
        xn, rd0 = {}, {}

        def first_norm(half):
            hs = slice(half * 4, half * 4 + 4)
            a = tilemean(XO, half, [t_x[half]] * 4)
            a = dve.op(lambda e: e.tensor_scalar(ve[:, hs], mv[:, hs, 1], 1e-5, None, ALU.add), a)
            p = rsqrt_small(rs[:, hs], ve[:, hs], a)
            a = dve.op(lambda e: e.reciprocal(v2[:, hs], ve[:, hs]), a)
            a = dve.op(lambda e: e.tensor_tensor(v2[:, hs], v2[:, hs], mv[:, hs, 1], ALU.mult), a)
            a = dve.op(lambda e: e.tensor_scalar(v2[:, hs], v2[:, hs], 1e-6, None, ALU.add), a)
            p2 = rsqrt_small(r2[:, hs], v2[:, hs], a)
            if half == 0:
                pump(1)
            xn[half] = layernorm_apply(XO, X1, half, p)
            rd0[half] = [dve.op(lambda e, t=t: e.tensor_scalar(NB[:, t, :], X1[:, t, :], r2[:, t:t + 1], None, ALU.mult), p2,
                                xn[half][t % 4]) for t in range(half * 4, half * 4 + 4)]
            if half == 0:
                pump(2)

        def first_turn(half):
            t_h[half] = turn(NB, AT, ring4, half, rd0[half], scale=sm_("nw")[:, 0:2])

        qkf = Ring([Slot(b) for b in QKf])
        qsf = Ring([Slot(b) for b in QSf])
        qrf = Ring([Slot(b) for b in QRf])
        t_vk, t_qkt, t_rope = [None] * NT, [None] * NT, [None] * NT
        t_gz, t_v, held, t_sq = [None] * NT, [None] * NT, {}, [None] * NT

        def project(t):
            tt = t % 2
            ts_ = slice(t * 128, (t + 1) * 128)
            sa, fa = ring4.take()
            ba = sa.parts[0]
            xs = [(AT[0][:, k, ts_], AT[1][:, k, ts_]) for k in range(2)]
            pa = mm3(ba[:, :], [(xs[0], (w0h[:, 0:512], w0l[:, 0:512])), (xs[1], (w1h[:, 0:512], w1l[:, 0:512]))],
                     t_h[t // 4], t_w0, t_w1, *fa)
            sv, fv = ring4.take()
            bv = sv.parts[0]
            project.last = mm3(bv[:, 0:320], [(xs[0], (w0h[:, 512:832], w0l[:, 512:832])),
                                              (xs[1], (w1h[:, 512:832], w1l[:, 512:832]))], *fv)
            s1, f1 = qkf.take()
            s2, f2 = qsf.take()
            QK, QS = s1.parts[0], s2.parts[0]
            a1 = act.op(lambda e: e.activation(QS[:, :], ba[:, :], ACT.Square), pa, *f2)
            a2 = act.op(lambda e: e.copy(QK[:, :], ba[:, :]), *f1)
            sa.free = (a2,)
            t_v[t] = act.op(lambda e: e.copy(vk4[:, t, :, 0:16], bv[:, 0:256].rearrange("p (h d) -> p h d", h=16)),
                            project.last)
            a4 = act.op(lambda e: e.activation(gth[:, tt, :], bv[:, 256:320], ACT.Tanh, scale=0.5),
                        *([t_gz[t - 2]] if t >= 2 else []))
            t_sq[t] = dve.op(lambda e: e.tensor_reduce(sso[:, t * 32:t * 32 + 32], QS[:, :].rearrange("p (h d) -> p h d", d=16),
                                                       AX_X, ALU.add), a1)
            d = dve.op(lambda e: e.scalar_tensor_tensor(out=gsl[:, tt, :], in0=gth[:, tt, :], scalar=1.0,
                       in1=bv[:, 256:320], op0=ALU.add, op1=ALU.mult), a4)
            sv.free = (d,)
            t_gz[t] = dve.op(lambda e: e.tensor_tensor_reduce(gj[:, :], gsl[:, tt, :], sm_("ggw2"), 0.5, 0.0,
                             ALU.mult, ALU.add, gz[:, t:t + 1]), d, *([t_gz[t - 1]] if t else []))
            held[t] = (s1, s2, a2)

        def head_norms(b):
            cs = slice(b * 64, b * 64 + 64)
            d = dve.op(lambda e: e.tensor_scalar(sso[:, cs], sso[:, cs], 1.0 / 16, 1e-6, ALU.mult, ALU.add), t_sq[2 * b + 1])
            t_rope[2 * b] = t_rope[2 * b + 1] = rsqrt_newton(rq[:, cs], sso[:, cs], hx[:, :], ntmp[:, :], d)
            ag = act.op(lambda e: e.activation(gt[:, 2 * b:2 * b + 2], gz[:, 2 * b:2 * b + 2], ACT.Tanh, scale=0.5),
                        t_gz[2 * b + 1])
            held[("g", b)] = dve.op(lambda e: e.scalar_tensor_tensor(out=gq[:, 2 * b:2 * b + 2], in0=gt[:, 2 * b:2 * b + 2],
                                    scalar=1.0, in1=sm_("dk"), op0=ALU.add, op1=ALU.mult), ag)

        def rotate(t):
            tt = t % 2
            s1, s2, a2 = held[t]
            s3, f3 = qrf.take()
            QK, QS, QR = s1.parts[0], s2.parts[0], s3.parts[0]
            d = dve.op(lambda e: e.tensor_tensor(
                QK[:, :].rearrange("p (h d) -> p h d", d=16), QK[:, :].rearrange("p (h d) -> p h d", d=16),
                rq[:, t * 32:t * 32 + 32].unsqueeze(2).to_broadcast([128, 32, 16]), ALU.mult), a2, t_rope[t])
            q4 = QK[:, :].rearrange("p (s h d) -> p s h d", s=2, d=16)
            o4 = QS[:, :].rearrange("p (s h d) -> p s h d", s=2, d=16)
            r4 = QR[:, :].rearrange("p (s h d) -> p s h d", s=2, d=16)
            for lo_ in (0, 8):
                for s_ in range(2):
                    pq = pool.op(lambda e, lo_=lo_, s_=s_: e.tensor_tensor(
                        o4[:, s_, :, lo_:lo_ + 8], q4[:, s_, :, 8 - lo_:16 - lo_],
                        ST[:, tt, s_, lo_:lo_ + 8].unsqueeze(1).to_broadcast([128, 16, 8]), ALU.mult), d, t_tab)
            for s_ in range(2):
                dc = dve.op(lambda e, s_=s_: e.tensor_tensor(
                    r4[:, s_], q4[:, s_], CT[:, tt, s_, :].unsqueeze(1).to_broadcast([128, 16, 16]), ALU.mult), d, *f3)
            held[t] = (s1, s2, s3, dc, pq)

        def rotated(t):
            tt = t % 2
            s1, s2, s3, dc, pq = held[t]
            QS, QR = s2.parts[0], s3.parts[0]
            dr = dve.op(lambda e: e.tensor_tensor(QR[:, :], QR[:, :], QS[:, :], ALU.add), dc, pq)
            s1.free = (dc, pq)
            s2.free = (dr,)
            t_vk[t] = dve.op(lambda e: e.tensor_scalar(
                vk4[:, t, :, 16:32], QR[:, 256:512].rearrange("p (h d) -> p h d", d=16),
                gq[:, t:t + 1], None, ALU.mult), dr, held[("g", t // 2)])
            held[t] = (s3, dr)

        def turned_qk(t):
            s3, dr = held[t]
            QR = s3.parts[0]
            bs, fr = ring4.take()
            b = bs.parts[0]
            for c in range(4):
                p = pe.op(lambda e, c=c: e.transpose(b[:, c * 128:(c + 1) * 128], QR[:, c * 128:(c + 1) * 128], ident),
                          dr, *fr, signal=c == 3)
            t_qkt[t] = act.op(lambda e: e.copy(QKT[:, :, t * 128:(t + 1) * 128],
                                               b[:, :].rearrange("p (c n) -> p c n", c=4)), p)
            bs.free = (t_qkt[t],)
            s3.free = (p, t_vk[t])

        first_norm(0)
        w0h, w0l, t_w0 = chunk("qkv0")
        w1h, w1l, t_w1 = chunk("qkv1")
        cosv = sm_("cos").rearrange("p (t d) -> p t d", t=2)
        sinv = sm_("sin").rearrange("p (t d) -> p t d", t=2)
        for s_, f_, nm in ((0, 0.25, "qs"), (1, 1.0, "ks")):
            sc = sm_(nm)
            full = sc.unsqueeze(1).to_broadcast([128, 2, 16])
            lowb = sc[:, 0:8].unsqueeze(1).to_broadcast([128, 2, 8])
            highb = sc[:, 8:16].unsqueeze(1).to_broadcast([128, 2, 8])
            dve.op(lambda e, s_=s_, f_=f_, full=full: e.scalar_tensor_tensor(
                out=CT[:, :, s_, :], in0=cosv, scalar=f_, in1=full, op0=ALU.mult, op1=ALU.mult), t_sm)
            dve.op(lambda e, s_=s_, f_=f_, highb=highb: e.scalar_tensor_tensor(
                out=ST[:, :, s_, 0:8], in0=sinv[:, :, 0:8], scalar=f_, in1=highb, op0=ALU.mult, op1=ALU.mult))
            t_tab = dve.op(lambda e, s_=s_, f_=f_, lowb=lowb: e.scalar_tensor_tensor(
                out=ST[:, :, s_, 8:16], in0=sinv[:, :, 8:16], scalar=f_, in1=lowb, op0=ALU.mult, op1=ALU.mult))
        fuse(0)
        fuse(1)
        first_turn(0)
        first_norm(1)
        nf = 2
        kbr = Ring([Slot(KB[0])])
        kb_now = {}

        def make_kb(b, g):
            s, fr = kbr.take()
            for h in range(8):
                eng = dve if h % 2 else pool
                tk = eng.op(lambda e, h=h, s=s: e.tensor_scalar(
                    s.parts[0][:, h, :], QKT[:, 2 + g, b * 256:(b + 1) * 256], sm_("mh")[:, h:h + 1], 0.0,
                    ALU.mult, ALU.add), t_qkt[2 * b], t_qkt[2 * b + 1], *fr)
                if h == 6:
                    tp = tk
            kb_now[(b, g)] = (s, (tp, tk))

        for b in range(5):
            for t in (2 * b, 2 * b + 1):
                if b < 4:
                    project(t)
                    for _ in range(2):
                        if nf < 16:
                            fuse(nf)
                            nf += 1
                    if t == 1:
                        first_turn(1)
                if b >= 1:
                    rotated(t - 2)
            if b >= 1:
                turned_qk(2 * b - 2)
                turned_qk(2 * b - 1)
            if b == 3:
                chunk_done("qkv0", project.last)
                chunk_done("qkv1", project.last)
            if b < 4:
                head_norms(b)
                rotate(2 * b)
                rotate(2 * b + 1)
            if b == 3:
                make_kb(0, 0)
                t_cb = act.op(lambda e: e.copy(identb[:, :], ident), t_sm)
                t_cb = act.op(lambda e: e.copy(mb0[:, :], masks[:, 0:512]), t_mk)
                t_cb = act.op(lambda e: e.copy(mb1[:, :], masks[:, 512:896]))
        ring_done(ring4, (4, 5, 6, 7))
        lq_end = (last_of(pe), last_of(act), last_of(dve), last_of(pool))
        lq.close()
        KB.append(sb("KB1", [128, 8, 256], ctx=l0))
        P0 = [sb(f"P0{i}", [128, 4, 128], ctx=l0) for i in range(2)]
        P1 = [sb(f"P1{i}", [128, 2, 256], ctx=l0) for i in range(3)]
        SS = [sb(f"SS{i}", [128, 512], ctx=l0) for i in range(2)]
        PT = [sb(f"PT{i}", [128, 512], ctx=l0) for i in range(3)]
        for b in P1:
            t_p1z = pool.op(lambda e, b=b: e.memset(b[:, :, 0:64], 0.0), *lq_end)
        rS, rT, rO, rM = bank_ring((0, 1, 2)), bank_ring((3, 4)), bank_ring((5, 6)), bank_ring((7,))
        pr0 = Ring([Slot(b) for b in P0])
        pr1 = Ring([Slot(b) for b in P1])
        ssr = Ring([Slot(b) for b in SS])
        ptr = Ring([Slot(b) for b in PT])
        for r in (pr0, pr1, ssr, ptr):
            for s in r.slots:
                s.free = lq_end
        mxr = Ring([Slot(mx[:, i, :]) for i in range(6)])
        rcr = Ring([Slot(rc[:, i, :], rg[:, i, :]) for i in range(4)])
        kbr.slots.append(Slot(KB[1]))
        kbr.slots[1].free = lq_end
        units = []
        for b in range(4):
            for g in range(2):
                for c in range(2):
                    units.append((b, g, 0, 4 * c, 4))
                for c in range(4):
                    units.append((b, g, 1, 2 * c, 2))
        def scores(u):
            b, g, qt, h0, nh = u
            kb, tk = kb_now[(b, g)]
            s, fr = rS.take()
            bk = s.parts[0]
            n = 512 if qt == 0 else 384
            cols = slice(0, 128) if qt == 0 else slice(64, 256)
            pe.op(lambda e: e.matmul(bk[:, 0:n], QKT[:, g, b * 256 + qt * 128:b * 256 + qt * 128 + 128],
                                     kb.parts[0][:, h0:h0 + nh, cols], start=True, stop=False), *tk, *fr, signal=False)
            p = pe.op(lambda e: e.matmul(bk[:, 0:n], identb[:, :], (mb0 if qt == 0 else mb1)[:, :], start=False,
                                         stop=True), t_cb)
            if h0 + nh == 8 and qt == 1:
                kb.free = (p,)
            sm1, fm = mxr.take()
            m = sm1.parts[0]
            v = bk[:, 0:n].rearrange("p (h k) -> p h k", h=nh)
            d1 = dve.op(lambda e: e.tensor_reduce(m[:, 0:nh], v, AX_X, ALU.max), p, *fm)
            s2, f2 = ssr.take()
            d2 = dve.op(lambda e: e.tensor_tensor(s2.parts[0][:, 0:n].rearrange("p (h k) -> p h k", h=nh), v,
                                                  m[:, 0:nh].unsqueeze(2).to_broadcast([128, nh, n // nh]),
                                                  ALU.subtract), d1, *f2)
            s.free = (d2,)
            sm1.free = (d2,)
            s3, f3 = (pr0 if qt == 0 else pr1).take()
            dst = s3.parts[0][:, :, :] if qt == 0 else s3.parts[0][:, :, 64:256]
            a = act.op(lambda e: e.activation(dst, s2.parts[0][:, 0:n].rearrange("p (h k) -> p h k", h=nh), ACT.Exp),
                       d2, *f3)
            s2.free = (a,)
            return s3, a

        def turns(u, s3, a):
            b, g, qt, h0, nh = u
            s, fr = rT.take()
            bk = s.parts[0]
            pf = s3.parts[0][:, :, :].rearrange("p h k -> p (h k)")
            for c in range(4):
                p = pe.op(lambda e, c=c: e.transpose(bk[:, c * 128:(c + 1) * 128], pf[:, c * 128:(c + 1) * 128], ident),
                          a, t_p1z, *fr, signal=c == 3)
            s3.free = (p,)
            s4, f4 = ptr.take()
            a = act.op(lambda e: e.copy(s4.parts[0][:, :], bk[:, :]), p, *f4)
            s.free = (a,)
            return s4, a

        obank = {}

        def weigh(u, s4, a):
            b, g, qt, h0, nh = u
            t = 2 * b + qt
            if h0 == 0:
                obank[(b, g, qt)] = rO.take()
            so, fo = obank[(b, g, qt)]
            bk = so.parts[0]
            for i in range(nh):
                h = h0 + i
                o = bk[:, h * 33:(h + 1) * 33]
                H = 8 * g + h
                if qt == 0:
                    p = pe.op(lambda e, o=o, i=i, H=H: e.matmul(o, s4.parts[0][:, i * 128:(i + 1) * 128], vk4[:, t, H, :],
                              start=True, stop=True), a, t_v[t], t_ones, t_vk[t], *fo, signal=i == nh - 1)
                else:
                    for k in range(2):
                        p = pe.op(lambda e, o=o, i=i, k=k, H=H: e.matmul(
                            o, s4.parts[0][:, (2 * i + k) * 128:(2 * i + k + 1) * 128], vk4[:, t - 1 + k, H, :],
                            start=k == 0, stop=k == 1), a, t_v[t], t_ones, t_vk[t], *fo,
                            signal=i == nh - 1 and k == 1)
            s4.free = (p,)
            if h0 + nh < 8:
                return
            o3 = bk[:, 0:264].rearrange("p (h e) -> p h e", h=8)
            sr, fr = rcr.take()
            c1, c2 = sr.parts
            d = dve.op(lambda e: e.reciprocal(c1, o3[:, :, 32]), p, *fr)
            d1 = dve.op(lambda e: e.tensor_scalar(c2, c1, sm_("dq")[:, qt:qt + 1], None, ALU.mult), d)
            hd = slice(g * 128, g * 128 + 128)
            d2 = dve.op(lambda e: e.tensor_tensor(AO[:, t, hd].rearrange("p (h d) -> p h d", d=16), o3[:, :, 0:16],
                                                  c1.unsqueeze(2).to_broadcast([128, 8, 16]), ALU.mult))
            d3 = dve.op(lambda e: e.tensor_tensor(NB[:, t, hd].rearrange("p (h d) -> p h d", d=16), o3[:, :, 16:32],
                                                  c2.unsqueeze(2).to_broadcast([128, 8, 16]), ALU.mult), d1, t_h[1])
            so.free = (d3,)
            sr.free = (d3,)
            t_ao[t] = d3

        t_ao = [None] * NT
        t_qm, t_at, t_ow = [None, None], [None, None], [None] * NT

        def o_project(t, ring):
            hi, lo, tw = chunk("wo")
            s, fr = ring.take()
            b = s.parts[0]
            ts_ = slice(t * 128, (t + 1) * 128)
            p = mm3(b[:, 0:256], [((BT[0][:, k, ts_], BT[1][:, k, ts_]), (hi[:, k * 256:k * 256 + 256], lo[:, k * 256:k * 256 + 256]))
                                  for k in range(2)], tw, t_at[t // 4], *fr)
            t_ow[t] = act.op(lambda e: e.copy(AO[:, t, :], b[:, 0:256]), p)
            s.free = (t_ow[t],)
            if t == NT - 1:
                chunk_done("wo", p)

        def turn_qm(half, ring, ks=(0, 1)):
            t_qm[half] = turn(NB, AT, ring, half, t_ao[half * 4:half * 4 + 4], ks=ks)

        def turn_at(half, ring, ks=(0, 1)):
            t_at[half] = turn(AO, BT, ring, half, t_ao[half * 4:half * 4 + 4], ks=ks)

        fill = {29: lambda: turn_qm(0, rM, (0,)), 31: lambda: turn_qm(0, rM, (1,)),
                33: lambda: turn_at(0, rM, (0,)), 35: lambda: turn_at(0, rM, (1,))}
        for t in range(4):
            fill[37 + 2 * t] = lambda t=t: o_project(t, rM)
        s_out_, t_out_ = {}, {}
        n = len(units)
        for i in range(n + 3):
            if 0 <= i - 2 < n:
                t_out_[i - 2] = turns(units[i - 2], *s_out_[i - 2])
            if i < n:
                if i % 6 == 3 and i // 6 + 1 < 8:
                    j = i // 6 + 1
                    make_kb(j // 2, j % 2)
                s_out_[i] = scores(units[i])
            if 0 <= i - 3 < n:
                weigh(units[i - 3], *t_out_[i - 3])
            if i in fill:
                fill[i]()
        ring_done(rS, (0, 1, 2))
        ring_done(rT, (3, 4))
        ring_done(rO, (5, 6))
        ring_done(rM, (7,))
        l0_end = (last_of(pe), last_of(act), last_of(dve), last_of(pool))
        l0.close()

        top = sb("top", [128, NT, 8])
        e2 = sb("e2", [128, 4, NT])
        pr = sb("pr", [128, NT, 24])
        rp = sb("rp", [128, NT, 24])
        tp8 = sb("tp8", [128, NT, 8])
        nm = sb("nm", [128, 4, NT])
        chr_ = sb("chr", [128, NT, 16], R32)
        cl = sb("cl", [128, NT, 32])
        mlp = ExitStack()
        T1 = [sb(f"T1{i}", [128, 512], ctx=mlp) for i in range(2)]
        T2 = [sb(f"T2{i}", [128, 512], ctx=mlp) for i in range(2)]
        HH = [(sb(f"HHh{i}", [128, 512], R32, ctx=mlp), sb(f"HHl{i}", [128, 512], R32, ctx=mlp)) for i in range(3)]
        t1r = Ring([Slot(b) for b in T1])
        t2r = Ring([Slot(b) for b in T2])
        hr = Ring([Slot(*b) for b in HH])
        for r in (t1r, t2r, hr):
            for s in r.slots:
                s.free = l0_end
        more_slots([(sb(f"xh{i}", [128, SLOT], R32, ctx=mlp), sb(f"xl{i}", [128, SLOT], R32, ctx=mlp)) for i in range(NMORE)],
                   "down", l0_end)

        def run_mlp(names, gated, ring, xin, ready, before=(), after=lambda half: (), combine=None, lag=LAG, wait_for=1, at={}):
            n = len(names)
            yfree = [bank_free[i] for i in range(4)]
            pend, pieces, tail = [], list(before), {}
            ytok = [None] * NT

            def down(j, half, hslot, th):
                hi, lo, _ = chunk(names[j])
                o = 512 if gated else 256
                for c in range(4):
                    t = half * 4 + c
                    tk = mm3(ybank(t), [((hslot.parts[0][:, c * 128:(c + 1) * 128], hslot.parts[1][:, c * 128:(c + 1) * 128]),
                                         (hi[:, o:o + 256], lo[:, o:o + 256]))], th, *(yfree[t // 2] if j == 0 else ()),
                             first=(j == 0 and t % 2 == 0), last=j == n - 1, skip=True, signal=c == 3 or j == n - 1)
                    ytok[t] = tk
                hslot.free = (tk,)
                if half == 1:
                    chunk_done(names[j], tk)
                if j == n - 1:
                    tail[half] = list(after(half, ytok))
                    if half == 0:
                        pieces.extend(tail[0])

            def step(j, half):
                hi, lo, tw = chunk(names[j])
                sl = slice(half * 512, half * 512 + 512)
                xs = [(xin[0][:, k, sl], xin[1][:, k, sl]) for k in range(2)]
                got = []
                cc = combine is not None and j >= 3
                for part in range(2 if gated else 1):
                    sg, fg = ring.take()
                    o = part * 256
                    pg = mm3(sg.parts[0][:, :], [((hi[:, o + k * 128:o + k * 128 + 128], lo[:, o + k * 128:o + k * 128 + 128]),
                                                  xs[k]) for k in range(2)], tw, ready[half], *fg)
                    got.append((sg, pg))
                if cc:
                    sc, fc = ring.take()
                    pc = combine(sc.parts[0], j - 3, sl, *fc)
                s1, f1 = t1r.take()
                s2, f2 = t2r.take()
                A, B = s1.parts[0], s2.parts[0]
                sg, pg = got[0]
                g = sg.parts[0]
                a = act.op(lambda e: e.activation(A[:, :], g[:, :], ACT.Silu), pg, *f1)
                sg.free = (a,)
                if gated:
                    su, pu = got[1]
                    u = su.parts[0]
                    d = dve.op(lambda e: e.tensor_tensor(B[:, :], A[:, :], u[:, :], ALU.mult), a, pu, *f2)
                    su.free = (d,)
                    s1.free = (d,)
                    if cc:
                        d = dve.op(lambda e, c=sc.parts[0]: e.tensor_tensor(B[:, :], B[:, :], c[:, :], ALU.mult), d, pc)
                        sc.free = (d,)
                else:
                    d = dve.op(lambda e: e.scalar_tensor_tensor(out=B[:, :], in0=A[:, :], scalar=1.0, in1=A[:, :],
                                                                op0=ALU.add, op1=ALU.mult), a, *f2)
                    s1.free = (d,)
                s3, f3 = hr.take()
                th = split_from(s3.parts[0][:, :], s3.parts[1][:, :], B[:, :], d, *f3)
                s2.free = (th,)
                pend.append((j, half, s3, th))

            order = []
            for j in range(n + lag):
                if j < n:
                    order.append((j, 0))
                if j >= lag:
                    order.append((j - lag, 1))
            for i, (j, half) in enumerate(order):
                if (j, half) == (0, 1):
                    while pieces:
                        pieces.pop(0)()
                step(j, half)
                if len(pend) > wait_for:
                    down(*pend.pop(0))
                if (j, half) in at:
                    at[(j, half)]()
                if pieces:
                    pieces.pop(0)()
            while pend:
                down(*pend.pop(0))
            for f in pieces:
                f()
            return tail[1]

        def ybank(t):
            return banks[t // 2][:, (t % 2) * 256:(t % 2) * 256 + 256]

        ring4 = bank_ring((4, 5, 6, 7))
        second_half = [lambda: turn_qm(1, ring4), lambda: turn_at(1, ring4)] + [
            lambda t=t: (o_project(t, ring4), o_project(t + 1, ring4)) for t in (4, 6)]

        t_x1, t_xo, t_x, t_x2 = [None] * NT, [None] * NT, [None] * NT, [None] * NT
        t_hf, t_hm = [None, None], [None, None]

        def after_mem(half, y):
            def one(t):
                s1, f1 = t1r.take()
                A = s1.parts[0]
                a = act.op(lambda e: e.activation(A[:, 0:256], ybank(t), ACT.Tanh, scale=0.5), y[t | 1], *f1)
                bank_free[t // 2] = (a,)
                d = dve.op(lambda e: e.scalar_tensor_tensor(out=A[:, 0:256], in0=A[:, 0:256], scalar=1.0,
                           in1=AO[:, t, :], op0=ALU.add, op1=ALU.mult), a, t_ow[t])
                d = dve.op(lambda e: e.scalar_tensor_tensor(out=X1[:, t, :], in0=A[:, 0:256], scalar=0.5,
                           in1=X1[:, t, :], op0=ALU.mult, op1=ALU.add), d)
                s1.free = (d,)
                t_x1[t] = d

            def pair(c):
                one(half * 4 + c)
                one(half * 4 + c + 1)

            def norm():
                hs = slice(half * 4, half * 4 + 4)
                a = tilemean(X1, half, t_x1[half * 4:half * 4 + 4])
                a = dve.op(lambda e: e.tensor_tensor(v2[:, hs], mv[:, hs, 0], mv[:, hs, 0], ALU.mult), a)
                a = dve.op(lambda e: e.scalar_tensor_tensor(out=v2[:, hs], in0=v2[:, hs], scalar=1e-6,
                           in1=mv[:, hs, 1], op0=ALU.add, op1=ALU.add), a)
                norm.p = rsqrt_small(r2[:, hs], v2[:, hs], a)

            def scaled():
                norm.rd = [dve.op(lambda e, t=t: e.tensor_scalar(NB[:, t, :], X1[:, t, :], r2[:, t:t + 1], None, ALU.mult),
                                  norm.p, t_qm[1]) for t in range(half * 4, half * 4 + 4)]

            def turned():
                for t in range(half * 4, half * 4 + 4):
                    t_xo[t] = pool.op(lambda e, t=t: e.tensor_tensor(XO[:, t, :], XO[:, t, :], X1[:, t, :], ALU.add),
                                      t_x1[t])
                t_hf[half] = turn(NB, BT, ring4, half, norm.rd, scale=sm_("nw")[:, 2:4])

            return [lambda: pair(0), lambda: pair(2), norm, scaled, turned]

        rest = run_mlp([f"mem{j}" for j in range(8)], False, ring4, AT, t_qm, before=second_half, after=after_mem,
                       wait_for=2)

        t_hn = [None, None]

        def after_ffn(half, y):
            def add():
                for t in range(half * 4, half * 4 + 4):
                    t_x[t] = dve.op(lambda e, t=t: e.tensor_tensor(XO[:, t, :], XO[:, t, :], ybank(t), ALU.add),
                                    y[t | 1], t_xo[t])
                    bank_free[t // 2] = (t_x[t],)

            def mean():
                mean.a = tilemean(XO, half, t_x[half * 4:half * 4 + 4])

            def rstd():
                rstd.p = layernorm_rstd(half, mean.a)

            def norm():
                norm.rd = layernorm_apply(XO, NB, half, rstd.p, free=(t_hf[half],))

            def turned():
                t_hn[half] = turn(NB, AT, ring4, half, norm.rd)

            if half == 1:
                return [add, lambda: (mean(), rstd()), norm, turned]
            return [lambda: (add(), mean(), rstd()), norm, turned] + [lambda: up(0), lambda: expert(0), lambda: ffn_down(0)]


        t_r = [None, None]
        lg = [None] * NT
        t_rw = [None] * NT
        t_hl = [None, None]

        def up(half):
            hi, lo, tw = chunk("up")
            sl = slice(half * 512, half * 512 + 512)
            for m in range(2):
                s, fr = ring4.take()
                b = s.parts[0]
                p = mm3(b[:, :], [((hi[:, m * 256 + k * 128:m * 256 + k * 128 + 128], lo[:, m * 256 + k * 128:m * 256 + k * 128 + 128]),
                                   (AT[0][:, k, sl], AT[1][:, k, sl])) for k in range(2)], tw, t_hn[half], *fr)
                a = act.op(lambda e, b=b, m=m: e.activation(BT[0][:, m, sl], b[:, :], ACT.Relu), p)
                d = dve.op(lambda e, b=b, m=m: e.scalar_tensor_tensor(
                    out=BT[1][:, m, sl], in0=b[:, :], scalar=0.0, in1=BT[0][:, m, sl].bitcast(F32), op0=ALU.max,
                    op1=ALU.subtract), a)
                s.free = (d,)
            t_r[half] = d
            if half == 1:
                chunk_done("up", p)

        def expert(half):
            hi, lo, tw = chunk("exp")
            for t in range(half * 4, half * 4 + 4):
                s, fr = ring4.take()
                b = s.parts[0]
                ts_ = slice(t * 128, (t + 1) * 128)
                p = mm3(b[:, 0:264], [((AT[0][:, k, ts_], AT[1][:, k, ts_]), (hi[:, k * 264:k * 264 + 264], lo[:, k * 264:k * 264 + 264]))
                                      for k in range(2)], tw, t_hn[half], *fr)
                d = dve.op(lambda e, b=b, t=t: e.max(top[:, t, :], b[:, 256:264]), p)
                lg[t] = act.op(lambda e, b=b, t=t: e.copy(AO[:, t, :], b[:, 0:256]), d)
                s.free = (lg[t],)
            if half == 1:
                chunk_done("exp", p)
            h = slice(half * 4, half * 4 + 4)
            d = dve.op(lambda e: e.tensor_tensor(e2[:, 0, h], top[:, h, 1], top[:, h, 0], ALU.subtract), d)
            a = act.op(lambda e: e.activation(e2[:, 1, h], e2[:, 0, h], ACT.Exp), d)
            d = dve.op(lambda e: e.tensor_scalar(e2[:, 2, h], e2[:, 1, h], 1.0, None, ALU.add), a)
            d = dve.op(lambda e: e.reciprocal(e2[:, 3, h], e2[:, 2, h]), d)
            d = dve.op(lambda e: e.tensor_tensor(e2[:, 2, h], e2[:, 1, h], e2[:, 3, h], ALU.mult), d)
            d = dve.op(lambda e: e.tensor_tensor(e2[:, 0, h], e2[:, 2, h], e2[:, 3, h], ALU.add), d)
            for t in range(half * 4, half * 4 + 4):
                p = pool.op(lambda e, t=t: e.tensor_scalar(AO[:, t, :], AO[:, t, :], e2[:, 0, t:t + 1], 1.0, ALU.mult,
                                                           ALU.mult), d, lg[t])
                t_rw[t] = pool.op(lambda e, t=t: e.tensor_tensor(XO[:, t, :], XO[:, t, :], AO[:, t, :], ALU.add), p, t_x[t])

        def ffn_down(half):
            hi, lo, tw = chunk("down")
            for t in range(half * 4, half * 4 + 4):
                s, fr = ring4.take()
                b = s.parts[0]
                ts_ = slice(t * 128, (t + 1) * 128)
                p = mm3(b[:, 0:256], [((BT[0][:, k, ts_], BT[1][:, k, ts_]), (hi[:, k * 256:k * 256 + 256], lo[:, k * 256:k * 256 + 256]))
                                      for k in range(2)], tw, t_r[half], *fr)
                d = dve.op(lambda e, b=b, t=t: e.tensor_tensor(XO[:, t, :], XO[:, t, :], b[:, 0:256], ALU.add), p, t_rw[t])
                s.free = (d,)
                ffn_down.mean = tilemean(XO, half, [d] * 4, (t % 4,))
            if half == 1:
                chunk_done("down", p)

        rest = run_mlp([f"ffn{j}" for j in range(6)], True, ring4, BT, t_hf, before=rest, after=after_ffn)
        rd_l = [layernorm_rstd(0, ffn_down.mean), None]
        rest[0]()
        rd_l[0] = layernorm_apply(XO, NB, 0, rd_l[0], free=(t_hn[0],))
        t_hl[0] = turn(NB, AT, ring4, 0, rd_l[0])
        mlp_end = (last_of(pe), last_of(act), last_of(dve), last_of(pool))
        mlp.close()

        l1 = ExitStack()
        QH = [(sb(f"QHh{i}", [128, 8, 256], R32, ctx=l1), sb(f"QHl{i}", [128, 8, 256], R32, ctx=l1)) for i in range(2)]
        UT = (sb("UTh", [128, 4, 256], R32, ctx=l1), sb("UTl", [128, 4, 256], R32, ctx=l1))
        CD = (sb("CDh", [128, T], R32, ctx=l1), sb("CDl", [128, T], R32, ctx=l1))
        x1f = X1[:, :, :].rearrange("p t d -> p (t d)")
        aof = AO[:, :, :].rearrange("p t d -> p (t d)")
        CF = x1f[:, 0:1024]
        CN = x1f[:, 1024:1536].rearrange("p (t c) -> p t c", t=NT)
        rr = sb("rr", [128, NT, 16], ctx=l1)
        rrs = sb("rrs", [128, NT, 16], ctx=l1)
        PB = [sb(f"PB{i}", [128, 4, 256], ctx=l1) for i in range(3)]
        PN = [aof[:, i * 512:i * 512 + 512] for i in range(4)]
        sml = sb("sml", [128, 4, 20], ctx=l1)

        cb = sm_("cb")
        t_c, t_cq, t_cn, t_rr = [None, None], [None, None], [None, None], [None, None]
        SC = float(1.0 / np.sqrt(128.0))

        def latent(half, m, ring):
            hi, lo, tw = chunk("proj")
            sl = slice(half * 512, half * 512 + 512)
            s, fr = ring.take()
            b = s.parts[0]
            p = mm3(b[:, :], [((hi[:, k * 384 + m * 128:k * 384 + m * 128 + 128], lo[:, k * 384 + m * 128:k * 384 + m * 128 + 128]),
                               (AT[0][:, k, sl], AT[1][:, k, sl])) for k in range(2)], tw, t_hl[half], *fr)
            ho, lo2 = (CD[0][:, sl], CD[1][:, sl]) if m == 0 else (BT[0][:, m - 1, sl], BT[1][:, m - 1, sl])
            a = act.op(lambda e: e.activation(ho, b[:, :], ACT.Identity, bias=cb[:, m:m + 1]), p, *mlp_end)
            d = dve.op(lambda e: e.scalar_tensor_tensor(
                out=lo2, in0=b[:, :], scalar=cb[:, m:m + 1], in1=ho.bitcast(F32), op0=ALU.add, op1=ALU.subtract), a)
            if m == 0:
                d = dve.op(lambda e: e.tensor_scalar(CF[:, sl], b[:, :], cb[:, 0:1], None, ALU.add))
                t_c[half] = d
            s.free = (d,)
            t_cq[half] = d
            if half == 1 and m == 2:
                chunk_done("proj", p)

        def latent_rest(half, ring):
            s, fr = ring.take()
            b = s.parts[0]
            for c in range(4):
                p = pe.op(lambda e, c=c: e.transpose(b[:, c * 64:c * 64 + 64],
                          CF[0:64, half * 512 + c * 128:half * 512 + (c + 1) * 128], ident[0:64, 0:64]), t_c[half], *fr)
            hs = slice(half * 4, half * 4 + 4)
            for c in range(4):
                t = half * 4 + c
                ts_ = slice(t * 128, (t + 1) * 128)
                p = mm3(b[:, 256 + c * 16:256 + (c + 1) * 16], [((BT[0][:, k, ts_], BT[1][:, k, ts_]),
                        (RTW[0][:, k, :], RTW[1][:, k, :])) for k in range(2)], t_cq[half], fuse.done)
            t_cn[half] = act.op(lambda e: e.copy(CN[:, hs, :], b[:, 0:256].rearrange("p (t c) -> p t c", c=64)), p)
            a = dve.op(lambda e: e.tensor_copy(rr[:, hs, :], b[:, 256:320].rearrange("p (t h) -> p t h", h=16)), t_cn[half])
            t_rr[half] = dve.op(lambda e: e.tensor_scalar(rrs[:, hs, :], rr[:, hs, :], SC, None, ALU.mult), a)
            s.free = (a,)

        rS = bank_ring((0, 1, 2, 3))
        pbr = Ring([Slot(b) for b in PB])
        pnr = Ring([Slot(b) for b in PN])
        smr = Ring([Slot(sml[:, i, :]) for i in range(4)])
        qhr = Ring([Slot(*q) for q in QH])
        for r in (pbr, smr, qhr):
            for s in r.slots:
                s.free = mlp_end
        qh = {}
        tq = {}

        def latent_q(b, j2, ring=None):
            if j2 == 0:
                qh[b] = qhr.take()
            sq, fq = qh[b]
            s, fr = (ring or rM).take()
            bk = s.parts[0]
            bs_ = slice(b * 256, b * 256 + 256)
            for i in range(2):
                j = 2 * j2 + i
                p = mm3(bk[:, i * 256:i * 256 + 256], [((MTW[0][:, k, j * 128:j * 128 + 128], MTW[1][:, k, j * 128:j * 128 + 128]),
                        (BT[0][:, k, bs_], BT[1][:, k, bs_])) for k in range(2)], t_cq[b // 2], fuse.done, *fr)
            t = split_from(sq.parts[0][:, 2 * j2:2 * j2 + 2, :].rearrange("p j n -> p (j n)"),
                           sq.parts[1][:, 2 * j2:2 * j2 + 2, :].rearrange("p j n -> p (j n)"), bk[:, :], p, *fq)
            s.free = (t,)
            tq[(b, j2)] = t

        def l1_scores(b, j):
            sq, _ = qh[b]
            got = []
            for i in range(2):
                o = 64 * i
                s, fr = rS.take()
                bk = s.parts[0]
                kv = [c[o:o + 64, b * 256:b * 256 + 256] for c in CD]
                for qt in range(2):
                    p = mm3(bk[:, qt * 256:qt * 256 + 256], [(tuple(q[o:o + 64, j, qt * 128:qt * 128 + 128] for q in sq.parts), kv)],
                            tq[(b, j // 2)], t_c[b // 2], *fr)
                got.append((s, bk[:, :].rearrange("p (q k) -> p q k", q=2), p))
            if j == 7:
                sq.free = (p,)
            return got

        def l1_exp(b, j, got):
            ss, fs = smr.take()
            m = ss.parts[0]
            m4 = lambda c: m[:, 4 * c:4 * c + 4]
            for i, (_, v, p) in enumerate(got):
                d = dve.op(lambda e, i=i, v=v: e.tensor_reduce(m[:, 2 * i:2 * i + 2], v, AX_X, ALU.max), p, *fs)
            rv, rsv = (a[:, 2 * b:2 * b + 2, 2 * j:2 * j + 2].rearrange("p t h -> p h t") for a in (rr, rrs))
            m3 = lambda c: m4(c).rearrange("p (h t) -> p h t", h=2)
            d = dve.op(lambda e: e.tensor_tensor(m3(1), m3(0), rv, ALU.add), d, t_rr[b // 2])
            d = dve.op(lambda e: e.scalar_tensor_tensor(out=m3(2), in0=m3(1), scalar=-SC, in1=rsv, op0=ALU.mult,
                                                        op1=ALU.add), d)
            sp_, fp = pbr.take()
            P = sp_.parts[0]
            for i, (s, v, _) in enumerate(got):
                for qt in range(2):
                    c = 2 * i + qt
                    a = act.op(lambda e, c=c, qt=qt, v=v: e.activation(P[:, c, :], v[:, qt, :], ACT.Exp, bias=m[:, 8 + c:9 + c],
                                                                       scale=SC, accum_out=m[:, 12 + c:13 + c]), d, *fp)
                s.free = (a,)
            return ss, sp_, a

        def l1_norm(ss, sp_, a):
            m, P = ss.parts[0], sp_.parts[0]
            d = dve.op(lambda e: e.reciprocal(m[:, 16:20], m[:, 12:16]), a)
            ready = []
            for c in range(4):
                t = pool.op(lambda e, c=c: e.tensor_scalar(P[:, c, :], P[:, c, :], m[:, 16 + c:17 + c], 1.0, ALU.mult,
                                                           ALU.mult), d)
                if c % 2:
                    ready.append(t)
            ss.free = (t,)
            return sp_, ready

        def l1_turns(b, j, sp_, ready):
            P = sp_.parts[0]
            got = []
            for i in range(2):
                s, fr = rT.take()
                bk = s.parts[0]
                for kc in range(2):
                    for qt in range(2):
                        p = pe.op(lambda e, kc=kc, qt=qt, bk=bk, i=i: e.transpose(
                            bk[:, kc * 256 + qt * 128:kc * 256 + qt * 128 + 128],
                            P[:, 2 * i + qt, kc * 128:kc * 128 + 128], ident), ready[i], *fr, signal=kc == 1 and qt == 1)
                s4, f4 = pnr.take()
                a = act.op(lambda e, s4=s4, bk=bk: e.copy(s4.parts[0], bk[:, :]), p, *f4)
                s.free = (a,)
                got.append((s4, a))
            sp_.free = (p,)
            return got

        def l1_weigh(b, j, got):
            s, fr = rU.take()
            bk = s.parts[0]
            for i, (s4, a) in enumerate(got):
                o = 64 * i
                for kc in range(2):
                    p = pe.op(lambda e, kc=kc, o=o, s4=s4: e.matmul(bk[o:o + 64, :], CN[:, 2 * b + kc, :],
                              s4.parts[0][:, kc * 256:kc * 256 + 256], start=kc == 0, stop=kc == 1),
                              a, t_cn[b // 2], *fr, signal=kc == 1)
                s4.free = (p,)
            return s, p

        def l1_keep_hi(s, p):
            su, fr = utr.take()
            return s, su, act.op(lambda e: e.copy(su.parts[0], s.parts[0]), p, *fr)

        def l1_keep_lo(s, su, a):
            s.free = (dve.op(lambda e: e.tensor_tensor(su.parts[1], s.parts[0], su.parts[0].bitcast(F32), ALU.subtract), a),)
            return su, s.free[0]

        t_x3 = [None] * NT

        def l1_out(b, j, su, ready):
            for qt in range(2):
                qs_ = slice(qt * 128, qt * 128 + 128)
                p = mm3(banks[7][:, qt * 256:qt * 256 + 256], [((su.parts[0][:, qs_], su.parts[1][:, qs_]),
                        (NTW[0][:, j, :], NTW[1][:, j, :]))], ready, *(bank_free[7] if j == 0 else ()),
                        first=j == 0 and qt == 0, last=j == 7, skip=True)
            su.free = (p,)
            return p

        def l1_add(b, p):
            v = XO[:, 2 * b:2 * b + 2, :]
            d = dve.op(lambda e: e.tensor_tensor(v, v, banks[7][:, :].rearrange("p (t n) -> p t n", t=2), ALU.add), p)
            bank_free[7] = (d,)
            t_x3[2 * b] = t_x3[2 * b + 1] = dve.op(lambda e: e.tensor_tensor(
                v, v, bout[:, :].unsqueeze(1).to_broadcast([128, 2, 256]), ALU.add), d, fuse.bias)

        t_h4 = [None, None]
        rd4 = [None, None]

        def last_norm(half):
            rd4[half] = layernorm(XO, NB, half, t_x3[half * 4:half * 4 + 4], free=(t_hl[half],),
                                  tiles=(2, 3) if half else (0, 1, 2, 3))

        def last_turn(half, ring):
            t_h4[half] = turn(NB, AT, ring, half, rd4[half], free=(t_cq[1],))

        t_pad = dve.op(lambda e: e.memset(pr[:, :, 16:24], -1.0), *mlp_end)
        gates = {}

        def gate(half, ring):
            hi, lo, tw = chunk("gate")
            s, fr = ring.take()
            for c in range(4):
                ts_ = slice((half * 4 + c) * 128, (half * 4 + c + 1) * 128)
                p = mm3(s.parts[0][:, c * 16:(c + 1) * 16], [((AT[0][:, k, ts_], AT[1][:, k, ts_]),
                        (hi[:, k * 16:k * 16 + 16], lo[:, k * 16:k * 16 + 16])) for k in range(2)], tw, t_h4[half], *fr)
            if half == 1:
                chunk_done("gate", p)
            g3 = s.parts[0][:, 0:64].rearrange("p (t h) -> p t h", h=16)
            hs = slice(half * 4, half * 4 + 4)
            d = dve.op(lambda e: e.tensor_reduce(nm[:, 0, hs], g3, AX_X, ALU.max), p)
            d = dve.op(lambda e: e.tensor_tensor(pr[:, hs, 0:16], g3, nm[:, 0, hs].unsqueeze(2).to_broadcast([128, 4, 16]),
                                                 ALU.subtract), d)
            s.free = (d,)
            gates[half] = act.op(lambda e: e.activation(pr[:, hs, 0:16], pr[:, hs, 0:16], ACT.Exp), d)

        def route(half):
            hs = slice(half * 4, half * 4 + 4)
            d = dve.op(lambda e: e.tensor_reduce(nm[:, 1, hs], pr[:, hs, 0:16], AX_X, ALU.add), gates[half])
            d = dve.op(lambda e: e.reciprocal(nm[:, 2, hs], nm[:, 1, hs]), d)
            d = dve.op(lambda e: e.tensor_tensor(pr[:, hs, 0:16], pr[:, hs, 0:16],
                                                 nm[:, 2, hs].unsqueeze(2).to_broadcast([128, 4, 16]), ALU.mult), d)
            for t in range(half * 4, half * 4 + 4):
                m = dve.op(lambda e, t=t: e.max(tp8[:, t, :], pr[:, t, 0:16]), d)
            d = dve.op(lambda e: e.memset(tp8[:, hs, 6:8], -1.0), m)
            for t in range(half * 4, half * 4 + 4):
                m = dve.op(lambda e, t=t: e.match_replace(rp[:, t, :], tp8[:, t, :], pr[:, t, :], -2.0), d, t_pad)
            d = dve.op(lambda e: e.scalar_tensor_tensor(out=cl[:, hs, 16:32], in0=rp[:, hs, 0:16], scalar=0.0,
                                                        in1=pr[:, hs, 0:16], op0=ALU.is_lt, op1=ALU.mult), m)
            d = dve.op(lambda e: e.tensor_copy(chr_[:, hs, :], cl[:, hs, 16:32]), d)
            d = dve.op(lambda e: e.tensor_copy(cl[:, hs, 0:16], chr_[:, hs, :].bitcast(F32)), d)
            gates[half] = dve.op(lambda e: e.tensor_tensor(cl[:, hs, 16:32], cl[:, hs, 16:32], chr_[:, hs, :].bitcast(F32),
                                                           ALU.subtract), d)

        rest[1]()
        for m in range(3):
            latent(0, m, rS)
        rest[2]()
        latent_rest(0, rS)
        rest[3]()
        latent_q(0, 0, rS)
        up(1)

        def half1_norm():
            rd_l[1] = layernorm_apply(XO, NB, 1, layernorm_rstd(1, ffn_down.mean), free=(t_hn[1],))

        def turn1(k):
            s, fr = rM.take()
            bk = s.parts[0]
            for c in range(4):
                t = pe.op(lambda e, c=c: e.transpose(bk[:, c * 128:(c + 1) * 128], NB[:, 4 + c, k * 128:(k + 1) * 128],
                                                     ident), rd_l[1][c], *fr, signal=c == 3)
            t_hl[1] = split_from(AT[0][:, k, 512:1024], AT[1][:, k, 512:1024], bk[:, :], t)
            s.free = (t_hl[1],)

        fill = {(0, 1): [lambda: expert(1)], (0, 2): [lambda: latent_q(0, 1, ring4), lambda: ffn_down(1)],
                (0, 3): [half1_norm, lambda: latent_q(0, 2)], (0, 4): [], (0, 5): [lambda: latent_q(0, 3)],
                (0, 6): [lambda: turn1(0)], (0, 7): [lambda: turn1(1)], (1, 0): [lambda: latent(1, 0, rM)],
                (1, 1): [lambda: latent(1, 1, rM)], (1, 2): [lambda: latent(1, 2, rM)],
                (1, 3): [lambda: latent_rest(1, rM)],
                (2, 6): [lambda: last_norm(0)], (3, 0): [lambda: last_turn(0, rM)],
                (3, 2): [lambda: gate(0, rM)], (3, 3): [lambda: route(0)],
                (3, 6): [lambda: tilemean(XO, 1, t_x3[4:8], (0, 1))]}
        for b in range(3):
            for j2 in range(4):
                fill.setdefault((b, 4 + j2), []).append(lambda b=b, j2=j2: latent_q(b + 1, j2))
        us = [(b, j) for b in range(4) for j in range(8)]
        n1 = len(us)
        so_, to_ = {}, {}
        for i in range(n1 + 1):
            unit = lambda d: 0 <= i - d < n1
            if i == 3:
                ring_done(ring4, (4, 5, 6, 7))
                rT = rM = bank_ring((4, 5))
                rU = Ring([Slot(banks[6][:, 0:256])])
                rU.slots[0].free = bank_free[6]
                utr = Ring([Slot(UT[0][:, i, :], UT[1][:, i, :]) for i in range(4)])
                for s in utr.slots:
                    s.free = mlp_end
                for s in pnr.slots:
                    s.free = (t_rw[NT - 1],)
            if unit(3):
                to_[i - 3] = l1_turns(*us[i - 3], *so_[i - 3])
            if unit(5):
                to_[i - 5] = l1_keep_hi(*to_[i - 5])
            if unit(1):
                so_[i - 1] = l1_exp(*us[i - 1], so_[i - 1])
            if unit(2):
                so_[i - 2] = l1_norm(*so_[i - 2])
            if unit(5):
                to_[i - 5] = l1_keep_lo(*to_[i - 5])
            if unit(7) and us[i - 7][1] == 7:
                l1_add(us[i - 7][0], to_[i - 7])
            if unit(0):
                for f in fill.get(us[i], ()):
                    f()
                so_[i] = l1_scores(*us[i])
            if unit(4):
                to_[i - 4] = l1_weigh(*us[i - 4], to_[i - 4])
            if unit(6):
                to_[i - 6] = l1_out(*us[i - 6], *to_[i - 6])
        ring_done(rS, (0, 1, 2, 3))
        for i in (0, 1):
            rU.slots.append(Slot(banks[i][:, 0:256]))
            rU.slots[-1].free = bank_free[i]
        rU.at = 1

        def keep(k):
            to_[k] = l1_keep_lo(*l1_keep_hi(*to_[k]))

        def share(k):
            to_[k] = l1_out(*us[k], *to_[k])

        keep(n1 - 4)
        so_[n1 - 1] = l1_norm(*so_[n1 - 1])
        to_[n1 - 2] = l1_turns(*us[n1 - 2], *so_[n1 - 2])
        to_[n1 - 3] = l1_weigh(*us[n1 - 3], to_[n1 - 3])
        share(n1 - 5)
        keep(n1 - 3)
        to_[n1 - 2] = l1_weigh(*us[n1 - 2], to_[n1 - 2])
        share(n1 - 4)
        to_[n1 - 1] = l1_turns(*us[n1 - 1], *so_[n1 - 1])
        keep(n1 - 2)
        share(n1 - 3)
        to_[n1 - 1] = l1_weigh(*us[n1 - 1], to_[n1 - 1])
        share(n1 - 2)
        keep(n1 - 1)
        share(n1 - 1)
        l1_add(3, to_[n1 - 1])
        ring_done(rT, (4, 5))
        ring_done(rU, (6, 0, 1))
        l1_end = (last_of(pe), last_of(act), last_of(dve), last_of(pool))
        l1.close()

        m1 = ExitStack()
        T1 = [sb(f"U1{i}", [128, 512], ctx=m1) for i in range(2)]
        T2 = [sb(f"U2{i}", [128, 512], ctx=m1) for i in range(3)]
        HH = [(sb(f"VVh{i}", [128, 512], R32, ctx=m1), sb(f"VVl{i}", [128, 512], R32, ctx=m1)) for i in range(3)]
        SELf = sb("SELf", [32, 22 * 128], ctx=m1)
        SELr = sb("SELr", [32, 22 * 128], R32, ctx=m1)
        CTr = sb("CTr", [32, T], R32, ctx=m1)
        t1r = Ring([Slot(b) for b in T1])
        t2r = Ring([Slot(b) for b in T2])
        hr = Ring([Slot(*b) for b in HH])
        for r in (t1r, t2r, hr):
            for s in r.slots:
                s.free = l1_end
        extra = [(sb(f"yh{i}", [128, SLOT], R32, ctx=m1), sb(f"yl{i}", [128, SLOT], R32, ctx=m1)) for i in range(2)]
        s_sel = semaphore("s_sel")
        t_sel = sp.dma(SELf[:, :], sel, s_sel, 16, *l1_end)

        ring4 = bank_ring((4, 5, 6, 7))
        t_ct = [None, None]

        def spread(half):
            s, fr = ring4.take()
            for c in range(4):
                p = pe.op(lambda e, c=c: e.transpose(s.parts[0][0:32, c * 128:(c + 1) * 128],
                          cl[:, half * 4 + c, :], ident), gates[half], *fr)
            t_ct[half] = act.op(lambda e: e.copy(CTr[:, half * 512:half * 512 + 512], s.parts[0][0:32, :]), p)
            s.free = (t_ct[half],)

        def combine(b, j, sl, *fr):
            return pe.op(lambda e: e.matmul(b[:, :], SELr[:, j * 128:(j + 1) * 128], CTr[:, sl], start=True, stop=True),
                         t_sel, t_ct[sl.start // 512], *fr)

        ov = out.rearrange("(t p) d -> p t d", p=128)
        sent = []

        def after_moe(half, y):
            def one(c):
                t = half * 4 + c
                d = dve.op(lambda e: e.tensor_tensor(XO[:, t, :], XO[:, t, :], ybank(t), ALU.add), y[t | 1])
                sent.append(sp.dma(ov[:, t, :], XO[:, t, :], s_out, 16 * len(sent) + 16, d))
            return [lambda c=c: one(c) for c in range(4)]

        last_norm(1)
        more_slots(extra, "moe24", l1_end)
        t_sel = pool.op(lambda e: e.tensor_scalar(SELr[:, :], SELf[:, :], 1.0, 0.0, ALU.mult, ALU.add), t_sel)
        rest = run_mlp([f"moe{j}" for j in range(25)], True, ring4, AT, t_h4, after=after_moe, combine=combine, lag=3,
                       before=[lambda: None, lambda: None, lambda: last_turn(1, ring4), lambda: gate(1, ring4)],
                       at={(1, 0): lambda: spread(0), (0, 1): lambda: route(1), (1, 1): lambda: spread(1)})
        for f in rest:
            f()
        sp.wait(sent[-1])
        m1.close()

        with nc.Block() as block:
            @block.sync
            def _(e):
                sp.play(e)

            @block.tensor
            def _(e):
                pe.play(e)

            @block.vector
            def _(e):
                dve.play(e)

            @block.scalar
            def _(e):
                act.play(e)

            @block.gpsimd
            def _(e):
                pool.play(e)


def last_of(engine):
    return (engine.sem, engine.count)


def _layout(i):
    f = np.float32
    a = {k: np.asarray(v) for k, v in i.items()}

    def kmajor(m):
        return m.reshape(-1, 128, m.shape[-1]).transpose(1, 0, 2).reshape(128, -1)

    def pad(m, n, axis):
        w = [(0, 0)] * m.ndim
        w[axis] = (0, n - m.shape[axis])
        return np.pad(m, w)

    ch = {}
    qkv = np.concatenate([a["L0_attn_w_qkv"], a["L0_attn_gg_w1"]], 1)
    ch["qkv0"], ch["qkv1"] = qkv[0:128], qkv[128:256]
    ch["wo"] = kmajor(a["L0_attn_w_o"])
    for j in range(8):
        s = slice(j * 128, j * 128 + 128)
        ch[f"mem{j}"] = np.concatenate([kmajor(a["L0_attn_mem_w1"][:, s]), a["L0_attn_mem_w2"][s]], 1)
    w1, w3 = pad(a["L0_attn_ffn_w1"], 768, 1), pad(a["L0_attn_ffn_w3"], 768, 1)
    w2 = pad(a["L0_attn_ffn_w2"], 768, 0)
    for j in range(6):
        s = slice(j * 128, j * 128 + 128)
        ch[f"ffn{j}"] = np.concatenate([kmajor(w1[:, s]), kmajor(w3[:, s]), w2[s]], 1)
    up = a["L0_ffn_W_up"].T
    ch["up"] = np.concatenate([kmajor(up[:, 0:128]), kmajor(up[:, 128:256])], 1)
    ch["exp"] = kmajor(np.concatenate([a["L0_ffn_W_expert"], a["L0_ffn_W_gate"].T], 1))
    ch["down"] = kmajor(a["L0_ffn_W_down"].T)
    uq, uk, uv = (a[f"L1_attn_W_{n}_w"].reshape(16, 128, -1) for n in ("UQ", "UK", "UV"))
    buq, buk, buv = (a[f"L1_attn_W_{n}_b"].reshape(16, 128, 1) for n in ("UQ", "UK", "UV"))
    wo = a["L1_attn_W_O_w"].T.reshape(16, 128, 256)
    for h in range(16):
        ch[f"fuse{h}"] = np.concatenate([pad(np.concatenate([uq[h], buq[h]], 1), 256, 1), uk[h], buk[h], uv[h], buv[h], wo[h]], 1)
    dkv, dq = a["L1_attn_W_DKV_w"].T, a["L1_attn_W_DQ_w"].T
    ch["proj"] = kmajor(np.concatenate([dkv, dkv, pad(dq, 256, 1)], 1))
    ch["gate"] = kmajor(a["L1_ffn_gate_w"].T)
    e1, e2 = a["L1_ffn_w1"], a["L1_ffn_w2"]
    g = e1[:, 0:176].reshape(2816, 256).T
    u = e1[:, 176:352].reshape(2816, 256).T
    dn = e2.transpose(0, 2, 1).reshape(2816, 256)
    s1 = a["L1_ffn_shared_w1"].T
    sg, su, sd = pad(s1[:, 0:352], 384, 1), pad(s1[:, 352:704], 384, 1), pad(a["L1_ffn_shared_w2"].T, 384, 0)
    g, u, dn = np.concatenate([sg, g], 1), np.concatenate([su, u], 1), np.concatenate([sd, dn], 0)
    for j in range(25):
        s = slice(j * 128, j * 128 + 128)
        ch[f"moe{j}"] = np.concatenate([kmajor(g[:, s]), kmajor(u[:, s]), dn[s]], 1)
    w = np.concatenate([ch[n] for n, _, _ in CHUNKS], 1)

    sm = np.zeros((128, SM_N), f)

    def put(name, v):
        sm[:, SM_OFF[name][0]:SM_OFF[name][1]] = v

    p = np.arange(128)
    put("ident", np.eye(128, dtype=f))
    inv = (f(1.0) / np.power(f(10000.0), np.arange(0, 16, 2, dtype=f) / f(16))).astype(f)
    fr = (np.arange(256, dtype=f)[:, None] * inv[None, :]).astype(f).astype(np.float64)
    fr = np.concatenate([fr, fr], 1)
    cos, sin = np.cos(fr).astype(f), np.sin(fr).astype(f)
    sin[:, 0:8] = -sin[:, 0:8]
    put("cos", cos.reshape(2, 128, 16).transpose(1, 0, 2).reshape(128, 32))
    put("sin", sin.reshape(2, 128, 16).transpose(1, 0, 2).reshape(128, 32))
    put("qs", a["L0_attn_q_scale"][None, :])
    put("ks", a["L0_attn_k_scale"][None, :])
    pos = (p[:, None] + 128 * np.arange(2)[None, :]).astype(np.float64)
    put("dk", (0.5 * 0.9 ** -pos).astype(f))
    put("dq", (0.9 ** pos).astype(f))
    put("mh", (p[:, None] // 16 == np.arange(8)[None, :]).astype(f))
    put("nw", np.concatenate([a["L0_attn_norm1_w"].reshape(2, 128).T, a["L0_attn_norm2_w"].reshape(2, 128).T], 1))
    put("ggw2", a["L0_attn_gg_w2"].reshape(1, 64))
    cb = np.zeros((128, 3), f)
    cb[0:64, 0] = cb[64:128, 0] = a["L1_attn_W_DKV_b"]
    cb[:, 1] = a["L1_attn_W_DQ_b"][0:128]
    cb[0:64, 2] = a["L1_attn_W_DQ_b"][128:192]
    cb[64, 2] = 1.0
    put("cb", cb)
    put("bo", a["L1_attn_W_O_b"][None, :])
    rel = p[:, None] - p[None, :]
    m0 = np.where((rel >= 0) & (rel < 64), 0.0, NEG).astype(f)
    rel = p[:, None] + 64 - np.arange(192)[None, :]
    m1 = np.where((rel >= 0) & (rel < 64), 0.0, NEG).astype(f)
    put("mask0", np.tile(m0, (1, 4)))
    put("mask1", np.tile(m1, (1, 2)))
    sel = np.zeros((32, 22 * 128), f)
    hid = np.arange(22 * 128)
    sel[hid // 176, hid] = 1.0
    sel[16 + hid // 176, hid] = 1.0
    return {"x": a["L0_attn_x"].reshape(T, 256), "w": w, "sm": sm, "sel": sel}


def kernel(**inputs):
    import concourse.bacc as _bacc
    from concourse import mybir as _mybir
    from concourse.bass_utils import run_bass_kernel_spmd as _run

    nc = _bacc.Bacc("TRN2", target_bir_lowering=False, num_devices=1)
    arrays = {f"in_{k}": np.ascontiguousarray(v) for k, v in _layout(inputs).items()}
    args = [nc.dram_tensor(k, v.shape, _mybir.dt.from_np(v.dtype), kind="ExternalInput").ap() for k, v in arrays.items()]
    o = nc.dram_tensor("out_dram", (T, 256), F32, kind="ExternalOutput").ap()
    build(nc, *args, o)
    r = _run(nc, [arrays], core_ids=[0])
    return r.results[0]["out_dram"].reshape(4, 256, 256)
```
